# Optimizing a Trainium2 kernel written in Bass

```python
import numpy as np
import jax
import jax.numpy as jnp

def _softmax(x, axis=-1):
    return jax.nn.softmax(x, axis=axis)

def _gelu(x):
    return jax.nn.gelu(x, approximate=True)

def _silu(x):
    return jax.nn.silu(x)

def _sigmoid(x):
    return jax.nn.sigmoid(x)

def _layernorm(x, axis=-1, eps=1e-05):
    m = jnp.mean(x, axis=axis, keepdims=True)
    v = jnp.var(x, axis=axis, keepdims=True)
    return (x - m) / jnp.sqrt(v + eps)

def _scatter_add(tgt, idx, src, axis=0):
    return tgt.at[idx].add(src)

def _segment_sum(src, seg, n):
    return jax.ops.segment_sum(src, seg, n)
kernel_name = 'mk_sandwich_d2_jaxref_r8_a6b464'

def setup_inputs(seed: int=0):
    np.random.seed(seed)
    _w = jnp.asarray

    def _L0_attn_setup():
        import jax, jax.numpy as jnp
        import numpy as np
        NH = 16
        key = jax.random.key(seed)
        ks = jax.random.split(key, 5)
        B, T, D = (2, 256, 256)
        scale = 0.02
        return {'x': jax.random.normal(ks[0], (B, T, D), dtype=jnp.float32), 'Wq': jax.random.normal(ks[1], (D, D), dtype=jnp.float32) * scale, 'Wk': jax.random.normal(ks[2], (D, D), dtype=jnp.float32) * scale, 'Wv': jax.random.normal(ks[3], (D, D), dtype=jnp.float32) * scale, 'Wo': jax.random.normal(ks[4], (D, D), dtype=jnp.float32) * scale}
    _L0_attn_in = _L0_attn_setup()

    def _L0_ffn_setup():
        import jax, jax.numpy as jnp
        import numpy as np
        B, T, D, E, F, K, ND = (2, 32, 256, 64, 64, 4, 4)
        H = F * K
        N_SHARED = 2
        key = jax.random.key(seed)
        ks = jax.random.split(key, 12)
        s = lambda k, shape: jax.random.normal(k, shape, jnp.float32) * 0.02
        x = jax.random.normal(ks[0], (B, T, D), jnp.float32)
        Wr = s(ks[1], (E, D))
        router_bias = jnp.zeros((E,), jnp.float32)
        affinity = s(ks[2], (E, ND))
        te_W1 = s(ks[3], (D // 2, D))
        te_b1 = jnp.zeros((D // 2,), jnp.float32)
        te_W2 = s(ks[4], (ND, D // 2))
        te_b2 = jnp.zeros((ND,), jnp.float32)
        Wg = s(ks[5], (E, D, F))
        Wu = s(ks[6], (E, D, F))
        Wd = s(ks[7], (E, F, D))
        Sg = s(ks[8], (N_SHARED, D, H))
        Su = s(ks[9], (N_SHARED, D, H))
        Sd = s(ks[10], (N_SHARED, H, D))
        return dict(x=x, Wr=Wr, router_bias=router_bias, affinity=affinity, te_W1=te_W1, te_b1=te_b1, te_W2=te_W2, te_b2=te_b2, Wg=Wg, Wu=Wu, Wd=Wd, Sg=Sg, Su=Su, Sd=Sd)
    _L0_ffn_in = _L0_ffn_setup()

    def _L1_attn_setup():
        import jax, jax.numpy as jnp
        import numpy as np
        EPS = 1e-06
        CAP = 15.0
        NH = 8

        def soft_cap(x, cap=CAP):
            return cap * jnp.tanh(x / cap)

        def _mlstm_scan(q, k, v, i_pre, f_pre):
            B, S, nh, DQ = q.shape
            DV = v.shape[-1]
            scale = DQ ** (-0.5)

            def step(carry, xs):
                C, n, m = carry
                q_t, k_t, v_t, i_t, f_t = xs
                f_log = jax.nn.log_sigmoid(f_t)
                m_new = jnp.maximum(f_log + m, i_t)
                F = jnp.exp(f_log + m - m_new)
                I = jnp.exp(i_t - m_new)
                C_new = F[..., None, None] * C + (I[..., None] * k_t)[..., :, None] * v_t[..., None, :]
                n_new = F[..., None] * n + I[..., None] * k_t
                qs = q_t * scale
                h_num = jnp.einsum('bhd,bhdv->bhv', qs, C_new)
                qn = jnp.einsum('bhd,bhd->bh', qs, n_new)
                denom = jnp.maximum(jnp.abs(qn), jnp.exp(-m_new)) + EPS
                h = h_num / denom[..., None]
                return ((C_new, n_new, m_new), h)
            C0 = jnp.zeros((B, nh, DQ, DV), q.dtype)
            n0 = jnp.zeros((B, nh, DQ), q.dtype)
            m0 = jnp.zeros((B, nh), q.dtype)
            to_s = lambda a: jnp.moveaxis(a, 1, 0)
            (Cf, nf, mf), hs = jax.lax.scan(step, (C0, n0, m0), (to_s(q), to_s(k), to_s(v), to_s(i_pre), to_s(f_pre)))
            return (jnp.moveaxis(hs, 0, 1), (Cf, nf, mf))

        def _multihead_norm(h, gamma):
            h32 = h.astype(jnp.float32)
            mu = jnp.mean(h32, axis=-1, keepdims=True)
            var = jnp.mean((h32 - mu) ** 2, axis=-1, keepdims=True)
            hn = (h32 - mu) * jax.lax.rsqrt(var + EPS)
            return (hn * gamma).astype(h.dtype)

        def _reference_tuple_inner(x, Wq, Wk, Wv, Wog, Wig, big, Wfg, bfg, gamma, Wout):
            B, S, D = x.shape
            q = x @ Wq.T
            k = x @ Wk.T
            v = x @ Wv.T
            o_preact = x @ Wog.T
            i_pre = soft_cap(x @ Wig.T + big)
            f_pre = soft_cap(x @ Wfg.T + bfg)
            q = q.reshape(B, S, NH, -1)
            k = k.reshape(B, S, NH, -1)
            v = v.reshape(B, S, NH, -1)
            h, state = _mlstm_scan(q, k, v, i_pre, f_pre)
            h_norm = _multihead_norm(h, gamma).reshape(B, S, -1)
            h_out = jax.nn.sigmoid(o_preact) * h_norm
            y = h_out @ Wout.T
            return (y, *state)
        key = jax.random.key(seed)
        ks = jax.random.split(key, 12)
        B, S, D = (2, 256, 256)
        QK, V = (D // 2, D)
        DHV = V // NH
        s = lambda fan_in: 1.0 / np.sqrt(fan_in)
        return {'x': jax.random.normal(ks[0], (B, S, D), jnp.float32), 'Wq': jax.random.normal(ks[1], (QK, D), jnp.float32) * s(D), 'Wk': jax.random.normal(ks[2], (QK, D), jnp.float32) * s(D), 'Wv': jax.random.normal(ks[3], (V, D), jnp.float32) * s(D), 'Wog': jax.random.normal(ks[4], (V, D), jnp.float32) * s(D), 'Wig': jax.random.normal(ks[5], (NH, D), jnp.float32) * s(D), 'big': jax.random.normal(ks[6], (NH,), jnp.float32) * 0.1, 'Wfg': jax.random.normal(ks[7], (NH, D), jnp.float32) * s(D), 'bfg': jax.random.normal(ks[8], (NH,), jnp.float32) * 0.1 + 3.0, 'gamma': jnp.ones((NH, DHV), jnp.float32), 'Wout': jax.random.normal(ks[9], (D, V), jnp.float32) * s(V)}
    _L1_attn_in = _L1_attn_setup()

    def _L1_ffn_setup():
        import jax, jax.numpy as jnp
        import numpy as np

        def _sparsify_2to4(h):
            B, S, I = h.shape
            g = h.reshape(B, S, I // 4, 4)
            a = jnp.abs(g)
            _, idx = jax.lax.top_k(a, 2)
            pos = jnp.arange(4)
            mask = (pos == idx[..., 0:1]) | (pos == idx[..., 1:2])
            return (g * mask.astype(g.dtype)).reshape(B, S, I)
        key = jax.random.key(seed)
        k1, k2, k3, k4 = jax.random.split(key, 4)
        B, S, H, I = (4, 256, 256, 1024)
        x = jax.random.normal(k1, (B, S, H), dtype=jnp.float32)
        w_gate = jax.random.normal(k2, (H, I), dtype=jnp.float32) / np.sqrt(H)
        w_up = jax.random.normal(k3, (H, I), dtype=jnp.float32) / np.sqrt(H)
        w_down = jax.random.normal(k4, (I, H), dtype=jnp.float32) / np.sqrt(I)
        return {'x': x, 'w_gate': w_gate, 'w_up': w_up, 'w_down': w_down}
    _L1_ffn_in = _L1_ffn_setup()
    _d = {'L0_attn_x': _L0_attn_in['x'], 'L0_attn_Wq': _L0_attn_in['Wq'], 'L0_attn_Wk': _L0_attn_in['Wk'], 'L0_attn_Wv': _L0_attn_in['Wv'], 'L0_attn_Wo': _L0_attn_in['Wo'], 'L0_ffn_Wr': _L0_ffn_in['Wr'], 'L0_ffn_router_bias': _L0_ffn_in['router_bias'], 'L0_ffn_affinity': _L0_ffn_in['affinity'], 'L0_ffn_te_W1': _L0_ffn_in['te_W1'], 'L0_ffn_te_b1': _L0_ffn_in['te_b1'], 'L0_ffn_te_W2': _L0_ffn_in['te_W2'], 'L0_ffn_te_b2': _L0_ffn_in['te_b2'], 'L0_ffn_Wg': _L0_ffn_in['Wg'], 'L0_ffn_Wu': _L0_ffn_in['Wu'], 'L0_ffn_Wd': _L0_ffn_in['Wd'], 'L0_ffn_Sg': _L0_ffn_in['Sg'], 'L0_ffn_Su': _L0_ffn_in['Su'], 'L0_ffn_Sd': _L0_ffn_in['Sd'], 'L1_attn_Wq': _L1_attn_in['Wq'], 'L1_attn_Wk': _L1_attn_in['Wk'], 'L1_attn_Wv': _L1_attn_in['Wv'], 'L1_attn_Wog': _L1_attn_in['Wog'], 'L1_attn_Wig': _L1_attn_in['Wig'], 'L1_attn_big': _L1_attn_in['big'], 'L1_attn_Wfg': _L1_attn_in['Wfg'], 'L1_attn_bfg': _L1_attn_in['bfg'], 'L1_attn_gamma': _L1_attn_in['gamma'], 'L1_attn_Wout': _L1_attn_in['Wout'], 'L1_ffn_w_gate': _L1_ffn_in['w_gate'], 'L1_ffn_w_up': _L1_ffn_in['w_up'], 'L1_ffn_w_down': _L1_ffn_in['w_down']}
    _x0 = _d['L0_attn_x']
    _d['L0_attn_x'] = jax.random.normal(jax.random.fold_in(jax.random.key(seed), 1), (8, 256, 256), dtype=_x0.dtype)
    del _x0
    return _d

def reference(L0_attn_x, L0_attn_Wq, L0_attn_Wk, L0_attn_Wv, L0_attn_Wo, L0_ffn_Wr, L0_ffn_router_bias, L0_ffn_affinity, L0_ffn_te_W1, L0_ffn_te_b1, L0_ffn_te_W2, L0_ffn_te_b2, L0_ffn_Wg, L0_ffn_Wu, L0_ffn_Wd, L0_ffn_Sg, L0_ffn_Su, L0_ffn_Sd, L1_attn_Wq, L1_attn_Wk, L1_attn_Wv, L1_attn_Wog, L1_attn_Wig, L1_attn_big, L1_attn_Wfg, L1_attn_bfg, L1_attn_gamma, L1_attn_Wout, L1_ffn_w_gate, L1_ffn_w_up, L1_ffn_w_down):

    def _L0_attn_ref(x, Wq, Wk, Wv, Wo):
        import jax, jax.numpy as jnp
        import numpy as np
        NH = 16
        B, T, D = x.shape
        hd = D // NH
        q = (x @ Wq.T).reshape(B, T, NH, hd).transpose(0, 2, 1, 3)
        k = (x @ Wk.T).reshape(B, T, NH, hd).transpose(0, 2, 1, 3)
        v = (x @ Wv.T).reshape(B, T, NH, hd).transpose(0, 2, 1, 3)
        att = jnp.einsum('bhtd,bhsd->bhts', q, k) / jnp.sqrt(jnp.asarray(hd, x.dtype))
        neg = jnp.finfo(att.dtype).min
        mask = jnp.triu(jnp.full((T, T), neg, dtype=att.dtype), k=1)
        att = att + mask
        w = jax.nn.softmax(att, axis=-1)
        z = jnp.einsum('bhts,bhsd->bhtd', w, v)
        z = z.transpose(0, 2, 1, 3).reshape(B, T, D)
        return z @ Wo.T

    def _L0_ffn_ref(x, Wr, router_bias, affinity, te_W1, te_b1, te_W2, te_b2, Wg, Wu, Wd, Sg, Su, Sd):
        import jax, jax.numpy as jnp
        import numpy as np
        B, T, D, E, F, K, ND = (2, 32, 256, 64, 64, 4, 4)
        H = F * K
        N_SHARED = 2
        b, t, d = x.shape
        n = b * t
        flat = x.reshape(n, d)
        xm = x.mean(axis=1)
        h1 = jax.nn.gelu(xm @ te_W1.T + te_b1, approximate=False)
        task_dist = jax.nn.softmax(h1 @ te_W2.T + te_b2, axis=-1)
        dom = task_dist @ affinity.T
        logits = (flat @ Wr.T).reshape(b, t, E) + 0.5 * dom[:, None, :]
        logits = logits.reshape(n, E)
        scores = jax.nn.softmax(logits, axis=-1)
        _, topk_idx = jax.lax.top_k(logits + router_bias, K)
        topk_scores = jnp.take_along_axis(scores, topk_idx, axis=-1)
        topk_scores = topk_scores / (topk_scores.sum(-1, keepdims=True) + 1e-08)
        combine = jnp.zeros((n, E), x.dtype).at[jnp.arange(n)[:, None], topk_idx].add(topk_scores)
        g = jnp.einsum('nd,edf->enf', flat, Wg)
        u = jnp.einsum('nd,edf->enf', flat, Wu)
        h = jax.nn.silu(g) * u
        hw = h * combine.T[:, :, None]
        out = jnp.einsum('enf,efd->nd', hw, Wd)
        for i in range(Sg.shape[0]):
            sh = jax.nn.silu(flat @ Sg[i]) * (flat @ Su[i])
            out = out + sh @ Sd[i]
        return out.reshape(b, t, d)

    def _L1_attn_ref(x, Wq, Wk, Wv, Wog, Wig, big, Wfg, bfg, gamma, Wout):
        import jax, jax.numpy as jnp
        import numpy as np
        EPS = 1e-06
        CAP = 15.0
        NH = 8

        def soft_cap(x, cap=CAP):
            return cap * jnp.tanh(x / cap)

        def _mlstm_scan(q, k, v, i_pre, f_pre):
            B, S, nh, DQ = q.shape
            DV = v.shape[-1]
            scale = DQ ** (-0.5)

            def step(carry, xs):
                C, n, m = carry
                q_t, k_t, v_t, i_t, f_t = xs
                f_log = jax.nn.log_sigmoid(f_t)
                m_new = jnp.maximum(f_log + m, i_t)
                F = jnp.exp(f_log + m - m_new)
                I = jnp.exp(i_t - m_new)
                C_new = F[..., None, None] * C + (I[..., None] * k_t)[..., :, None] * v_t[..., None, :]
                n_new = F[..., None] * n + I[..., None] * k_t
                qs = q_t * scale
                h_num = jnp.einsum('bhd,bhdv->bhv', qs, C_new)
                qn = jnp.einsum('bhd,bhd->bh', qs, n_new)
                denom = jnp.maximum(jnp.abs(qn), jnp.exp(-m_new)) + EPS
                h = h_num / denom[..., None]
                return ((C_new, n_new, m_new), h)
            C0 = jnp.zeros((B, nh, DQ, DV), q.dtype)
            n0 = jnp.zeros((B, nh, DQ), q.dtype)
            m0 = jnp.zeros((B, nh), q.dtype)
            to_s = lambda a: jnp.moveaxis(a, 1, 0)
            (Cf, nf, mf), hs = jax.lax.scan(step, (C0, n0, m0), (to_s(q), to_s(k), to_s(v), to_s(i_pre), to_s(f_pre)))
            return (jnp.moveaxis(hs, 0, 1), (Cf, nf, mf))

        def _multihead_norm(h, gamma):
            h32 = h.astype(jnp.float32)
            mu = jnp.mean(h32, axis=-1, keepdims=True)
            var = jnp.mean((h32 - mu) ** 2, axis=-1, keepdims=True)
            hn = (h32 - mu) * jax.lax.rsqrt(var + EPS)
            return (hn * gamma).astype(h.dtype)

        def _reference_tuple_inner(x, Wq, Wk, Wv, Wog, Wig, big, Wfg, bfg, gamma, Wout):
            B, S, D = x.shape
            q = x @ Wq.T
            k = x @ Wk.T
            v = x @ Wv.T
            o_preact = x @ Wog.T
            i_pre = soft_cap(x @ Wig.T + big)
            f_pre = soft_cap(x @ Wfg.T + bfg)
            q = q.reshape(B, S, NH, -1)
            k = k.reshape(B, S, NH, -1)
            v = v.reshape(B, S, NH, -1)
            h, state = _mlstm_scan(q, k, v, i_pre, f_pre)
            h_norm = _multihead_norm(h, gamma).reshape(B, S, -1)
            h_out = jax.nn.sigmoid(o_preact) * h_norm
            y = h_out @ Wout.T
            return (y, *state)
        return _reference_tuple_inner(x, Wq, Wk, Wv, Wog, Wig, big, Wfg, bfg, gamma, Wout)[0]

    def _L1_ffn_ref(x, w_gate, w_up, w_down):
        import jax, jax.numpy as jnp
        import numpy as np

        def _sparsify_2to4(h):
            B, S, I = h.shape
            g = h.reshape(B, S, I // 4, 4)
            a = jnp.abs(g)
            _, idx = jax.lax.top_k(a, 2)
            pos = jnp.arange(4)
            mask = (pos == idx[..., 0:1]) | (pos == idx[..., 1:2])
            return (g * mask.astype(g.dtype)).reshape(B, S, I)
        h = jax.nn.silu(jnp.einsum('bsh,hi->bsi', x, w_gate)) * jnp.einsum('bsh,hi->bsi', x, w_up)
        h_sparse = _sparsify_2to4(h)
        return jnp.einsum('bsi,ih->bsh', h_sparse, w_down)
    x = L0_attn_x
    x = x + _layernorm(_L0_attn_ref(_layernorm(x, axis=-1), L0_attn_Wq, L0_attn_Wk, L0_attn_Wv, L0_attn_Wo), axis=-1)
    x = x + _layernorm(_L0_ffn_ref(_layernorm(x, axis=-1), L0_ffn_Wr, L0_ffn_router_bias, L0_ffn_affinity, L0_ffn_te_W1, L0_ffn_te_b1, L0_ffn_te_W2, L0_ffn_te_b2, L0_ffn_Wg, L0_ffn_Wu, L0_ffn_Wd, L0_ffn_Sg, L0_ffn_Su, L0_ffn_Sd), axis=-1)
    x = x + _layernorm(_L1_attn_ref(_layernorm(x, axis=-1), L1_attn_Wq, L1_attn_Wk, L1_attn_Wv, L1_attn_Wog, L1_attn_Wig, L1_attn_big, L1_attn_Wfg, L1_attn_bfg, L1_attn_gamma, L1_attn_Wout), axis=-1)
    x = x + _layernorm(_L1_ffn_ref(_layernorm(x, axis=-1), L1_ffn_w_gate, L1_ffn_w_up, L1_ffn_w_down), axis=-1)
    return x

_drawn_inputs = setup_inputs


def setup_inputs(seed=0):
    import zlib

    import numpy as np

    out = dict(_drawn_inputs(seed))
    spreads = {'L0_ffn_router_bias': (0.0, 0.1),
     'L0_ffn_te_b1': (0.0, 2.0),
     'L0_ffn_te_b2': (0.0, 2.0),
     'L1_attn_gamma': (1.0, 0.2)}
    factors = {'L0_ffn_te_W1': 24.089, 'L0_ffn_te_W2': 8.0, 'L1_attn_big': 64.0}
    for name, (base, spread) in spreads.items():
        noise = np.random.default_rng([zlib.crc32(name.encode()), seed]).standard_normal(out[name].shape)
        drawn = base * np.exp(spread * noise) if base else spread * noise
        out[name] = jnp.asarray(drawn.astype(out[name].dtype))
    for name, factor in factors.items():
        out[name] = (out[name] * factor).astype(out[name].dtype)
    return out
```

```python
from contextlib import ExitStack

import numpy as np
import concourse.bass as bass
from concourse import mybir

ALU = mybir.AluOpType
ACT = mybir.ActivationFunctionType
AXX = mybir.AxisListType.X
F32 = mybir.dt.float32
BF16 = mybir.dt.bfloat16
U32 = mybir.dt.uint32

P = 128
NB, T, D = 8, 256, 256
NT = NB * T // P
KC = D // P
NG = NB * T // 512
H0, HD0 = 16, 16
H1, QK1, DV1 = 8, 16, 32
E, FE, TOPK, ND = 64, 64, 4, 4
NPAIR = E // 2
NSH = 4
NI = 8
CAP = 15.0
NEG = -3.0e38
LN_EPS, HEAD_EPS = 1e-5, 1e-6


class Chain:

    def __init__(self, eng, sem, base=0):
        self.eng, self.sem, self.base, self.n = eng, sem, base, 0

    def __call__(self, ins):
        self.n += 1
        ins.then_inc(self.sem, 1)
        self.eng.wait_ge(self.sem, self.base + self.n)


def build(nc, io, out):
    ctx = ExitStack()
    with ctx:
        def sb(name, shape, dt=F32):
            return ctx.enter_context(nc.sbuf_tensor(name, shape, dt))

        def sem(name):
            return ctx.enter_context(nc.semaphore(name))

        S = [ctx.enter_context(nc.psum_tensor(f"S{i}", [P, 512], F32)) for i in range(4)]
        T0 = ctx.enter_context(nc.psum_tensor("T0", [P, 512], F32))
        T1 = ctx.enter_context(nc.psum_tensor("T1", [P, 512], F32))
        Z = ctx.enter_context(nc.psum_tensor("Z", [P, 512], F32))
        O = ctx.enter_context(nc.psum_tensor("O", [P, 512], F32))
        TB = [T0, T1]

        x_sb = sb("x_sb", [P, NT, D])
        xall = sb("xall", [P, KC, NB * T])
        ident = sb("ident", [P, P])
        identb = sb("identb", [P, P], BF16)
        mask_ts = sb("mask_ts", [P, P], BF16)
        mask_st = sb("mask_st", [P, P], BF16)
        sel1 = sb("sel1", [H1, H1, P])
        iota = sb("iota", [P, E])
        mhalf = sb("mhalf", [P, 16])
        mv = sb("mv", [P, 2, 2])
        st = sb("st", [P, 2, 6])
        veps = sb("veps", [P, 2])
        rstd = sb("rstd", [P, 2])

        def views(name, nbytes):
            arena = sb(name, [P, nbytes // 4])
            at = [0]

            def view(shape, dt=F32):
                n = int(np.prod(shape[1:]))
                words = n if dt in (F32, U32) else (n + 1) // 2
                v = arena[0:shape[0], at[0]:at[0] + words]
                at[0] += words
                assert at[0] * 4 <= nbytes, (name, at[0] * 4)
                if dt != F32:
                    v = v.bitcast(dt)
                if len(shape) == 3:
                    v = v.rearrange("p (a b) -> p a b", b=shape[2])
                if len(shape) == 4:
                    v = v.rearrange("p (a b c) -> p a b c", b=shape[2], c=shape[3])
                return v

            def rewind():
                at[0] = 0
            return view, rewind

        view, rewind = views("attn_w", 25 * 512)
        wq0 = view([P, KC, 512])
        wk0 = view([P, KC, 512])
        wv0 = view([P, KC, D])
        wo0 = view([P, KC, D])
        wr = view([P, KC, E])
        rewind()
        wq1 = view([P, KC, 256])
        wk1 = view([P, KC, 256])
        wv1 = view([P, KC, D])
        wog1 = view([P, KC, D])
        wo1 = view([P, KC, D])
        gam = view([P, D])
        wig = view([P, KC, H1])
        wfg = view([P, KC, H1])
        big = view([H1, 1])
        bfg = view([H1, 1])
        big15 = view([H1, 1])
        bfg15 = view([H1, 1])

        view, rewind = views("ffn_w", (96 + 12) * 1024)
        wg = view([P, KC, E * FE])
        wu = view([P, KC, E * FE])
        wd = view([P, NPAIR, D])
        sg_w = view([P, KC, 512])
        su_w = view([P, KC, 512])
        sd_w = view([P, NSH, D])
        rewind()
        gate = view([P, KC, 1024])
        up = view([P, KC, 1024])
        down = view([P, NI, D])
        hb = [view([P, 4, 512]) for _ in range(2)]
        hs = [view([P, 4, 512]) for _ in range(2)]
        ab = view([P, 4, 512])
        c01_23 = view([P, 2, 512], BF16)
        c02_13 = view([P, 2, 512], BF16)
        c03 = view([P, 512], BF16)
        c12 = view([P, 512], BF16)
        tally = view([P, 4, 512], BF16)
        half = view([P, 4, 512], BF16)

        te1 = sb("te1", [P, KC, P])
        te_b1 = sb("te_b1", [P, 1])
        te2 = sb("te2", [P, ND])
        te_b2 = sb("te_b2", [NB, ND])
        aff = sb("aff", [ND, E])
        rbias = sb("rbias", [P, E])
        lg_all = sb("lg_all", [P, NT, E])
        xmT = sb("xmT", [P, KC, NB])

        view, rewind = views("work", 39 * 1024)
        xn = view([P, 2, D])
        xnT = view([P, KC, T])
        tmp = view([P, 2, D])
        qT = view([P, 4, T])
        kT = view([P, 4, T])
        vaug = view([P, 2, H0, HD0 + 1])
        prob = [view([P, 2, 384]) for _ in range(2)]
        probT = [view([P, 2, 384]) for _ in range(2)]
        negmax = view([P, 2, H0])
        rden = view([P, 2, 4])
        z_sb = view([P, 2, D])
        zT = view([P, KC, T])
        xn2 = view([P, 2, D])
        xn2T = view([P, KC, T])
        rewind()
        tdx = view([ND, NB, P])
        rewind()
        c_hi = view([E, NB * T], BF16)
        c_mid = view([E, NB * T], BF16)
        c_lo = view([E, NB * T], BF16)
        selE = view([E, NPAIR, P], BF16)
        b_tmp = view([P, 512])
        lg = view([P, NT, E])
        rsel = view([P, NT, E])
        comb = view([P, NT, E])
        rmask = view([P, NT, E])
        rewind()
        for _ in range(3):
            view([E, NB * T], BF16)
        view([E, NPAIR, P], BF16)
        sgl = [view([P, 512]) for _ in range(2)]
        hh = [view([P, 512]) for _ in range(2)]
        tmp4 = view([P, 4, D])
        rewind()
        view([P, 2, D])
        view([P, KC, T])
        view([P, 2, D])
        q1 = view([P, 2, T])
        k1 = view([P, 2, T])
        v1 = view([P, 2, H1, DV1 + 1])
        eo = view([P, 2, D])
        gi = view([H1, T])
        gf = view([H1, T])
        gls = view([H1, T])
        gF = view([H1, T])
        gm = view([H1, T])
        gA = view([H1, T])
        gG = view([H1, T])
        ones1 = view([H1, T])
        gcol = view([P, 2, H1])
        em = view([P, 2, H1])
        dec = [view([P, 384]) for _ in range(2)]
        wt = [view([P, 384]) for _ in range(2)]
        den = view([P, 2, H1])
        hn = view([P, 2, D])
        hc = view([P, 2, D])
        sq = view([P, 2, D])
        hT = view([P, KC, T])
        mu = view([P, 16])
        hv = view([P, 16])
        xn4 = view([P, 2, D])

        top = sb("top", [P, NT, 8])
        topi = sb("topi", [P, NT, 8], U32)
        topf = sb("topf", [P, NT, 8])
        rmx = sb("rmx", [P, NT])
        rZ = sb("rZ", [P, NT])
        rS = sb("rS", [P, NT])
        h1T = sb("h1T", [P, NB])
        tl = sb("tl", [NB, ND])
        tm = sb("tm", [NB, 1])
        td = sb("td", [NB, ND])
        dom = sb("dom", [P, NB, E])

        names = """x_in w_a w_te w_moe w_sh w_c w_d pool_c const_done vones
            ln_mv ln_rs
            a_xn a_xt a_xtc a_qk a_q a_k a_vps a_v a_sc a_mx a_exp a_pt a_ptc a_pv a_z a_zt a_ztc a_y
            a_xn2 a_x2t a_x2c a_xall a_xm a_lg a_lgc
            t_h1 t_h1c t_lg t_sub t_exp t_td t_tT t_tx t_dom r_sub r_exp r_comb r_cT r_split sel_done
            f_gu f_sg f_cb f_h f_y f_post
            c_xn c_xt c_xtc c_qk c_q c_k c_vog c_v c_eo c_gt c_tanh c_ls c_gates c_gT c_gcol c_em
            c_sd c_dec c_w c_pv c_hv c_hr c_ho c_hoT c_hoTc c_y c_xn4 c_x4t c_xall c_ones
            d_gu d_sg d_h d_abs d_hs d_y d_x o_out
            turn_v turn_p turn_t ch0 cha chr chb chc chd chp chpa chpb chpc chpd""".split()
        s = {n: sem(n) for n in names}

        block = ctx.enter_context(nc.Block())

        def hold(eng, name):
            eng.sem_inc(s[name], 1)

        def bc(ap, shape):
            return ap.to_broadcast(shape)

        @block.sync
        def _(sp):
            sp.dma_start(x_sb[:], io["x"].rearrange("(n p) d -> p n d", p=P)).then_inc(s["x_in"], 16)
            for dst, name in ((wq0, "wq0"), (wk0, "wk0"), (wv0, "wv0"), (wo0, "wo0"), (wr, "wr")):
                sp.dma_start(dst, io[name]).then_inc(s["w_a"], 16)
            for dst, name in ((te1[:], "te1"), (te_b1[:], "te_b1"), (te2[:], "te2"), (aff[:], "aff")):
                sp.dma_start(dst, io[name]).then_inc(s["w_te"], 16)
            sp.dma_start(te_b2[:], io["te_b2"].partition_broadcast(NB)).then_inc(s["w_te"], 16)
            sp.dma_start(rbias[:], io["rbias"].partition_broadcast(P)).then_inc(s["w_te"], 16)
            for dst, name in ((wg, "wg"), (wu, "wu"), (wd, "wd"), (sg_w, "sg"), (su_w, "su"), (sd_w, "sd")):
                sp.dma_start(dst, io[name]).then_inc(s["w_moe"], 16)
            sp.wait_ge(s["a_lg"], NB)
            for dst, name in ((wq1, "wq1"), (wk1, "wk1"), (wv1, "wv1"), (wog1, "wog1"), (wo1, "wo1"),
                              (wig, "wig"), (wfg, "wfg"), (big, "big"), (bfg, "bfg")):
                sp.dma_start(dst, io[name]).then_inc(s["w_c"], 16)
            sp.dma_start(gam, io["gam"].partition_broadcast(P)).then_inc(s["w_c"], 16)
            sp.wait_ge(s["f_y"], NG)
            for dst, name in ((gate, "gate"), (up, "up"), (down, "down")):
                sp.dma_start(dst, io[name]).then_inc(s["w_d"], 16)
            for g in range(NG):
                sp.wait_ge(s["d_x"], g + 2)
                sp.dma_start(out[g * 512:(g + 1) * 512, :].rearrange("(n p) d -> p n d", p=P),
                             x_sb[:, 4 * g:4 * g + 4, :]).then_inc(s["o_out"], 16)
            sp.wait_ge(s["o_out"], 16 * NG)

        @block.gpsimd
        def _(pool):
            ch = Chain(pool, s["pool_c"])
            pool.memset(ident[:], 0.0)
            pool.memset(identb[:], 0.0)
            pool.memset(mask_ts[:], 0.0)
            pool.memset(mask_st[:], 0.0)
            pool.memset(sel1[:], 0.0)
            pool.memset(mhalf[:], -0.5)
            pool.memset(vaug, 1.0)
            ch(pool.iota(iota[:], [[1, E]], base=0, channel_multiplier=0, allow_small_or_imprecise_dtypes=True))
            for m in (ident, identb):
                pool.affine_select(out=m[:], in_=m[:], compare_op=ALU.not_equal, fill=1.0, base=0,
                                   pattern=[[-1, P]], channel_multiplier=1)
            pool.affine_select(out=mask_ts[:], in_=mask_ts[:], compare_op=ALU.is_ge, fill=NEG, base=0,
                               pattern=[[-1, P]], channel_multiplier=1)
            pool.affine_select(out=mask_st[:], in_=mask_st[:], compare_op=ALU.is_ge, fill=NEG, base=0,
                               pattern=[[1, P]], channel_multiplier=-1)
            pool.affine_select(out=sel1[:], in_=sel1[:], compare_op=ALU.not_equal, fill=1.0, base=0,
                               pattern=[[-1, H1], [0, P]], channel_multiplier=1).then_inc(s["const_done"], 1)

            def ln_event(event, cp):
                pool.wait_ge(s["ln_mv"], event + 1)
                hold(pool, "turn_p")
                cp(pool.tensor_scalar(veps[:], mv[:, :, 1], LN_EPS, None, ALU.add))
                pool.tensor_tensor(rstd[:], veps[:], mhalf[:, 0:2], ALU.pow).then_inc(s["ln_rs"], 1)

            with pool.Fori(0, NB) as b:
                cp = Chain(pool, s["chpa"], b * 3)
                for k in range(3):
                    ln_event(b * 3 + k, cp)
            cs = Chain(pool, s["chp"])
            pool.wait_ge(s["a_lgc"], NB)
            cs(pool.memset(selE, 0.0))
            cs(pool.affine_select(out=selE[:, :, 0:64], in_=selE[:, :, 0:64], compare_op=ALU.not_equal, fill=1.0,
                                  base=0, pattern=[[-2, NPAIR], [0, 64]], channel_multiplier=1))
            pool.affine_select(out=selE[:, :, 64:128], in_=selE[:, :, 64:128], compare_op=ALU.not_equal, fill=1.0,
                               base=-1, pattern=[[-2, NPAIR], [0, 64]], channel_multiplier=1).then_inc(s["sel_done"], 1)
            with pool.Fori(0, NG) as g:
                cp = Chain(pool, s["chpb"], g * 2)
                for k in range(2):
                    ln_event(3 * NB + g * 2 + k, cp)
            pool.wait_ge(s["f_post"], NG + 1)
            pool.memset(v1, 1.0)
            pool.memset(ones1, 1.0).then_inc(s["c_ones"], 1)
            base = 3 * NB + 2 * NG
            with pool.Fori(0, NB) as b:
                cp = Chain(pool, s["chpc"], b * 4)
                ln_event(base + b * 3, cp)
                pool.wait_ge(s["c_hv"], b + 1)
                hold(pool, "turn_p")
                cp(pool.tensor_scalar(hv, hv, 1.0 / DV1, HEAD_EPS, ALU.mult, ALU.add))
                pool.tensor_tensor(hv, hv, mhalf[:], ALU.pow).then_inc(s["c_hr"], 1)
                ln_event(base + b * 3 + 1, cp)
                ln_event(base + b * 3 + 2, cp)
            with pool.Fori(0, NG) as g:
                cp = Chain(pool, s["chpd"], g * 2)
                for k in range(2):
                    ln_event(base + 3 * NB + g * 2 + k, cp)

        @block.scalar
        def _(act):
            with act.Fori(0, NB) as b:
                act.wait_ge(s["a_xt"], b + 1)
                act.activation(xnT, T0[:].rearrange("p (a b) -> p a b", b=T), ACT.Copy).then_inc(s["a_xtc"], 1)
                for g in range(4):
                    act.wait_ge(s["a_qk"], b * 4 + g + 1)
                    act.activation(qT[:, g, :], S[g][:, 0:T], ACT.Copy, scale=0.25).then_inc(s["a_q"], 1)
                for u in range(8):
                    act.wait_ge(s["a_mx"], b * 8 + u + 1)
                    if u >= 2:
                        act.wait_ge(s["a_pt"], b * 8 + u - 1)
                    for r in range(2):
                        h = 2 * u + r
                        bank = S[2 * (u % 2) + r]
                        act.activation(prob[u % 2][:, r, 0:128], bank[:, 0:128], ACT.Exp, bias=negmax[:, 0, h:h + 1])
                        last = act.activation(prob[u % 2][:, r, 128:384], bank[:, 128:384], ACT.Exp,
                                              bias=negmax[:, 1, h:h + 1])
                    last.then_inc(s["a_exp"], 1)
                act.wait_ge(s["a_zt"], b + 1)
                act.activation(zT, T0[:].rearrange("p (a b) -> p a b", b=T), ACT.Copy).then_inc(s["a_ztc"], 1)
                act.wait_ge(s["a_x2t"], b + 1)
                act.activation(xn2T, T0[:].rearrange("p (a b) -> p a b", b=T), ACT.Copy).then_inc(s["a_x2c"], 1)
                act.activation(xall[:, :, bass.ds(b * T, T)], T0[:].rearrange("p (a b) -> p a b", b=T),
                               ACT.Copy).then_inc(s["a_xall"], 1)
            act.wait_ge(s["t_h1"], 1)
            act.wait_ge(s["w_te"], 96)
            act.activation(h1T[:], S[0][:, 0:NB], ACT.Gelu, bias=te_b1[:, 0:1], scale=1.0 / T).then_inc(s["t_h1c"], 1)
            act.wait_ge(s["t_sub"], 1)
            act.activation(td[:], tl[:], ACT.Exp).then_inc(s["t_exp"], 1)
            act.wait_ge(s["r_sub"], 1)
            act.activation(comb, lg, ACT.Exp).then_inc(s["r_exp"], 1)
            with act.Fori(0, NG) as g:
                for j in range(NPAIR + NSH):
                    act.wait_ge(s["f_gu"], g * (NPAIR + NSH) + j + 1)
                    if j >= 2:
                        act.wait_ge(s["f_h"], g * (NPAIR + NSH) + j - 1)
                    act.activation(sgl[j % 2], S[j % 2][:], ACT.Silu).then_inc(s["f_sg"], 1)
            with act.Fori(0, NB) as b:
                act.wait_ge(s["c_xt"], b + 1)
                act.activation(xnT, T0[:].rearrange("p (a b) -> p a b", b=T), ACT.Copy).then_inc(s["c_xtc"], 1)
                act.wait_ge(s["c_gt"], b + 1)
                act.activation(gi, S[2][0:H1, 0:T], ACT.Tanh, bias=big15, scale=1.0 / CAP)
                act.activation(gf, S[2][0:H1, T:2 * T], ACT.Tanh, bias=bfg15, scale=1.0 / CAP).then_inc(s["c_tanh"], 1)
                for g in range(2):
                    act.wait_ge(s["c_qk"], b * 2 + g + 1)
                    act.activation(q1[:, g, :], S[g][:, 0:T], ACT.Copy, scale=0.25).then_inc(s["c_q"], 1)
                act.wait_ge(s["c_vog"], b + 1)
                act.activation(eo, Z[:].rearrange("p (a b) -> p a b", b=D), ACT.Exp, scale=-1.0).then_inc(s["c_eo"], 1)
                act.wait_ge(s["c_tanh"], b * 3 + 1)
                act.activation(gf, gf, ACT.Exp, scale=-CAP).then_inc(s["c_tanh"], 1)
                act.wait_ge(s["c_tanh"], b * 3 + 2)
                act.activation(gls, gf, ACT.Ln, bias=1.0).then_inc(s["c_ls"], 1)
                act.wait_ge(s["c_gcol"], b + 1)
                act.activation(em, S[3][:, 16:32].rearrange("p (a b) -> p a b", b=H1), ACT.Exp,
                               scale=-1.0).then_inc(s["c_em"], 1)
                for h in range(H1):
                    act.wait_ge(s["c_sd"], b * H1 + h + 1)
                    if h >= 2:
                        act.wait_ge(s["c_w"], b * H1 + h - 1)
                    act.activation(dec[h % 2][:, 0:256], S[2 + h % 2][:, 0:256], ACT.Exp, bias=gcol[:, 0, h:h + 1])
                    act.activation(dec[h % 2][:, 256:384], S[2 + h % 2][:, 256:384], ACT.Exp,
                                   bias=gcol[:, 1, h:h + 1]).then_inc(s["c_dec"], 1)
                act.wait_ge(s["c_hoT"], b + 1)
                act.activation(hT, T0[:].rearrange("p (a b) -> p a b", b=T), ACT.Copy).then_inc(s["c_hoTc"], 1)
                act.wait_ge(s["c_x4t"], b + 1)
                act.activation(xall[:, :, bass.ds(b * T, T)], T0[:].rearrange("p (a b) -> p a b", b=T),
                               ACT.Copy).then_inc(s["c_xall"], 1)
                act.nop().then_inc(s["c_tanh"], 1)
            with act.Fori(0, NG) as g:
                for q in range(2):
                    for j in range(4):
                        n = g * NI + 4 * q + j
                        act.wait_ge(s["d_gu"], n + 1)
                        if 4 * q + j >= 2:
                            act.wait_ge(s["d_h"], n - 1)
                        act.activation(sgl[j % 2], S[j % 2][:], ACT.Silu).then_inc(s["d_sg"], 1)
                    act.wait_ge(s["d_h"], g * NI + 4 * q + 4)
                    if q:
                        act.wait_ge(s["d_hs"], g * 2 + 1)
                    act.activation(ab, hb[q], ACT.Abs).then_inc(s["d_abs"], 1)

        @block.tensor
        def _(pe):
            def transposes(src, bank):
                for t in range(2):
                    for c in range(KC):
                        last = pe.transpose(bank[:, c * T + t * P:c * T + (t + 1) * P], src[:, t, c * P:(c + 1) * P],
                                            ident[:])
                return last

            def project(dst, lhs, rhs, t):
                for c in range(KC):
                    last = pe.matmul(dst, lhs[:, c, t * P:(t + 1) * P], rhs[:, c, :], start=(c == 0), stop=(c == KC - 1))
                return last

            pe.wait_ge(s["const_done"], 1)
            pe.wait_ge(s["w_a"], 80)
            for n in ("a_xall", "f_post", "c_xall", "d_x"):
                pe.sem_inc(s[n], 1)
            with pe.Fori(0, NB) as b:
                pe.wait_ge(s["a_xn"], b + 1)
                pe.wait_ge(s["a_xall"], b + 1)
                transposes(xn, T0).then_inc(s["a_xt"], 1)
                pe.wait_ge(s["a_xtc"], b + 1)
                for g in range(4):
                    for w, o in ((wq0, 0), (wk0, T)):
                        for c in range(KC):
                            last = pe.matmul(S[g][:, o:o + T], w[:, c, g * P:(g + 1) * P], xnT[:, c, :],
                                             start=(c == 0), stop=(c == KC - 1))
                    last.then_inc(s["a_qk"], 1)
                for t in range(2):
                    last = project(O[:, t * D:(t + 1) * D], xnT, wv0, t)
                last.then_inc(s["a_vps"], 1)
                pe.wait_ge(s["a_q"], b * 4 + 4)
                pe.wait_ge(s["a_k"], b * 4 + 4)

                def scores(u):
                    if u >= 2:
                        pe.wait_ge(s["a_exp"], b * 8 + u - 1)
                    for r in range(2):
                        h = 2 * u + r
                        g, p0 = h // 4, 32 * (h % 4)
                        bank = S[2 * (u % 2) + r]
                        q, k = qT[p0:p0 + HD0, g, :], kT[p0:p0 + HD0, g, :]
                        pe.matmul(bank[:, 0:128], q[:, 0:128], k[:, 0:128], start=True, stop=False)
                        pe.matmul(bank[:, 0:128], identb[:], mask_ts[:], start=False, stop=True)
                        pe.matmul(bank[:, 128:384], q[:, 128:256], k, start=True, stop=True)
                        last = pe.matmul(bank[:, 256:384], identb[:], mask_ts[:], start=False, stop=True,
                                         skip_group_check=True)
                    last.then_inc(s["a_sc"], 1)

                def prob_transposes(u):
                    pe.wait_ge(s["a_exp"], b * 8 + u + 1)
                    if u >= 1:
                        pe.wait_ge(s["a_ptc"], b * 8 + u)
                    for r in range(2):
                        for c in range(3):
                            last = pe.transpose(TB[r][:, c * P:(c + 1) * P], prob[u % 2][:, r, c * P:(c + 1) * P],
                                                ident[:])
                    last.then_inc(s["a_pt"], 1)

                def values(u):
                    pe.wait_ge(s["a_ptc"], b * 8 + u + 1)
                    g = u // 2
                    if u % 2 == 0 and g >= 2:
                        pe.wait_ge(s["a_z"], b * 4 + g - 1)
                    for r in range(2):
                        h = 2 * u + r
                        zb, o = (Z, O)[g % 2], (h % 4) * (HD0 + 1)
                        pt = probT[u % 2][:, r, :]
                        pe.matmul(zb[:, o:o + 17], pt[:, 0:128], vaug[:, 0, h, :], start=True, stop=True)
                        pe.matmul(zb[:, o + 68:o + 85], pt[:, 128:256], vaug[:, 0, h, :], start=True, stop=False)
                        last = pe.matmul(zb[:, o + 68:o + 85], pt[:, 256:384], vaug[:, 1, h, :], start=False, stop=True)
                    last.then_inc(s["a_pv"], 1)

                pe.wait_ge(s["a_v"], b + 1)
                for u in range(10):
                    if u < 8:
                        scores(u)
                    if u >= 2:
                        values(u - 2)
                    if 1 <= u <= 8:
                        prob_transposes(u - 1)
                pe.wait_ge(s["a_z"], b * 4 + 4)
                transposes(z_sb, T0).then_inc(s["a_zt"], 1)
                pe.wait_ge(s["a_ztc"], b + 1)
                for t in range(2):
                    last = project(O[:, t * D:(t + 1) * D], zT, wo0, t)
                last.then_inc(s["a_y"], 1)
                pe.wait_ge(s["a_xn2"], b + 1)
                transposes(xn2, T0).then_inc(s["a_x2t"], 1)
                pe.wait_ge(s["a_x2c"], b + 1)
                for t in range(2):
                    last = project(Z[:, t * E:(t + 1) * E], xn2T, wr, t)
                last.then_inc(s["a_lg"], 1)

            pe.wait_ge(s["a_xm"], NB)
            pe.wait_ge(s["w_te"], 96)
            for c in range(KC):
                last = pe.matmul(S[0][:, 0:NB], te1[:, c, :], xmT[:, c, :], start=(c == 0), stop=(c == KC - 1))
            last.then_inc(s["t_h1"], 1)
            pe.wait_ge(s["t_h1c"], 1)
            pe.matmul(S[1][0:NB, 0:ND], h1T[:], te2[:], start=True, stop=True).then_inc(s["t_lg"], 1)
            pe.wait_ge(s["t_td"], 1)
            pe.transpose(S[2][0:ND, 0:NB], td[:], ident[0:NB, 0:NB]).then_inc(s["t_tT"], 1)
            pe.wait_ge(s["t_tx"], 1)
            for i in range(NB):
                last = pe.matmul(S[3][:, i * E:(i + 1) * E], tdx[:, i, :], aff[:], start=True, stop=True)
            last.then_inc(s["t_dom"], 1)
            pe.wait_ge(s["r_comb"], 1)
            for i in range(NT):
                last = pe.transpose(S[i // 4][0:E, (i % 4) * P:(i % 4 + 1) * P], comb[:, i, :], ident[:])
            last.then_inc(s["r_cT"], 1)
            pe.wait_ge(s["r_split"], 1)
            pe.wait_ge(s["sel_done"], 1)
            pe.wait_ge(s["w_moe"], 96)
            pe.wait_ge(s["a_xall"], NB + 1)

            def group_down(h, w, first, final):
                for t in range(4):
                    bank, o = (Z, O)[t // 2], (t % 2) * D
                    last = pe.matmul(bank[:, o:o + D], h[:, t * P:(t + 1) * P], w, start=(first and t % 2 == 0),
                                     stop=final, skip_group_check=True)
                return last

            NJ = NPAIR + NSH
            with pe.Fori(0, NG) as g:
                def gate_up(j):
                    if j >= 2:
                        pe.wait_ge(s["f_h"], g * NJ + j - 1)
                    wa, wb, jj = (wg, wu, j) if j < NPAIR else (sg_w, su_w, j - NPAIR)
                    for bank, w in ((S[j % 2], wa), (S[2 + j % 2], wb)):
                        for c in range(KC):
                            last = pe.matmul(bank[:], w[:, c, jj * P:(jj + 1) * P], xall[:, c, bass.ds(g * 512, 512)],
                                             start=(c == 0), stop=(c == KC - 1))
                    last.then_inc(s["f_gu"], 1)
                    if j < NPAIR:
                        for n, part in enumerate((c_hi, c_mid, c_lo)):
                            last = pe.matmul(TB[j % 2][:], selE[:, j, :], part[:, bass.ds(g * 512, 512)],
                                             start=(n == 0), stop=(n == 2))
                        last.then_inc(s["f_cb"], 1)

                def down_block(j):
                    pe.wait_ge(s["f_h"], g * NJ + j + 1)
                    if j == 0:
                        pe.wait_ge(s["f_post"], g + 1)
                    w = wd[:, j, :] if j < NPAIR else sd_w[:, j - NPAIR, :]
                    return group_down(hh[j % 2], w, j == 0, j == NJ - 1)

                for j in range(NJ):
                    gate_up(j)
                    if j:
                        down_block(j - 1)
                down_block(NJ - 1).then_inc(s["f_y"], 1)

            pe.wait_ge(s["w_c"], 160)
            pe.wait_ge(s["f_post"], NG + 1)
            with pe.Fori(0, NB) as b:
                pe.wait_ge(s["c_xn"], b + 1)
                pe.wait_ge(s["c_xall"], b + 1)
                transposes(xn, T0).then_inc(s["c_xt"], 1)
                pe.wait_ge(s["c_xtc"], b + 1)
                for w, o in ((wig, 0), (wfg, T)):
                    for c in range(KC):
                        last = pe.matmul(S[2][0:H1, o:o + T], w[:, c, :], xnT[:, c, :], start=(c == 0),
                                         stop=(c == KC - 1))
                last.then_inc(s["c_gt"], 1)
                for g in range(2):
                    for w, o in ((wq1, 0), (wk1, T)):
                        for c in range(KC):
                            last = pe.matmul(S[g][:, o:o + T], w[:, c, g * P:(g + 1) * P], xnT[:, c, :],
                                             start=(c == 0), stop=(c == KC - 1))
                    last.then_inc(s["c_qk"], 1)
                for t in range(2):
                    project(O[:, t * D:(t + 1) * D], xnT, wv1, t)
                    last = project(Z[:, t * D:(t + 1) * D], xnT, wog1, t)
                last.then_inc(s["c_vog"], 1)
                pe.wait_ge(s["c_gates"], b + 1)
                hold(pe, "turn_t")
                for i, src in enumerate((gG, gm)):
                    for t in range(2):
                        o = (2 * i + t) * H1
                        last = pe.transpose(S[3][:, o:o + H1], src[:, t * P:(t + 1) * P], ident[0:H1, 0:H1])
                last.then_inc(s["c_gT"], 1)
                pe.wait_ge(s["c_q"], b * 2 + 2)
                pe.wait_ge(s["c_k"], b * 2 + 2)
                pe.wait_ge(s["c_gcol"], b + 1)
                pe.wait_ge(s["c_em"], b + 1)

                def scores1(h):
                    if h >= 2:
                        pe.wait_ge(s["c_w"], b * H1 + h - 1)
                    g, p0 = h // 4, 32 * (h % 4)
                    q, k = q1[p0:p0 + QK1, g, :], k1[p0:p0 + QK1, g, :]
                    sc, dc = S[h % 2], S[2 + h % 2]
                    pe.matmul(sc[:, 0:256], k[:, 0:128], q, start=True, stop=True)
                    pe.matmul(sc[:, 256:384], k[:, 128:256], q[:, 128:256], start=True, stop=True)
                    for o, t0 in ((0, 0), (256, 128)):
                        pe.matmul(dc[:, o:o + 256 - t0], sel1[:, h, :], gA[:, t0:256], start=True, stop=True)
                        last = pe.matmul(dc[:, o:o + 128], identb[:], mask_st[:], start=False, stop=True,
                                         skip_group_check=True)
                    last.then_inc(s["c_sd"], 1)

                def values1(h):
                    pe.wait_ge(s["c_w"], b * H1 + h + 1)
                    o = h * (DV1 + 1)
                    w = wt[h % 2]
                    pe.matmul(Z[:, o:o + 33], w[:, 0:128], v1[:, 0, h, :], start=True, stop=True)
                    pe.matmul(O[:, o:o + 33], w[:, 128:256], v1[:, 0, h, :], start=True, stop=False)
                    return pe.matmul(O[:, o:o + 33], w[:, 256:384], v1[:, 1, h, :], start=False, stop=True)

                for h in range(H1 + 1):
                    if h < H1:
                        scores1(h)
                    if h == 1:
                        pe.wait_ge(s["c_v"], b + 1)
                        pe.wait_ge(s["c_eo"], b + 1)
                    if h:
                        last = values1(h - 1)
                last.then_inc(s["c_pv"], 1)
                pe.wait_ge(s["c_ho"], b + 1)
                transposes(hn, T0).then_inc(s["c_hoT"], 1)
                pe.wait_ge(s["c_hoTc"], b + 1)
                for t in range(2):
                    last = project(T1[:, t * D:(t + 1) * D], hT, wo1, t)
                last.then_inc(s["c_y"], 1)
                pe.wait_ge(s["c_xn4"], b + 1)
                transposes(xn4, T0).then_inc(s["c_x4t"], 1)

            pe.wait_ge(s["w_d"], 48)
            pe.wait_ge(s["c_xall"], NB + 1)
            with pe.Fori(0, NG) as g:
                def gate_up2(n):
                    if n >= 2:
                        pe.wait_ge(s["d_h"], g * NI + n - 1)
                    for bank, w in ((S[n % 2], gate), (S[2 + n % 2], up)):
                        for c in range(KC):
                            last = pe.matmul(bank[:], w[:, c, n * P:(n + 1) * P], xall[:, c, bass.ds(g * 512, 512)],
                                             start=(c == 0), stop=(c == KC - 1))
                    last.then_inc(s["d_gu"], 1)

                def down2(q):
                    pe.wait_ge(s["d_hs"], g * 2 + q + 1)
                    for j in range(4):
                        last = group_down(hs[q][:, j, :], down[:, 4 * q + j, :], q == 0 and j == 0, q == 1 and j == 3)
                    return last

                for n in range(NI):
                    gate_up2(n)
                pe.wait_ge(s["d_x"], g + 1)
                down2(0)
                down2(1).then_inc(s["d_y"], 1)

        @block.vector
        def _(dve):
            def ln_stats(srcs, event, ch):
                hold(dve, "turn_v")
                for t, src in enumerate(srcs):
                    last = dve.bn_stats(st[:, t, :], src)
                ch(last)
                hold(dve, "turn_v")
                for t in range(2):
                    last = dve.bn_aggr(mv[:, t, :], st[:, t, :])
                last.then_inc(s["ln_mv"], 1)
                dve.wait_ge(s["ln_rs"], event + 1)

            def ln_apply(dsts, srcs):
                for t, (dst, src) in enumerate(zip(dsts, srcs)):
                    last = dve.tensor_scalar(dst, src, mv[:, t, 0:1], rstd[:, t:t + 1], ALU.subtract, ALU.mult)
                return last

            def tile(i):
                return x_sb[:, bass.ds(i, 1), :].squeeze(1)

            dve.wait_ge(s["x_in"], 16)
            PER = 9
            with dve.Fori(0, NB) as b:
                ch = Chain(dve, s["cha"], b * PER)
                rows = [tile(2 * b + t) for t in range(2)]
                ln_stats(rows, b * 3, ch)
                ln_apply([xn[:, t, :] for t in range(2)], rows).then_inc(s["a_xn"], 1)
                for g in range(4):
                    dve.wait_ge(s["a_q"], b * 4 + g + 1)
                    dve.tensor_copy(kT[:, g, :], S[g][:, T:2 * T]).then_inc(s["a_k"], 1)
                dve.wait_ge(s["a_vps"], b + 1)
                dve.wait_ge(s["const_done"], 1)
                dve.tensor_copy(vaug[:, :, :, 0:HD0].rearrange("p t h e -> p (t h) e"),
                                O[:].rearrange("p (h e) -> p h e", e=HD0)).then_inc(s["a_v"], 1)

                def maxima(u):
                    dve.wait_ge(s["a_sc"], b * 8 + u + 1)
                    for r in range(2):
                        h = 2 * u + r
                        bank = S[2 * (u % 2) + r]
                        dve.tensor_reduce(negmax[:, 0, h:h + 1], bank[:, 0:128], AXX, ALU.max, negate=True)
                        last = dve.tensor_reduce(negmax[:, 1, h:h + 1], bank[:, 128:384], AXX, ALU.max, negate=True)
                    last.then_inc(s["a_mx"], 1)

                def copies(u):
                    dve.wait_ge(s["a_pt"], b * 8 + u + 1)
                    for r in range(2):
                        last = dve.tensor_copy(probT[u % 2][:, r, :], TB[r][:, 0:384])
                    last.then_inc(s["a_ptc"], 1)

                def normalise(g):
                    dve.wait_ge(s["a_pv"], b * 8 + 2 * g + 2)
                    zz = (Z, O)[g % 2][:, 0:136].rearrange("p (t h e) -> p t h e", t=2, e=HD0 + 1)
                    ch(dve.reciprocal(rden, zz[:, :, :, HD0]))
                    dve.tensor_tensor(z_sb[:, :, g * 64:(g + 1) * 64].rearrange("p t (h e) -> p t h e", e=HD0),
                                      zz[:, :, :, 0:HD0], bc(rden.unsqueeze(3), [P, 2, 4, HD0]),
                                      ALU.mult).then_inc(s["a_z"], 1)

                for u in range(10):
                    if u < 8:
                        maxima(u)
                    if u >= 4 and u % 2 == 0:
                        normalise(u // 2 - 2)
                    if 1 <= u <= 8:
                        copies(u - 1)
                normalise(3)
                dve.wait_ge(s["a_y"], b + 1)
                ys = [O[:, t * D:(t + 1) * D] for t in range(2)]
                ln_stats(ys, b * 3 + 1, ch)
                ch(ln_apply([tmp[:, t, :] for t in range(2)], ys))
                both = x_sb[:, bass.ds(2 * b, 2), :]
                ch(dve.tensor_tensor(both, both, tmp, ALU.add))
                ln_stats(rows, b * 3 + 2, ch)
                ln_apply([xn2[:, t, :] for t in range(2)], rows).then_inc(s["a_xn2"], 1)
                dve.wait_ge(s["a_x2c"], b + 1)
                dve.tensor_reduce(xmT[:, :, bass.ds(b, 1)], xn2T, AXX,
                                  ALU.add).then_inc(s["a_xm"], 1)
                dve.wait_ge(s["a_lg"], b + 1)
                dve.tensor_copy(lg_all[:, bass.ds(2 * b, 2), :],
                                Z[:, 0:2 * E].rearrange("p (t e) -> p t e", e=E)).then_inc(s["a_lgc"], 1)
                assert ch.n == PER, ch.n

            ch = Chain(dve, s["chr"])
            dve.wait_ge(s["w_te"], 96)
            dve.wait_ge(s["t_lg"], 1)
            ch(dve.tensor_tensor(tl[:], S[1][0:NB, 0:ND], te_b2[:], ALU.add))
            ch(dve.tensor_reduce(tm[:], tl[:], AXX, ALU.max, negate=True))
            dve.tensor_scalar(tl[:], tl[:], tm[:, 0:1], None, ALU.add).then_inc(s["t_sub"], 1)
            dve.wait_ge(s["t_exp"], 1)
            ch(dve.tensor_reduce(tm[:], td[:], AXX, ALU.add))
            ch(dve.reciprocal(tm[:], tm[:]))
            dve.tensor_scalar(td[:], td[:], tm[:, 0:1], None, ALU.mult).then_inc(s["t_td"], 1)
            dve.wait_ge(s["t_tT"], 1)
            dve.tensor_copy(tdx, bc(S[2][0:ND, 0:NB].unsqueeze(2), [ND, NB, P])).then_inc(s["t_tx"], 1)
            dve.wait_ge(s["t_dom"], 1)
            ch(dve.tensor_scalar(dom[:].rearrange("p b e -> p (b e)"), S[3][:], 0.5, None, ALU.mult))
            dve.wait_ge(s["a_lgc"], NB)
            ch(dve.tensor_tensor(lg.rearrange("p (b t) e -> p b t e", t=2),
                                 lg_all[:].rearrange("p (b t) e -> p b t e", t=2),
                                 bc(dom[:].unsqueeze(2), [P, NB, 2, E]), ALU.add))
            dve.tensor_tensor(rsel, lg, bc(rbias[:].unsqueeze(1), [P, NT, E]), ALU.add)
            ch(dve.tensor_reduce(rmx[:], lg, AXX, ALU.max))
            for i in range(NT):
                last = dve.max(top[:, i, :], rsel[:, i, :])
            ch(last)
            for i in range(NT):
                last = dve.max_index(topi[:, i, :], top[:, i, :], rsel[:, i, :])
            ch(last)
            ch(dve.tensor_copy(topf[:], topi[:]))
            dve.tensor_tensor(lg, lg, bc(rmx[:].unsqueeze(2), [P, NT, E]), ALU.subtract).then_inc(s["r_sub"], 1)
            iob = bc(iota[:].unsqueeze(1), [P, NT, E])
            for k in range(TOPK):
                dst = rmask if k == 0 else rsel
                ch(dve.tensor_tensor(dst, iob, bc(topf[:, :, k:k + 1], [P, NT, E]), ALU.is_equal))
                if k:
                    ch(dve.tensor_tensor(rmask, rmask, rsel, ALU.add))
            dve.wait_ge(s["r_exp"], 1)
            ch(dve.tensor_reduce(rZ[:], comb, AXX, ALU.add))
            ch(dve.tensor_tensor(comb, comb, rmask, ALU.mult))
            ch(dve.tensor_reduce(rS[:], comb, AXX, ALU.add))
            ch(dve.scalar_tensor_tensor(rS[:], rZ[:], 1e-8, rS[:], ALU.mult, ALU.add))
            ch(dve.reciprocal(rS[:], rS[:]))
            dve.tensor_tensor(comb, comb, bc(rS[:].unsqueeze(2), [P, NT, E]), ALU.mult).then_inc(s["r_comb"], 1)
            dve.wait_ge(s["r_cT"], 1)
            for i in range(4):
                cols = slice(i * 512, (i + 1) * 512)
                ch(dve.tensor_copy(c_hi[:, cols], S[i][0:E, :]))
                ch(dve.tensor_tensor(b_tmp[0:E, :], S[i][0:E, :], c_hi[:, cols], ALU.subtract))
                ch(dve.tensor_copy(c_mid[:, cols], b_tmp[0:E, :]))
                last = dve.tensor_tensor(c_lo[:, cols], b_tmp[0:E, :], c_mid[:, cols], ALU.subtract)
                if i < 3:
                    ch(last)
            last.then_inc(s["r_split"], 1)

            def group_residual(g, event, ch, done):
                for k, bank in enumerate((Z, O)):
                    ys = [bank[:, t * D:(t + 1) * D] for t in range(2)]
                    ln_stats(ys, event + k, ch)
                    ch(ln_apply([tmp4[:, 2 * k + t, :] for t in range(2)], ys))
                rows = x_sb[:, bass.ds(4 * g, 4), :]
                dve.tensor_tensor(rows, rows, tmp4, ALU.add).then_inc(done, 1)

            NJ = NPAIR + NSH
            PERB = NPAIR + 4
            with dve.Fori(0, NG) as g:
                ch = Chain(dve, s["chb"], g * PERB)
                for j in range(NJ):
                    dve.wait_ge(s["f_sg"], g * NJ + j + 1)
                    sg = sgl[j % 2]
                    if j < NPAIR:
                        dve.wait_ge(s["f_cb"], g * NPAIR + j + 1)
                        ch(dve.tensor_tensor(sg, sg, TB[j % 2][:], ALU.mult))
                    dve.tensor_tensor(hh[j % 2], sg, S[2 + j % 2][:], ALU.mult).then_inc(s["f_h"], 1)
                dve.wait_ge(s["f_y"], g + 1)
                group_residual(g, 3 * NB + 2 * g, ch, s["f_post"])
                assert ch.n == PERB, ch.n

            ch = Chain(dve, s["ch0"])
            dve.wait_ge(s["w_c"], 160)
            dve.wait_ge(s["c_ones"], 1)
            dve.tensor_scalar(big15, big, 1.0 / CAP, None, ALU.mult)
            ch(dve.tensor_scalar(bfg15, bfg, 1.0 / CAP, None, ALU.mult))
            base = 3 * NB + 2 * NG
            PERC = 21
            with dve.Fori(0, NB) as b:
                ch = Chain(dve, s["chc"], b * PERC)
                rows = [tile(2 * b + t) for t in range(2)]
                ln_stats(rows, base + b * 3, ch)
                ln_apply([xn[:, t, :] for t in range(2)], rows).then_inc(s["c_xn"], 1)
                for g in range(2):
                    dve.wait_ge(s["c_q"], b * 2 + g + 1)
                    dve.tensor_copy(k1[:, g, :], S[g][:, T:2 * T]).then_inc(s["c_k"], 1)
                dve.wait_ge(s["c_vog"], b + 1)
                dve.tensor_copy(v1[:, :, :, 0:DV1].rearrange("p t h e -> p (t h) e"),
                                O[:].rearrange("p (h e) -> p h e", e=DV1)).then_inc(s["c_v"], 1)
                dve.wait_ge(s["c_ls"], b + 1)
                dve.tensor_scalar(gi, gi, CAP, None, ALU.mult)
                ch(dve.tensor_scalar(gls, gls, -1.0, None, ALU.mult))
                dve.tensor_tensor_scan(gF, ones1, gls, 0.0, ALU.mult, ALU.add)
                ch(dve.tensor_tensor_scan(gm, gls, gi, 0.0, ALU.add, ALU.max))
                dve.tensor_tensor(gA, gF, gm, ALU.subtract)
                dve.tensor_tensor(gG, gi, gF, ALU.subtract).then_inc(s["c_gates"], 1)
                dve.wait_ge(s["c_gT"], b + 1)
                dve.tensor_copy(gcol, S[3][:, 0:16].rearrange("p (a b) -> p a b", b=H1)).then_inc(s["c_gcol"], 1)
                dve.wait_ge(s["c_eo"], b + 1)
                ch(dve.tensor_scalar(eo, eo, 1.0, None, ALU.add))
                ch(dve.reciprocal(eo, eo))
                ch(dve.tensor_tensor(eo, eo, bc(gam.unsqueeze(1), [P, 2, D]), ALU.mult))
                for h in range(H1):
                    dve.wait_ge(s["c_dec"], b * H1 + h + 1)
                    dve.tensor_tensor(wt[h % 2], dec[h % 2], S[h % 2][:, 0:384], ALU.mult).then_inc(s["c_w"], 1)
                dve.wait_ge(s["c_pv"], b + 1)
                dve.wait_ge(s["c_em"], b + 1)
                both = [bank[:, 0:H1 * (DV1 + 1)].rearrange("p (h e) -> p h e", e=DV1 + 1) for bank in (Z, O)]
                for t in range(2):
                    last = dve.tensor_copy(den[:, t, :], both[t][:, :, DV1])
                ch(last)
                ch(dve.scalar_tensor_tensor(den, den, -1.0, den, ALU.mult, ALU.max))
                ch(dve.tensor_tensor(den, den, em, ALU.max))
                ch(dve.tensor_scalar(den, den, HEAD_EPS, None, ALU.add))
                ch(dve.reciprocal(den, den))
                hn4 = hn.rearrange("p t (h e) -> p t h e", e=DV1)
                for t in range(2):
                    last = dve.tensor_tensor(hn4[:, t], both[t][:, :, 0:DV1], bc(den[:, t, :].unsqueeze(2), [P, H1, DV1]),
                                             ALU.mult)
                ch(last)
                hnf = hn.rearrange("p t (h e) -> p (t h) e", e=DV1)
                hcf = hc.rearrange("p t (h e) -> p (t h) e", e=DV1)
                sqf = sq.rearrange("p t (h e) -> p (t h) e", e=DV1)
                ch(dve.tensor_reduce(mu, hnf, AXX, ALU.add))
                ch(dve.tensor_scalar(mu, mu, 1.0 / DV1, None, ALU.mult))
                ch(dve.tensor_tensor(hcf, hnf, bc(mu.unsqueeze(2), [P, 16, DV1]), ALU.subtract))
                ch(dve.tensor_tensor(sq, hc, hc, ALU.mult))
                dve.tensor_reduce(hv, sqf, AXX, ALU.add).then_inc(s["c_hv"], 1)
                ch(dve.tensor_tensor(hc, hc, eo, ALU.mult))
                dve.wait_ge(s["c_hr"], b + 1)
                dve.tensor_tensor(hnf, hcf, bc(hv.unsqueeze(2), [P, 16, DV1]), ALU.mult).then_inc(s["c_ho"], 1)
                dve.wait_ge(s["c_y"], b + 1)
                ys = [T1[:, t * D:(t + 1) * D] for t in range(2)]
                ln_stats(ys, base + b * 3 + 1, ch)
                ch(ln_apply([tmp[:, t, :] for t in range(2)], ys))
                res = x_sb[:, bass.ds(2 * b, 2), :]
                ch(dve.tensor_tensor(res, res, tmp, ALU.add))
                ln_stats(rows, base + b * 3 + 2, ch)
                ln_apply([xn4[:, t, :] for t in range(2)], rows).then_inc(s["c_xn4"], 1)
                assert ch.n == PERC, ch.n

            base += 3 * NB
            PERD = 10
            dve.wait_ge(s["w_d"], 48)
            with dve.Fori(0, NG) as g:
                ch = Chain(dve, s["chd"], g * PERD)
                for q in range(2):
                    for j in range(4):
                        n = 4 * q + j
                        dve.wait_ge(s["d_sg"], g * NI + n + 1)
                        dve.tensor_tensor(hb[q][:, j, :], sgl[n % 2], S[2 + n % 2][:], ALU.mult).then_inc(s["d_h"], 1)
                    dve.wait_ge(s["d_abs"], g * 2 + q + 1)
                    dve.tensor_tensor(c01_23, ab[:, 0::2, :], ab[:, 1::2, :], ALU.is_ge)
                    dve.tensor_tensor(c02_13, ab[:, 0:2, :], ab[:, 2:4, :], ALU.is_ge)
                    dve.tensor_tensor(c03, ab[:, 0, :], ab[:, 3, :], ALU.is_ge)
                    ch(dve.tensor_tensor(c12, ab[:, 1, :], ab[:, 2, :], ALU.is_ge))
                    c01, c23, c02, c13 = c01_23[:, 0], c01_23[:, 1], c02_13[:, 0], c02_13[:, 1]
                    dve.tensor_tensor(half[:, 0], c01, c02, ALU.add)
                    dve.tensor_tensor(half[:, 1], c12, c13, ALU.add)
                    dve.tensor_tensor(half[:, 2], c23, c02, ALU.subtract)
                    ch(dve.tensor_tensor(half[:, 3], c03, c13, ALU.add))
                    dve.tensor_tensor(tally[:, 0], half[:, 0], c03, ALU.add)
                    dve.tensor_tensor(tally[:, 1], half[:, 1], c01, ALU.subtract)
                    dve.tensor_tensor(tally[:, 2], half[:, 2], c12, ALU.subtract)
                    ch(dve.tensor_tensor(tally[:, 3], half[:, 3], c23, ALU.add))
                    for j, (op, least) in enumerate(((ALU.is_ge, 2.0), (ALU.is_ge, 1.0), (ALU.is_ge, 0.0), (ALU.is_le, 1.0))):
                        last = dve.scalar_tensor_tensor(hs[q][:, j, :], tally[:, j], least, hb[q][:, j, :], op, ALU.mult)
                    last.then_inc(s["d_hs"], 1)
                dve.wait_ge(s["d_y"], g + 1)
                group_residual(g, base + 2 * g, ch, s["d_x"])
                assert ch.n == PERD, ch.n


def _laid_out(a):
    def kmajor(w):
        return np.ascontiguousarray(w.reshape(KC, P, -1).transpose(1, 0, 2))

    def heads(w, n, k):
        wt = np.zeros((D, n, 32), w.dtype)
        wt[:, :, :k] = w.T.reshape(D, n, k)
        return kmajor(wt.reshape(D, n * 32))

    def strips(w):
        return np.ascontiguousarray(w.reshape(-1, P, D).transpose(1, 0, 2))

    quads = lambda w: w.reshape(D, 2, P, 4).transpose(0, 1, 3, 2).reshape(D, 1024)
    return {
        "x": a["L0_attn_x"].reshape(NB * T, D),
        "wq0": heads(a["L0_attn_Wq"], H0, HD0), "wk0": heads(a["L0_attn_Wk"], H0, HD0),
        "wv0": kmajor(a["L0_attn_Wv"].T), "wo0": kmajor(a["L0_attn_Wo"].T), "wr": kmajor(a["L0_ffn_Wr"].T),
        "te1": kmajor(a["L0_ffn_te_W1"].T), "te_b1": a["L0_ffn_te_b1"].reshape(P, 1),
        "te2": np.ascontiguousarray(a["L0_ffn_te_W2"].T), "te_b2": a["L0_ffn_te_b2"],
        "aff": np.ascontiguousarray(a["L0_ffn_affinity"].T), "rbias": a["L0_ffn_router_bias"],
        "wg": kmajor(a["L0_ffn_Wg"].transpose(1, 0, 2).reshape(D, E * FE)),
        "wu": kmajor(a["L0_ffn_Wu"].transpose(1, 0, 2).reshape(D, E * FE)),
        "wd": strips(a["L0_ffn_Wd"].reshape(E * FE, D)),
        "sg": kmajor(a["L0_ffn_Sg"].transpose(1, 0, 2).reshape(D, 512)),
        "su": kmajor(a["L0_ffn_Su"].transpose(1, 0, 2).reshape(D, 512)),
        "sd": strips(a["L0_ffn_Sd"].reshape(512, D)),
        "wq1": heads(a["L1_attn_Wq"], H1, QK1), "wk1": heads(a["L1_attn_Wk"], H1, QK1),
        "wv1": kmajor(a["L1_attn_Wv"].T), "wog1": kmajor(a["L1_attn_Wog"].T), "wo1": kmajor(a["L1_attn_Wout"].T),
        "wig": kmajor(a["L1_attn_Wig"].T), "wfg": kmajor(a["L1_attn_Wfg"].T),
        "big": a["L1_attn_big"].reshape(H1, 1), "bfg": a["L1_attn_bfg"].reshape(H1, 1),
        "gam": a["L1_attn_gamma"].reshape(D),
        "gate": kmajor(quads(a["L1_ffn_w_gate"])), "up": kmajor(quads(a["L1_ffn_w_up"])),
        "down": np.ascontiguousarray(a["L1_ffn_w_down"].reshape(2, P, 4, D).transpose(1, 0, 2, 3).reshape(P, NI, D)),
    }


def kernel(**inputs):
    import concourse.bacc as bacc
    from concourse.bass_utils import run_bass_kernel_spmd

    nc = bacc.Bacc("TRN2", target_bir_lowering=False, num_devices=1)
    arrays, io = {}, {}
    for name, v in _laid_out({k: np.asarray(v) for k, v in inputs.items()}).items():
        arrays[f"in_{name}"] = np.ascontiguousarray(v)
        io[name] = nc.dram_tensor(f"in_{name}", v.shape, mybir.dt.from_np(v.dtype), kind="ExternalInput").ap()
    out = nc.dram_tensor("out", (NB * T, D), F32, kind="ExternalOutput").ap()
    build(nc, io, out)
    r = run_bass_kernel_spmd(nc, [arrays], core_ids=[0])
    return r.results[0]["out"].reshape(NB, T, D)
```

```python
from contextlib import ExitStack

import numpy as np
import concourse.bass as bass
from concourse import mybir

ALU = mybir.AluOpType
ACT = mybir.ActivationFunctionType
AXX = mybir.AxisListType.X
F32 = mybir.dt.float32
BF16 = mybir.dt.bfloat16
U32 = mybir.dt.uint32

P = 128
NB, T, D = 8, 256, 256
NT = NB * T // P
KC = D // P
NG = NB * T // 512
H0, HD0 = 16, 16
H1, QK1, DV1 = 8, 16, 32
E, FE, TOPK, ND = 64, 64, 4, 4
NPAIR = E // 2
NSH = 4
NI = 8
CAP = 15.0
NEG = -3.0e38
LN_EPS, HEAD_EPS = 1e-5, 1e-6


class Chain:

    def __init__(self, eng, sem, base=0):
        self.eng, self.sem, self.base, self.n = eng, sem, base, 0

    def __call__(self, ins):
        self.n += 1
        ins.then_inc(self.sem, 1)
        self.eng.wait_ge(self.sem, self.base + self.n)


def build(nc, io, out):
    ctx = ExitStack()
    with ctx:
        def sb(name, shape, dt=F32):
            return ctx.enter_context(nc.sbuf_tensor(name, shape, dt))

        def sem(name):
            return ctx.enter_context(nc.semaphore(name))

        S = [ctx.enter_context(nc.psum_tensor(f"S{i}", [P, 512], F32)) for i in range(4)]
        T0 = ctx.enter_context(nc.psum_tensor("T0", [P, 512], F32))
        T1 = ctx.enter_context(nc.psum_tensor("T1", [P, 512], F32))
        Z = ctx.enter_context(nc.psum_tensor("Z", [P, 512], F32))
        O = ctx.enter_context(nc.psum_tensor("O", [P, 512], F32))
        TB = [T0, T1]

        x_sb = sb("x_sb", [P, NT, D])
        xall = sb("xall", [P, KC, NB * T])
        ident = sb("ident", [P, P])
        identb = sb("identb", [P, P], BF16)
        mask_ts = sb("mask_ts", [P, P], BF16)
        mask_st = sb("mask_st", [P, P], BF16)
        sel1 = sb("sel1", [H1, H1, P])
        iota = sb("iota", [P, E])
        mhalf = sb("mhalf", [P, 16])
        mv = sb("mv", [P, 2, 2])
        st = sb("st", [P, 2, 6])
        veps = sb("veps", [P, 2])
        rstd = sb("rstd", [P, 2])

        def views(name, nbytes):
            arena = sb(name, [P, nbytes // 4])
            at = [0]

            def view(shape, dt=F32):
                n = int(np.prod(shape[1:]))
                words = n if dt in (F32, U32) else (n + 1) // 2
                v = arena[0:shape[0], at[0]:at[0] + words]
                at[0] += words
                assert at[0] * 4 <= nbytes, (name, at[0] * 4)
                if dt != F32:
                    v = v.bitcast(dt)
                if len(shape) == 3:
                    v = v.rearrange("p (a b) -> p a b", b=shape[2])
                if len(shape) == 4:
                    v = v.rearrange("p (a b c) -> p a b c", b=shape[2], c=shape[3])
                return v

            def rewind():
                at[0] = 0
            return view, rewind

        view, rewind = views("attn_w", 25 * 512)
        wq0 = view([P, KC, 512])
        wk0 = view([P, KC, 512])
        wv0 = view([P, KC, D])
        wo0 = view([P, KC, D])
        wr = view([P, KC, E])
        rewind()
        wq1 = view([P, KC, 256])
        wk1 = view([P, KC, 256])
        wv1 = view([P, KC, D])
        wog1 = view([P, KC, D])
        wo1 = view([P, KC, D])
        gam = view([P, D])
        wig = view([P, KC, H1])
        wfg = view([P, KC, H1])
        big = view([H1, 1])
        bfg = view([H1, 1])
        big15 = view([H1, 1])
        bfg15 = view([H1, 1])

        view, rewind = views("ffn_w", (96 + 12) * 1024)
        wg = view([P, KC, E * FE])
        wu = view([P, KC, E * FE])
        wd = view([P, NPAIR, D])
        sg_w = view([P, KC, 512])
        su_w = view([P, KC, 512])
        sd_w = view([P, NSH, D])
        rewind()
        gate = view([P, KC, 1024])
        up = view([P, KC, 1024])
        down = view([P, NI, D])
        hb = [view([P, 4, 512]) for _ in range(2)]
        hs = [view([P, 4, 512]) for _ in range(2)]
        ab = view([P, 4, 512])
        c01_23 = view([P, 2, 512], BF16)
        c02_13 = view([P, 2, 512], BF16)
        c03 = view([P, 512], BF16)
        c12 = view([P, 512], BF16)
        tally = view([P, 4, 512], BF16)
        half = view([P, 4, 512], BF16)

        te1 = sb("te1", [P, KC, P])
        te_b1 = sb("te_b1", [P, 1])
        te2 = sb("te2", [P, ND])
        te_b2 = sb("te_b2", [NB, ND])
        aff = sb("aff", [ND, E])
        rbias = sb("rbias", [P, E])
        lg_all = sb("lg_all", [P, NT, E])
        xmT = sb("xmT", [P, KC, NB])

        view, rewind = views("work", 39 * 1024 + 768)
        xn = view([P, 2, D])
        xnT = view([P, KC, T])
        tmp = view([P, 2, D])
        qT = view([P, 4, T])
        kT = view([P, 4, T])
        vpad = view([P, 2, H0, 2 * HD0])
        prob = [view([P, 2, 384]) for _ in range(3)]
        probT = [view([P, 2, 384]) for _ in range(2)]
        negmax = view([P, 2, H0])
        rowsum = view([P, 2, H0])
        zT = view([P, KC, T])
        xn2 = view([P, 2, D])
        xn2T = view([P, KC, T])
        rewind()
        tdx = view([ND, NB, P])
        rewind()
        c_hi = view([E, NB * T], BF16)
        c_mid = view([E, NB * T], BF16)
        c_lo = view([E, NB * T], BF16)
        selE = view([E, NPAIR, P], BF16)
        b_tmp = view([P, 512])
        lg = view([P, NT, E])
        rsel = view([P, NT, E])
        comb = view([P, NT, E])
        rmask = view([P, NT, E])
        rewind()
        for _ in range(3):
            view([E, NB * T], BF16)
        view([E, NPAIR, P], BF16)
        sgl = [view([P, 512]) for _ in range(2)]
        hh = [view([P, 512]) for _ in range(2)]
        tmp4 = view([P, 4, D])
        rewind()
        view([P, 2, D])
        view([P, KC, T])
        view([P, 2, D])
        q1 = view([P, 2, T])
        k1 = view([P, 2, T])
        v1 = view([P, 2, H1, DV1 + 1])
        eo = view([P, 2, D])
        gi = view([H1, T])
        gf = view([H1, T])
        gls = view([H1, T])
        gF = view([H1, T])
        gm = view([H1, T])
        gA = view([H1, T])
        gG = view([H1, T])
        ones1 = view([H1, T])
        gcol = view([P, 2, H1])
        em = view([P, 2, H1])
        dec = [view([P, 384]) for _ in range(2)]
        wt = [view([P, 384]) for _ in range(2)]
        den = view([P, 2, H1])
        hn = view([P, 2, D])
        hc = view([P, 2, D])
        sq = view([P, 2, D])
        hT = view([P, KC, T])
        mu = view([P, 16])
        hv = view([P, 16])
        xn4 = view([P, 2, D])

        top = sb("top", [P, NT, 8])
        topi = sb("topi", [P, NT, 8], U32)
        topf = sb("topf", [P, NT, 8])
        rmx = sb("rmx", [P, NT])
        rZ = sb("rZ", [P, NT])
        rS = sb("rS", [P, NT])
        h1T = sb("h1T", [P, NB])
        tl = sb("tl", [NB, ND])
        tm = sb("tm", [NB, 1])
        td = sb("td", [NB, ND])
        dom = sb("dom", [P, NB, E])

        names = """x_in w_a w_te w_moe w_sh w_c w_d pool_c const_done vones
            ln_mv ln_rs
            a_xn a_xt a_xtc a_qk a_q a_k a_vps a_v a_sc a_mx a_exp a_pt a_ptc a_pv a_z a_zt a_ztc a_y
            a_norm a_yr a_xn2 a_x2t a_x2c a_xall a_xm a_lg a_lgc
            t_h1 t_h1c t_lg t_sub t_exp t_td t_tT t_tx t_dom r_sub r_exp r_comb r_cT r_split sel_done
            f_gu f_sg f_cb f_h f_y f_post
            c_xn c_xt c_xtc c_qk c_q c_k c_vog c_v c_eo c_gt c_tanh c_ef c_ls c_gates c_gT c_gcol c_em
            c_sd c_dec c_w c_pv c_hv c_hr c_ho c_hoT c_hoTc c_y c_xn4 c_x4t c_xall c_ones
            d_gu d_sg d_h d_abs d_hs d_y d_x o_out
            turn_v turn_p turn_t ch0 chc0 cha chr chb chc chd chp chpa chpb chpc chpd""".split()
        s = {n: sem(n) for n in names}

        block = ctx.enter_context(nc.Block())

        def hold(eng, name):
            eng.sem_inc(s[name], 1)

        def halves(bank):
            return bank[:].rearrange("p (a b) -> p a b", b=T)

        def bc(ap, shape):
            return ap.to_broadcast(shape)

        @block.sync
        def _(sp):
            sp.dma_start(x_sb[:], io["x"].rearrange("(n p) d -> p n d", p=P)).then_inc(s["x_in"], 16)
            for dst, name in ((wq0, "wq0"), (wk0, "wk0"), (wv0, "wv0"), (wo0, "wo0"), (wr, "wr")):
                sp.dma_start(dst, io[name]).then_inc(s["w_a"], 16)
            for dst, name in ((te1[:], "te1"), (te_b1[:], "te_b1"), (te2[:], "te2"), (aff[:], "aff")):
                sp.dma_start(dst, io[name]).then_inc(s["w_te"], 16)
            sp.dma_start(te_b2[:], io["te_b2"].partition_broadcast(NB)).then_inc(s["w_te"], 16)
            sp.dma_start(rbias[:], io["rbias"].partition_broadcast(P)).then_inc(s["w_te"], 16)
            for dst, name in ((wg, "wg"), (wu, "wu"), (wd, "wd"), (sg_w, "sg"), (su_w, "su"), (sd_w, "sd")):
                sp.dma_start(dst, io[name]).then_inc(s["w_moe"], 16)
            sp.wait_ge(s["a_lg"], NB)
            for dst, name in ((wq1, "wq1"), (wk1, "wk1"), (wv1, "wv1"), (wog1, "wog1"), (wo1, "wo1"),
                              (wig, "wig"), (wfg, "wfg"), (big, "big"), (bfg, "bfg")):
                sp.dma_start(dst, io[name]).then_inc(s["w_c"], 16)
            sp.dma_start(gam, io["gam"].partition_broadcast(P)).then_inc(s["w_c"], 16)
            sp.wait_ge(s["f_y"], NG)
            for dst, name in ((gate, "gate"), (up, "up"), (down, "down")):
                sp.dma_start(dst, io[name]).then_inc(s["w_d"], 16)
            for g in range(NG):
                sp.wait_ge(s["d_x"], g + 2)
                sp.dma_start(out[g * 512:(g + 1) * 512, :].rearrange("(n p) d -> p n d", p=P),
                             x_sb[:, 4 * g:4 * g + 4, :]).then_inc(s["o_out"], 16)
            sp.wait_ge(s["o_out"], 16 * NG)

        @block.gpsimd
        def _(pool):
            ch = Chain(pool, s["pool_c"])
            pool.memset(ident[:], 0.0)
            pool.memset(identb[:], 0.0)
            pool.memset(mask_ts[:], 0.0)
            pool.memset(mask_st[:], 0.0)
            pool.memset(sel1[:], 0.0)
            pool.memset(mhalf[:], -0.5)
            pool.memset(vpad, 0.0)
            ch(pool.iota(iota[:], [[1, E]], base=0, channel_multiplier=0, allow_small_or_imprecise_dtypes=True))
            for m in (ident, identb):
                pool.affine_select(out=m[:], in_=m[:], compare_op=ALU.not_equal, fill=1.0, base=0,
                                   pattern=[[-1, P]], channel_multiplier=1)
            pool.affine_select(out=mask_ts[:], in_=mask_ts[:], compare_op=ALU.is_ge, fill=NEG, base=0,
                               pattern=[[-1, P]], channel_multiplier=1)
            pool.affine_select(out=mask_st[:], in_=mask_st[:], compare_op=ALU.is_ge, fill=NEG, base=0,
                               pattern=[[1, P]], channel_multiplier=-1)
            pool.affine_select(out=sel1[:], in_=sel1[:], compare_op=ALU.not_equal, fill=1.0, base=0,
                               pattern=[[-1, H1], [0, P]], channel_multiplier=1).then_inc(s["const_done"], 1)

            def ln_event(event, cp):
                pool.wait_ge(s["ln_mv"], event + 1)
                hold(pool, "turn_p")
                cp(pool.tensor_scalar(veps[:], mv[:, :, 1], LN_EPS, None, ALU.add))
                pool.tensor_tensor(rstd[:], veps[:], mhalf[:, 0:2], ALU.pow).then_inc(s["ln_rs"], 1)

            with pool.Fori(0, 3 * NB) as e:
                ln_event(e, Chain(pool, s["chpa"], e))
            cs = Chain(pool, s["chp"])
            pool.wait_ge(s["a_lgc"], NB)
            cs(pool.memset(selE, 0.0))
            cs(pool.affine_select(out=selE[:, :, 0:64], in_=selE[:, :, 0:64], compare_op=ALU.not_equal, fill=1.0,
                                  base=0, pattern=[[-2, NPAIR], [0, 64]], channel_multiplier=1))
            pool.affine_select(out=selE[:, :, 64:128], in_=selE[:, :, 64:128], compare_op=ALU.not_equal, fill=1.0,
                               base=-1, pattern=[[-2, NPAIR], [0, 64]], channel_multiplier=1).then_inc(s["sel_done"], 1)
            with pool.Fori(0, NG) as g:
                cp = Chain(pool, s["chpb"], g * 2)
                for k in range(2):
                    ln_event(3 * NB + g * 2 + k, cp)
            pool.wait_ge(s["f_post"], NG + 1)
            pool.memset(v1, 1.0)
            pool.memset(ones1, 1.0).then_inc(s["c_ones"], 1)
            base = 3 * NB + 2 * NG

            def head_event(b, cp):
                pool.wait_ge(s["c_hv"], b + 1)
                hold(pool, "turn_p")
                cp(pool.tensor_scalar(hv, hv, 1.0 / DV1, HEAD_EPS, ALU.mult, ALU.add))
                pool.tensor_tensor(hv, hv, mhalf[:], ALU.pow).then_inc(s["c_hr"], 1)

            cp = Chain(pool, s["chpc"])
            ln_event(base, cp)
            ln_event(base + 1, cp)
            head_event(0, cp)
            with pool.Fori(1, NB - 1) as b:
                cp = Chain(pool, s["chpc"], b * 4 - 1)
                for k in range(3):
                    ln_event(base + b * 3 - 1 + k, cp)
                head_event(b, cp)
            cp = Chain(pool, s["chpc"], 4 * NB - 5)
            for k in range(2):
                ln_event(base + 3 * NB - 4 + k, cp)
            head_event(NB - 1, cp)
            for k in range(2):
                ln_event(base + 3 * NB - 2 + k, cp)
            with pool.Fori(0, NG) as g:
                cp = Chain(pool, s["chpd"], g * 2)
                for k in range(2):
                    ln_event(base + 3 * NB + g * 2 + k, cp)

        @block.scalar
        def _(act):
            def input_copy(b):
                act.wait_ge(s["a_xt"], b + 1)
                act.activation(xnT, halves(O), ACT.Copy).then_inc(s["a_xtc"], 1)

            def query_copies(b, groups):
                for g in groups:
                    act.wait_ge(s["a_qk"], b * 4 + g + 1)
                    act.activation(qT[:, g, :], S[g][:, 0:T], ACT.Copy, scale=0.25).then_inc(s["a_q"], 1)

            def exponentials(b, u):
                act.wait_ge(s["a_mx"], b * 8 + u + 1)
                if u >= 3:
                    act.wait_ge(s["a_pt"], b * 8 + u - 2)
                for r in range(2):
                    h = 2 * u + r
                    bank = S[2 * (u % 2) + r]
                    act.activation(prob[u % 3][:, r, 0:128], bank[:, 0:128], ACT.Exp, bias=negmax[:, 0, h:h + 1],
                                   accum_out=rowsum[:, 0, h:h + 1])
                    last = act.activation(prob[u % 3][:, r, 128:384], bank[:, 128:384], ACT.Exp,
                                          bias=negmax[:, 1, h:h + 1], accum_out=rowsum[:, 1, h:h + 1])
                last.then_inc(s["a_exp"], 1)

            def next_input_copies(b):
                act.wait_ge(s["a_x2t"], b + 1)
                act.activation(xn2T, halves(O), ACT.Copy).then_inc(s["a_x2c"], 1)
                act.activation(xall[:, :, bass.ds(b * T, T)], halves(O), ACT.Copy).then_inc(s["a_xall"], 1)

            def attention(b, first, last):
                for u in range(8):
                    exponentials(b, u)
                    if u == 2 and not first:
                        next_input_copies(b - 1)
                    if u == 6 and not last:
                        input_copy(b + 1)
                if not last:
                    query_copies(b + 1, range(4))
                act.wait_ge(s["a_pv"], b * 8 + 8)
                act.activation(zT, halves(Z), ACT.Copy).then_inc(s["a_ztc"], 1)

            input_copy(0)
            query_copies(0, range(4))
            attention(0, True, False)
            with act.Fori(1, NB - 1) as b:
                attention(b, False, False)
            attention(NB - 1, False, True)
            next_input_copies(NB - 1)
            act.wait_ge(s["t_h1"], 1)
            act.wait_ge(s["w_te"], 96)
            act.activation(h1T[:], S[0][:, 0:NB], ACT.Gelu, bias=te_b1[:, 0:1], scale=1.0 / T).then_inc(s["t_h1c"], 1)
            act.wait_ge(s["t_sub"], 1)
            act.activation(td[:], tl[:], ACT.Exp).then_inc(s["t_exp"], 1)
            act.wait_ge(s["r_sub"], 1)
            act.activation(comb, lg, ACT.Exp).then_inc(s["r_exp"], 1)
            with act.Fori(0, NG) as g:
                for j in range(NPAIR + NSH):
                    act.wait_ge(s["f_gu"], g * (NPAIR + NSH) + j + 1)
                    if j >= 2:
                        act.wait_ge(s["f_h"], g * (NPAIR + NSH) + j - 1)
                    act.activation(sgl[j % 2], S[j % 2][:], ACT.Silu).then_inc(s["f_sg"], 1)
            def input_copy1(b):
                act.wait_ge(s["c_xt"], b + 1)
                act.activation(xnT, halves(T0), ACT.Copy).then_inc(s["c_xtc"], 1)

            def gate_functions(b):
                act.wait_ge(s["c_gt"], b + 1)
                act.activation(gi, T1[0:H1, 0:T], ACT.Tanh, bias=big15, scale=1.0 / CAP)
                act.activation(gf, T1[0:H1, T:2 * T], ACT.Tanh, bias=bfg15, scale=1.0 / CAP).then_inc(s["c_tanh"], 1)
                act.wait_ge(s["c_tanh"], b + 1)
                act.activation(gf, gf, ACT.Exp, scale=-CAP).then_inc(s["c_ef"], 1)
                act.wait_ge(s["c_ef"], b + 1)
                act.activation(gls, gf, ACT.Ln, bias=1.0).then_inc(s["c_ls"], 1)

            def query_copies1(b):
                for g in range(2):
                    act.wait_ge(s["c_qk"], b * 2 + g + 1)
                    act.activation(q1[:, g, :], S[g][:, 0:T], ACT.Copy, scale=0.25).then_inc(s["c_q"], 1)

            def output_gate(b):
                act.wait_ge(s["c_vog"], b + 1)
                act.activation(eo, halves(S[3]), ACT.Exp, scale=-1.0).then_inc(s["c_eo"], 1)
                act.wait_ge(s["c_gcol"], b + 1)
                act.activation(em, T1[:, 16:32].rearrange("p (a b) -> p a b", b=H1), ACT.Exp,
                               scale=-1.0).then_inc(s["c_em"], 1)

            def final_input_copy(b):
                act.wait_ge(s["c_x4t"], b + 1)
                act.activation(xall[:, :, bass.ds(b * T, T)], halves(T0), ACT.Copy).then_inc(s["c_xall"], 1)

            def mlstm(b, first, last):
                for h in range(H1):
                    act.wait_ge(s["c_sd"], b * H1 + h + 1)
                    if h >= 2:
                        act.wait_ge(s["c_w"], b * H1 + h - 1)
                    act.activation(dec[h % 2][:, 0:256], S[2 + h % 2][:, 0:256], ACT.Exp, bias=gcol[:, 0, h:h + 1])
                    act.activation(dec[h % 2][:, 256:384], S[2 + h % 2][:, 256:384], ACT.Exp,
                                   bias=gcol[:, 1, h:h + 1]).then_inc(s["c_dec"], 1)
                    if h == 3 and not first:
                        final_input_copy(b - 1)
                    if h == 5 and not last:
                        input_copy1(b + 1)
                    if h == 6 and not last:
                        gate_functions(b + 1)
                if not last:
                    query_copies1(b + 1)
                act.wait_ge(s["c_hoT"], b + 1)
                act.activation(hT, halves(T0), ACT.Copy).then_inc(s["c_hoTc"], 1)
                if not last:
                    output_gate(b + 1)

            input_copy1(0)
            gate_functions(0)
            query_copies1(0)
            output_gate(0)
            mlstm(0, True, False)
            with act.Fori(1, NB - 1) as b:
                mlstm(b, False, False)
            mlstm(NB - 1, False, True)
            final_input_copy(NB - 1)
            with act.Fori(0, NG) as g:
                for q in range(2):
                    for j in range(4):
                        n = g * NI + 4 * q + j
                        act.wait_ge(s["d_gu"], n + 1)
                        if 4 * q + j >= 2:
                            act.wait_ge(s["d_h"], n - 1)
                        act.activation(sgl[j % 2], S[j % 2][:], ACT.Silu).then_inc(s["d_sg"], 1)
                    act.wait_ge(s["d_h"], g * NI + 4 * q + 4)
                    if q:
                        act.wait_ge(s["d_hs"], g * 2 + 1)
                    act.activation(ab, hb[q], ACT.Abs).then_inc(s["d_abs"], 1)

        @block.tensor
        def _(pe):
            def transposes(src, bank):
                for t in range(2):
                    for c in range(KC):
                        last = pe.transpose(bank[:, c * T + t * P:c * T + (t + 1) * P], src[:, t, c * P:(c + 1) * P],
                                            ident[:])
                return last

            def project(dst, lhs, rhs, t):
                for c in range(KC):
                    last = pe.matmul(dst, lhs[:, c, t * P:(t + 1) * P], rhs[:, c, :], start=(c == 0), stop=(c == KC - 1))
                return last

            pe.wait_ge(s["const_done"], 1)
            pe.wait_ge(s["w_a"], 80)
            for n in ("a_xall", "f_post", "c_xall", "d_x"):
                pe.sem_inc(s[n], 1)
            def input_transposes(b):
                pe.wait_ge(s["a_xn"], b + 1)
                transposes(xn, O).then_inc(s["a_xt"], 1)

            def project_qk(b, g):
                if g == 0:
                    pe.wait_ge(s["a_xtc"], b + 1)
                for w, o in ((wq0, 0), (wk0, T)):
                    for c in range(KC):
                        last = pe.matmul(S[g][:, o:o + T], w[:, c, g * P:(g + 1) * P], xnT[:, c, :],
                                         start=(c == 0), stop=(c == KC - 1))
                last.then_inc(s["a_qk"], 1)

            def project_v(b):
                for t in range(2):
                    last = project(O[:, t * D:(t + 1) * D], xnT, wv0, t)
                last.then_inc(s["a_vps"], 1)

            def scores(b, u):
                if u >= 2:
                    pe.wait_ge(s["a_exp"], b * 8 + u - 1)
                for r in range(2):
                    h = 2 * u + r
                    g, p0 = h // 4, 32 * (h % 4)
                    bank = S[2 * (u % 2) + r]
                    q, k = qT[p0:p0 + HD0, g, :], kT[p0:p0 + HD0, g, :]
                    pe.matmul(bank[:, 0:128], q[:, 0:128], k[:, 0:128], start=True, stop=False)
                    pe.matmul(bank[:, 0:128], identb[:], mask_ts[:], start=False, stop=True)
                    pe.matmul(bank[:, 128:384], q[:, 128:256], k, start=True, stop=True)
                    last = pe.matmul(bank[:, 256:384], identb[:], mask_ts[:], start=False, stop=True,
                                     skip_group_check=True)
                last.then_inc(s["a_sc"], 1)

            def prob_transposes(b, u, first):
                pe.wait_ge(s["a_norm"], b * 8 + u + 1)
                if u >= 1:
                    pe.wait_ge(s["a_ptc"], b * 8 + u)
                elif not first:
                    pe.wait_ge(s["a_yr"], b)
                for r in range(2):
                    for c in range(3):
                        last = pe.transpose(TB[r][:, c * P:(c + 1) * P], prob[u % 3][:, r, c * P:(c + 1) * P],
                                            ident[:])
                last.then_inc(s["a_pt"], 1)

            def values(b, u):
                pe.wait_ge(s["a_ptc"], b * 8 + u + 1)
                p0, o = 32 * (u % 4), (u // 4) * T
                for r in range(2):
                    h, pt = 2 * u + r, probT[u % 2][:, r, :]
                    pe.matmul(Z[p0:p0 + 32, o:o + T], vpad[:, 0, h, :], pt[:, 0:256], start=(r == 0), stop=True,
                              skip_group_check=True)
                    last = pe.matmul(Z[p0:p0 + 32, o + 128:o + T], vpad[:, 1, h, :], pt[:, 256:384], start=False,
                                     stop=True, skip_group_check=True)
                last.then_inc(s["a_pv"], 1)

            def next_input_transposes(b):
                pe.wait_ge(s["a_xn2"], b + 1)
                transposes(xn2, O).then_inc(s["a_x2t"], 1)

            def router_logits(b):
                pe.wait_ge(s["a_xall"], b + 2)
                for t in range(2):
                    last = project(O[:, t * E:(t + 1) * E], xn2T, wr, t)
                last.then_inc(s["a_lg"], 1)

            def attention(b, first, last):
                pe.wait_ge(s["a_q"], b * 4 + 4)
                pe.wait_ge(s["a_k"], b * 4 + 4)
                for u in range(11):
                    if u < 8:
                        scores(b, u)
                    if u == 0:
                        pe.wait_ge(s["a_v"], b + 1)
                    if 2 <= u <= 9:
                        prob_transposes(b, u - 2, first)
                    if u == 3 and not first:
                        next_input_transposes(b - 1)
                    if u == 4 and not first:
                        router_logits(b - 1)
                    if u == 6 and not last:
                        if not first:
                            pe.wait_ge(s["a_lgc"], b)
                        input_transposes(b + 1)
                    if u >= 3:
                        values(b, u - 3)
                    if u == 8 and not last:
                        pe.wait_ge(s["a_exp"], b * 8 + 7)
                        project_qk(b + 1, 0)
                        project_qk(b + 1, 1)
                    if u == 9 and not last:
                        pe.wait_ge(s["a_exp"], b * 8 + 8)
                        project_qk(b + 1, 2)
                        project_qk(b + 1, 3)
                if not last:
                    project_v(b + 1)
                pe.wait_ge(s["a_ztc"], b + 1)
                for t in range(2):
                    last_mm = project(T1[:, t * D:(t + 1) * D], zT, wo0, t)
                last_mm.then_inc(s["a_y"], 1)

            input_transposes(0)
            for g in range(4):
                project_qk(0, g)
            project_v(0)
            attention(0, True, False)
            with pe.Fori(1, NB - 1) as b:
                attention(b, False, False)
            attention(NB - 1, False, True)
            next_input_transposes(NB - 1)
            router_logits(NB - 1)

            pe.wait_ge(s["a_xm"], NB)
            pe.wait_ge(s["w_te"], 96)
            for c in range(KC):
                last = pe.matmul(S[0][:, 0:NB], te1[:, c, :], xmT[:, c, :], start=(c == 0), stop=(c == KC - 1))
            last.then_inc(s["t_h1"], 1)
            pe.wait_ge(s["t_h1c"], 1)
            pe.matmul(S[1][0:NB, 0:ND], h1T[:], te2[:], start=True, stop=True).then_inc(s["t_lg"], 1)
            pe.wait_ge(s["t_td"], 1)
            pe.transpose(S[2][0:ND, 0:NB], td[:], ident[0:NB, 0:NB]).then_inc(s["t_tT"], 1)
            pe.wait_ge(s["t_tx"], 1)
            for i in range(NB):
                last = pe.matmul(S[3][:, i * E:(i + 1) * E], tdx[:, i, :], aff[:], start=True, stop=True)
            last.then_inc(s["t_dom"], 1)
            pe.wait_ge(s["r_comb"], 1)
            for i in range(NT):
                last = pe.transpose(S[i // 4][0:E, (i % 4) * P:(i % 4 + 1) * P], comb[:, i, :], ident[:])
            last.then_inc(s["r_cT"], 1)
            pe.wait_ge(s["r_split"], 1)
            pe.wait_ge(s["sel_done"], 1)
            pe.wait_ge(s["w_moe"], 96)
            pe.wait_ge(s["a_xall"], NB + 1)

            def group_down(h, w, first, final):
                for t in range(4):
                    bank, o = (Z, O)[t // 2], (t % 2) * D
                    last = pe.matmul(bank[:, o:o + D], h[:, t * P:(t + 1) * P], w, start=(first and t % 2 == 0),
                                     stop=final, skip_group_check=True)
                return last

            NJ = NPAIR + NSH
            with pe.Fori(0, NG) as g:
                def gate_up(j):
                    if j >= 2:
                        pe.wait_ge(s["f_h"], g * NJ + j - 1)
                    wa, wb, jj = (wg, wu, j) if j < NPAIR else (sg_w, su_w, j - NPAIR)
                    for bank, w in ((S[j % 2], wa), (S[2 + j % 2], wb)):
                        for c in range(KC):
                            last = pe.matmul(bank[:], w[:, c, jj * P:(jj + 1) * P], xall[:, c, bass.ds(g * 512, 512)],
                                             start=(c == 0), stop=(c == KC - 1))
                    last.then_inc(s["f_gu"], 1)
                    if j < NPAIR:
                        for n, part in enumerate((c_hi, c_mid, c_lo)):
                            last = pe.matmul(TB[j % 2][:], selE[:, j, :], part[:, bass.ds(g * 512, 512)],
                                             start=(n == 0), stop=(n == 2))
                        last.then_inc(s["f_cb"], 1)

                def down_block(j):
                    pe.wait_ge(s["f_h"], g * NJ + j + 1)
                    if j == 0:
                        pe.wait_ge(s["f_post"], g + 1)
                    w = wd[:, j, :] if j < NPAIR else sd_w[:, j - NPAIR, :]
                    return group_down(hh[j % 2], w, j == 0, j == NJ - 1)

                for j in range(NJ):
                    gate_up(j)
                    if j:
                        down_block(j - 1)
                down_block(NJ - 1).then_inc(s["f_y"], 1)

            pe.wait_ge(s["w_c"], 160)
            pe.wait_ge(s["f_post"], NG + 1)
            def input_transposes1(b):
                pe.wait_ge(s["c_xn"], b + 1)
                transposes(xn, T0).then_inc(s["c_xt"], 1)

            def gates(b):
                pe.wait_ge(s["c_xtc"], b + 1)
                for w, o in ((wig, 0), (wfg, T)):
                    for c in range(KC):
                        last = pe.matmul(T1[0:H1, o:o + T], w[:, c, :], xnT[:, c, :], start=(c == 0),
                                         stop=(c == KC - 1))
                last.then_inc(s["c_gt"], 1)

            def projections(b):
                for g in range(2):
                    for w, o in ((wq1, 0), (wk1, T)):
                        for c in range(KC):
                            last = pe.matmul(S[g][:, o:o + T], w[:, c, g * P:(g + 1) * P], xnT[:, c, :],
                                             start=(c == 0), stop=(c == KC - 1))
                    last.then_inc(s["c_qk"], 1)
                for t in range(2):
                    project(S[2][:, t * D:(t + 1) * D], xnT, wv1, t)
                    last = project(S[3][:, t * D:(t + 1) * D], xnT, wog1, t)
                last.then_inc(s["c_vog"], 1)

            def gate_columns(b):
                pe.wait_ge(s["c_gates"], b + 1)
                hold(pe, "turn_t")
                for i, src in enumerate((gG, gm)):
                    for t in range(2):
                        o = (2 * i + t) * H1
                        last = pe.transpose(T1[:, o:o + H1], src[:, t * P:(t + 1) * P], ident[0:H1, 0:H1])
                last.then_inc(s["c_gT"], 1)

            def scores1(b, h):
                if h >= 2:
                    pe.wait_ge(s["c_w"], b * H1 + h - 1)
                g, p0 = h // 4, 32 * (h % 4)
                q, k = q1[p0:p0 + QK1, g, :], k1[p0:p0 + QK1, g, :]
                sc, dc = S[h % 2], S[2 + h % 2]
                pe.matmul(sc[:, 0:256], k[:, 0:128], q, start=True, stop=True)
                pe.matmul(sc[:, 256:384], k[:, 128:256], q[:, 128:256], start=True, stop=True)
                for o, t0 in ((0, 0), (256, 128)):
                    pe.matmul(dc[:, o:o + 256 - t0], sel1[:, h, :], gA[:, t0:256], start=True, stop=True)
                    last = pe.matmul(dc[:, o:o + 128], identb[:], mask_st[:], start=False, stop=True,
                                     skip_group_check=True)
                last.then_inc(s["c_sd"], 1)

            def values1(b, h):
                pe.wait_ge(s["c_w"], b * H1 + h + 1)
                o = h * (DV1 + 1)
                w = wt[h % 2]
                pe.matmul(Z[:, o:o + 33], w[:, 0:128], v1[:, 0, h, :], start=True, stop=True)
                pe.matmul(O[:, o:o + 33], w[:, 128:256], v1[:, 0, h, :], start=True, stop=False)
                return pe.matmul(O[:, o:o + 33], w[:, 256:384], v1[:, 1, h, :], start=False, stop=True)

            def final_input_transposes(b):
                pe.wait_ge(s["c_xn4"], b + 1)
                transposes(xn4, T0).then_inc(s["c_x4t"], 1)

            def mlstm(b, first, last):
                pe.wait_ge(s["c_q"], b * 2 + 2)
                pe.wait_ge(s["c_k"], b * 2 + 2)
                pe.wait_ge(s["c_v"], b + 1)
                pe.wait_ge(s["c_em"], b + 1)
                for h in range(H1 + 1):
                    if h < H1:
                        scores1(b, h)
                    if h == 3 and not first:
                        final_input_transposes(b - 1)
                    if h == 5 and not last:
                        if not first:
                            pe.wait_ge(s["c_xall"], b + 1)
                        input_transposes1(b + 1)
                    if h == 6 and not last:
                        gates(b + 1)
                    if h:
                        last_mm = values1(b, h - 1)
                last_mm.then_inc(s["c_pv"], 1)
                if not last:
                    projections(b + 1)
                    gate_columns(b + 1)
                pe.wait_ge(s["c_ho"], b + 1)
                transposes(hn, T0).then_inc(s["c_hoT"], 1)
                pe.wait_ge(s["c_hoTc"], b + 1)
                for t in range(2):
                    last_mm = project(T0[:, t * D:(t + 1) * D], hT, wo1, t)
                last_mm.then_inc(s["c_y"], 1)

            input_transposes1(0)
            gates(0)
            projections(0)
            gate_columns(0)
            mlstm(0, True, False)
            with pe.Fori(1, NB - 1) as b:
                mlstm(b, False, False)
            mlstm(NB - 1, False, True)
            final_input_transposes(NB - 1)

            pe.wait_ge(s["w_d"], 48)
            pe.wait_ge(s["c_xall"], NB + 1)
            with pe.Fori(0, NG) as g:
                def gate_up2(n):
                    if n >= 2:
                        pe.wait_ge(s["d_h"], g * NI + n - 1)
                    for bank, w in ((S[n % 2], gate), (S[2 + n % 2], up)):
                        for c in range(KC):
                            last = pe.matmul(bank[:], w[:, c, n * P:(n + 1) * P], xall[:, c, bass.ds(g * 512, 512)],
                                             start=(c == 0), stop=(c == KC - 1))
                    last.then_inc(s["d_gu"], 1)

                def down2(q):
                    pe.wait_ge(s["d_hs"], g * 2 + q + 1)
                    for j in range(4):
                        last = group_down(hs[q][:, j, :], down[:, 4 * q + j, :], q == 0 and j == 0, q == 1 and j == 3)
                    return last

                for n in range(NI):
                    gate_up2(n)
                pe.wait_ge(s["d_x"], g + 1)
                down2(0)
                down2(1).then_inc(s["d_y"], 1)

        @block.vector
        def _(dve):
            def ln_stats(srcs, event, ch):
                hold(dve, "turn_v")
                for t, src in enumerate(srcs):
                    last = dve.bn_stats(st[:, t, :], src)
                ch(last)
                hold(dve, "turn_v")
                for t in range(2):
                    last = dve.bn_aggr(mv[:, t, :], st[:, t, :])
                last.then_inc(s["ln_mv"], 1)
                dve.wait_ge(s["ln_rs"], event + 1)

            def ln_apply(dsts, srcs):
                for t, (dst, src) in enumerate(zip(dsts, srcs)):
                    last = dve.tensor_scalar(dst, src, mv[:, t, 0:1], rstd[:, t:t + 1], ALU.subtract, ALU.mult)
                return last

            def tile(i):
                return x_sb[:, bass.ds(i, 1), :].squeeze(1)

            dve.wait_ge(s["x_in"], 16)
            def input_norm(b, ch):
                rows = [tile(2 * b + t) for t in range(2)]
                ln_stats(rows, event(b), ch)
                ln_apply([xn[:, t, :] for t in range(2)], rows).then_inc(s["a_xn"], 1)

            def key_copies(b):
                for g in range(4):
                    dve.wait_ge(s["a_q"], b * 4 + g + 1)
                    dve.tensor_copy(kT[:, g, :], S[g][:, T:2 * T]).then_inc(s["a_k"], 1)

            def value_copy(b):
                dve.wait_ge(s["a_vps"], b + 1)
                for r in range(2):
                    last = dve.tensor_copy(
                        vpad[:, :, r::2, r * HD0:(r + 1) * HD0].rearrange("p t h e -> p (t h) e"),
                        O[:].rearrange("p (t h r e) -> p (t h) r e", t=2, r=2, e=HD0)[:, :, r, :])
                last.then_inc(s["a_v"], 1)

            def maxima(b, u):
                dve.wait_ge(s["a_sc"], b * 8 + u + 1)
                for r in range(2):
                    h = 2 * u + r
                    bank = S[2 * (u % 2) + r]
                    dve.tensor_reduce(negmax[:, 0, h:h + 1], bank[:, 0:128], AXX, ALU.max, negate=True)
                    last = dve.tensor_reduce(negmax[:, 1, h:h + 1], bank[:, 128:384], AXX, ALU.max, negate=True)
                last.then_inc(s["a_mx"], 1)

            def normalise(b, u, ch):
                dve.wait_ge(s["a_exp"], b * 8 + u + 1)
                sums = rowsum[:, :, 2 * u:2 * u + 2]
                ch(dve.reciprocal(sums, sums))
                for r in range(2):
                    h, pr = 2 * u + r, prob[u % 3][:, r, :]
                    dve.tensor_scalar(pr[:, 0:128], pr[:, 0:128], rowsum[:, 0, h:h + 1], None, ALU.mult)
                    last = dve.tensor_scalar(pr[:, 128:384], pr[:, 128:384], rowsum[:, 1, h:h + 1], None, ALU.mult)
                last.then_inc(s["a_norm"], 1)

            def copies(b, u):
                dve.wait_ge(s["a_pt"], b * 8 + u + 1)
                for r in range(2):
                    last = dve.tensor_copy(probT[u % 2][:, r, :], TB[r][:, 0:384])
                last.then_inc(s["a_ptc"], 1)

            def residual(b, ch):
                rows = [tile(2 * b + t) for t in range(2)]
                dve.wait_ge(s["a_y"], b + 1)
                ys = [T1[:, t * D:(t + 1) * D] for t in range(2)]
                ln_stats(ys, post_event(b), ch)
                ch(ln_apply([tmp[:, t, :] for t in range(2)], ys))
                both = x_sb[:, bass.ds(2 * b, 2), :]
                dve.sem_inc(s["a_yr"], 1)
                ch(dve.tensor_tensor(both, both, tmp, ALU.add))
                ln_stats(rows, post_event(b) + 1, ch)
                ln_apply([xn2[:, t, :] for t in range(2)], rows).then_inc(s["a_xn2"], 1)

            def router_copies(b):
                dve.wait_ge(s["a_x2c"], b + 1)
                dve.tensor_reduce(xmT[:, :, bass.ds(b, 1)], xn2T, AXX, ALU.add).then_inc(s["a_xm"], 1)
                dve.wait_ge(s["a_lg"], b + 1)
                dve.tensor_copy(lg_all[:, bass.ds(2 * b, 2), :],
                                O[:, 0:2 * E].rearrange("p (t e) -> p t e", e=E)).then_inc(s["a_lgc"], 1)

            def event(b):
                return b if isinstance(b, int) and b == 0 else 3 * b - 2

            def post_event(b):
                return 3 * b + (1 if isinstance(b, int) and b == NB - 1 else 2)

            def attention(b, first, last):
                ch = Chain(dve, s["cha"], A_LINKS(b))
                for u in range(11):
                    if u < 8:
                        maxima(b, u)
                    if u == 1 and not first:
                        residual(b - 1, ch)
                    if 1 <= u <= 8:
                        normalise(b, u - 1, ch)
                    if u == 5 and not first:
                        router_copies(b - 1)
                    if u == 5 and not last:
                        input_norm(b + 1, ch)
                    if 2 <= u <= 9:
                        copies(b, u - 2)
                if not last:
                    key_copies(b + 1)
                    value_copy(b + 1)
                return ch.n

            ch = Chain(dve, s["ch0"])
            input_norm(0, ch)
            key_copies(0)
            dve.wait_ge(s["const_done"], 1)
            value_copy(0)
            def A_LINKS(b):
                return 0 if isinstance(b, int) and b == 0 else 9 + (b - 1) * 13
            assert attention(0, True, False) == 9
            with dve.Fori(1, NB - 1) as b:
                assert attention(b, False, False) == 13
            n = attention(NB - 1, False, True)
            ch = Chain(dve, s["cha"], A_LINKS(NB - 1) + n)
            residual(NB - 1, ch)
            router_copies(NB - 1)

            ch = Chain(dve, s["chr"])
            dve.wait_ge(s["w_te"], 96)
            dve.wait_ge(s["t_lg"], 1)
            ch(dve.tensor_tensor(tl[:], S[1][0:NB, 0:ND], te_b2[:], ALU.add))
            ch(dve.tensor_reduce(tm[:], tl[:], AXX, ALU.max, negate=True))
            dve.tensor_scalar(tl[:], tl[:], tm[:, 0:1], None, ALU.add).then_inc(s["t_sub"], 1)
            dve.wait_ge(s["t_exp"], 1)
            ch(dve.tensor_reduce(tm[:], td[:], AXX, ALU.add))
            ch(dve.reciprocal(tm[:], tm[:]))
            dve.tensor_scalar(td[:], td[:], tm[:, 0:1], None, ALU.mult).then_inc(s["t_td"], 1)
            dve.wait_ge(s["t_tT"], 1)
            dve.tensor_copy(tdx, bc(S[2][0:ND, 0:NB].unsqueeze(2), [ND, NB, P])).then_inc(s["t_tx"], 1)
            dve.wait_ge(s["t_dom"], 1)
            ch(dve.tensor_scalar(dom[:].rearrange("p b e -> p (b e)"), S[3][:], 0.5, None, ALU.mult))
            dve.wait_ge(s["a_lgc"], NB)
            ch(dve.tensor_tensor(lg.rearrange("p (b t) e -> p b t e", t=2),
                                 lg_all[:].rearrange("p (b t) e -> p b t e", t=2),
                                 bc(dom[:].unsqueeze(2), [P, NB, 2, E]), ALU.add))
            dve.tensor_tensor(rsel, lg, bc(rbias[:].unsqueeze(1), [P, NT, E]), ALU.add)
            ch(dve.tensor_reduce(rmx[:], lg, AXX, ALU.max))
            for i in range(NT):
                last = dve.max(top[:, i, :], rsel[:, i, :])
            ch(last)
            for i in range(NT):
                last = dve.max_index(topi[:, i, :], top[:, i, :], rsel[:, i, :])
            ch(last)
            ch(dve.tensor_copy(topf[:], topi[:]))
            dve.tensor_tensor(lg, lg, bc(rmx[:].unsqueeze(2), [P, NT, E]), ALU.subtract).then_inc(s["r_sub"], 1)
            iob = bc(iota[:].unsqueeze(1), [P, NT, E])
            for k in range(TOPK):
                dst = rmask if k == 0 else rsel
                ch(dve.tensor_tensor(dst, iob, bc(topf[:, :, k:k + 1], [P, NT, E]), ALU.is_equal))
                if k:
                    ch(dve.tensor_tensor(rmask, rmask, rsel, ALU.add))
            dve.wait_ge(s["r_exp"], 1)
            ch(dve.tensor_reduce(rZ[:], comb, AXX, ALU.add))
            ch(dve.tensor_tensor(comb, comb, rmask, ALU.mult))
            ch(dve.tensor_reduce(rS[:], comb, AXX, ALU.add))
            ch(dve.scalar_tensor_tensor(rS[:], rZ[:], 1e-8, rS[:], ALU.mult, ALU.add))
            ch(dve.reciprocal(rS[:], rS[:]))
            dve.tensor_tensor(comb, comb, bc(rS[:].unsqueeze(2), [P, NT, E]), ALU.mult).then_inc(s["r_comb"], 1)
            dve.wait_ge(s["r_cT"], 1)
            for i in range(4):
                cols = slice(i * 512, (i + 1) * 512)
                ch(dve.tensor_copy(c_hi[:, cols], S[i][0:E, :]))
                ch(dve.tensor_tensor(b_tmp[0:E, :], S[i][0:E, :], c_hi[:, cols], ALU.subtract))
                ch(dve.tensor_copy(c_mid[:, cols], b_tmp[0:E, :]))
                last = dve.tensor_tensor(c_lo[:, cols], b_tmp[0:E, :], c_mid[:, cols], ALU.subtract)
                if i < 3:
                    ch(last)
            last.then_inc(s["r_split"], 1)

            def group_residual(g, event, ch, done):
                for k, bank in enumerate((Z, O)):
                    ys = [bank[:, t * D:(t + 1) * D] for t in range(2)]
                    ln_stats(ys, event + k, ch)
                    ch(ln_apply([tmp4[:, 2 * k + t, :] for t in range(2)], ys))
                rows = x_sb[:, bass.ds(4 * g, 4), :]
                dve.tensor_tensor(rows, rows, tmp4, ALU.add).then_inc(done, 1)

            NJ = NPAIR + NSH
            PERB = NPAIR + 4
            with dve.Fori(0, NG) as g:
                ch = Chain(dve, s["chb"], g * PERB)
                for j in range(NJ):
                    dve.wait_ge(s["f_sg"], g * NJ + j + 1)
                    sg = sgl[j % 2]
                    if j < NPAIR:
                        dve.wait_ge(s["f_cb"], g * NPAIR + j + 1)
                        ch(dve.tensor_tensor(sg, sg, TB[j % 2][:], ALU.mult))
                    dve.tensor_tensor(hh[j % 2], sg, S[2 + j % 2][:], ALU.mult).then_inc(s["f_h"], 1)
                dve.wait_ge(s["f_y"], g + 1)
                group_residual(g, 3 * NB + 2 * g, ch, s["f_post"])
                assert ch.n == PERB, ch.n

            ch = Chain(dve, s["chc0"])
            dve.wait_ge(s["w_c"], 160)
            dve.wait_ge(s["c_ones"], 1)
            dve.tensor_scalar(big15, big, 1.0 / CAP, None, ALU.mult)
            ch(dve.tensor_scalar(bfg15, bfg, 1.0 / CAP, None, ALU.mult))
            base = 3 * NB + 2 * NG

            def input_norm1(b, ch):
                rows = [tile(2 * b + t) for t in range(2)]
                ln_stats(rows, base + event(b), ch)
                ln_apply([xn[:, t, :] for t in range(2)], rows).then_inc(s["c_xn"], 1)

            def scans(b, ch):
                dve.wait_ge(s["c_ls"], b + 1)
                dve.tensor_scalar(gi, gi, CAP, None, ALU.mult)
                ch(dve.tensor_scalar(gls, gls, -1.0, None, ALU.mult))
                dve.tensor_tensor_scan(gF, ones1, gls, 0.0, ALU.mult, ALU.add)
                ch(dve.tensor_tensor_scan(gm, gls, gi, 0.0, ALU.add, ALU.max))

            def gate_rows(b):
                dve.tensor_tensor(gA, gF, gm, ALU.subtract)
                dve.tensor_tensor(gG, gi, gF, ALU.subtract).then_inc(s["c_gates"], 1)

            def gate_columns(b):
                dve.wait_ge(s["c_gT"], b + 1)
                dve.tensor_copy(gcol, T1[:, 0:16].rearrange("p (a b) -> p a b", b=H1)).then_inc(s["c_gcol"], 1)

            def key_value_copies(b):
                for g in range(2):
                    dve.wait_ge(s["c_q"], b * 2 + g + 1)
                    dve.tensor_copy(k1[:, g, :], S[g][:, T:2 * T]).then_inc(s["c_k"], 1)
                dve.wait_ge(s["c_vog"], b + 1)
                dve.tensor_copy(v1[:, :, :, 0:DV1].rearrange("p t h e -> p (t h) e"),
                                S[2][:].rearrange("p (h e) -> p h e", e=DV1)).then_inc(s["c_v"], 1)

            def output_gate(b, ch):
                dve.wait_ge(s["c_eo"], b + 1)
                ch(dve.tensor_scalar(eo, eo, 1.0, None, ALU.add))
                ch(dve.reciprocal(eo, eo))
                ch(dve.tensor_tensor(eo, eo, bc(gam.unsqueeze(1), [P, 2, D]), ALU.mult))

            def residual1(b, ch):
                dve.wait_ge(s["c_y"], b + 1)
                ys = [T0[:, t * D:(t + 1) * D] for t in range(2)]
                ln_stats(ys, base + post_event(b), ch)
                ch(ln_apply([tmp[:, t, :] for t in range(2)], ys))
                res = x_sb[:, bass.ds(2 * b, 2), :]
                ch(dve.tensor_tensor(res, res, tmp, ALU.add))

            def final_input_norm(b, ch):
                rows = [tile(2 * b + t) for t in range(2)]
                ln_stats(rows, base + post_event(b) + 1, ch)
                ln_apply([xn4[:, t, :] for t in range(2)], rows).then_inc(s["c_xn4"], 1)

            def weights1(b, h):
                dve.wait_ge(s["c_dec"], b * H1 + h + 1)
                dve.tensor_tensor(wt[h % 2], dec[h % 2], S[h % 2][:, 0:384], ALU.mult).then_inc(s["c_w"], 1)

            def mlstm(b, ch, first, last):
                for h in range(H1):
                    weights1(b, h)
                    if h == 1 and not first:
                        residual1(b - 1, ch)
                    if h == 2 and not first:
                        final_input_norm(b - 1, ch)
                    if h == 3:
                        output_gate(b, ch)
                    if h == 4 and not last:
                        input_norm1(b + 1, ch)
                if not last:
                    scans(b + 1, ch)
                    gate_rows(b + 1)
                dve.wait_ge(s["c_pv"], b + 1)
                both = [bank[:, 0:H1 * (DV1 + 1)].rearrange("p (h e) -> p h e", e=DV1 + 1) for bank in (Z, O)]
                for t in range(2):
                    last_op = dve.tensor_copy(den[:, t, :], both[t][:, :, DV1])
                ch(last_op)
                ch(dve.scalar_tensor_tensor(den, den, -1.0, den, ALU.mult, ALU.max))
                ch(dve.tensor_tensor(den, den, em, ALU.max))
                ch(dve.tensor_scalar(den, den, HEAD_EPS, None, ALU.add))
                ch(dve.reciprocal(den, den))
                hn4 = hn.rearrange("p t (h e) -> p t h e", e=DV1)
                for t in range(2):
                    last_op = dve.tensor_tensor(hn4[:, t], both[t][:, :, 0:DV1],
                                                bc(den[:, t, :].unsqueeze(2), [P, H1, DV1]), ALU.mult)
                ch(last_op)
                hnf = hn.rearrange("p t (h e) -> p (t h) e", e=DV1)
                hcf = hc.rearrange("p t (h e) -> p (t h) e", e=DV1)
                sqf = sq.rearrange("p t (h e) -> p (t h) e", e=DV1)
                ch(dve.tensor_reduce(mu, hnf, AXX, ALU.add))
                ch(dve.tensor_scalar(mu, mu, 1.0 / DV1, None, ALU.mult))
                ch(dve.tensor_tensor(hcf, hnf, bc(mu.unsqueeze(2), [P, 16, DV1]), ALU.subtract))
                ch(dve.tensor_tensor(sq, hc, hc, ALU.mult))
                dve.tensor_reduce(hv, sqf, AXX, ALU.add).then_inc(s["c_hv"], 1)
                ch(dve.tensor_tensor(hc, hc, eo, ALU.mult))
                if not last:
                    gate_columns(b + 1)
                dve.wait_ge(s["c_hr"], b + 1)
                dve.tensor_tensor(hnf, hcf, bc(hv.unsqueeze(2), [P, 16, DV1]), ALU.mult).then_inc(s["c_ho"], 1)
                if not last:
                    key_value_copies(b + 1)

            FIRST1, PER1 = 17, 21
            ch = Chain(dve, s["chc"])
            input_norm1(0, ch)
            scans(0, ch)
            gate_rows(0)
            gate_columns(0)
            key_value_copies(0)
            head = ch.n
            mlstm(0, ch, True, False)
            assert ch.n == head + FIRST1, ch.n
            with dve.Fori(1, NB - 1) as b:
                ch = Chain(dve, s["chc"], head + FIRST1 + (b - 1) * PER1)
                mlstm(b, ch, False, False)
                assert ch.n == PER1, ch.n
            ch = Chain(dve, s["chc"], head + FIRST1 + (NB - 2) * PER1)
            mlstm(NB - 1, ch, False, True)
            residual1(NB - 1, ch)
            final_input_norm(NB - 1, ch)

            base += 3 * NB
            PERD = 10
            dve.wait_ge(s["w_d"], 48)
            with dve.Fori(0, NG) as g:
                ch = Chain(dve, s["chd"], g * PERD)
                for q in range(2):
                    for j in range(4):
                        n = 4 * q + j
                        dve.wait_ge(s["d_sg"], g * NI + n + 1)
                        dve.tensor_tensor(hb[q][:, j, :], sgl[n % 2], S[2 + n % 2][:], ALU.mult).then_inc(s["d_h"], 1)
                    dve.wait_ge(s["d_abs"], g * 2 + q + 1)
                    dve.tensor_tensor(c01_23, ab[:, 0::2, :], ab[:, 1::2, :], ALU.is_ge)
                    dve.tensor_tensor(c02_13, ab[:, 0:2, :], ab[:, 2:4, :], ALU.is_ge)
                    dve.tensor_tensor(c03, ab[:, 0, :], ab[:, 3, :], ALU.is_ge)
                    ch(dve.tensor_tensor(c12, ab[:, 1, :], ab[:, 2, :], ALU.is_ge))
                    c01, c23, c02, c13 = c01_23[:, 0], c01_23[:, 1], c02_13[:, 0], c02_13[:, 1]
                    dve.tensor_tensor(half[:, 0], c01, c02, ALU.add)
                    dve.tensor_tensor(half[:, 1], c12, c13, ALU.add)
                    dve.tensor_tensor(half[:, 2], c23, c02, ALU.subtract)
                    ch(dve.tensor_tensor(half[:, 3], c03, c13, ALU.add))
                    dve.tensor_tensor(tally[:, 0], half[:, 0], c03, ALU.add)
                    dve.tensor_tensor(tally[:, 1], half[:, 1], c01, ALU.subtract)
                    dve.tensor_tensor(tally[:, 2], half[:, 2], c12, ALU.subtract)
                    ch(dve.tensor_tensor(tally[:, 3], half[:, 3], c23, ALU.add))
                    for j, (op, least) in enumerate(((ALU.is_ge, 2.0), (ALU.is_ge, 1.0), (ALU.is_ge, 0.0), (ALU.is_le, 1.0))):
                        last = dve.scalar_tensor_tensor(hs[q][:, j, :], tally[:, j], least, hb[q][:, j, :], op, ALU.mult)
                    last.then_inc(s["d_hs"], 1)
                dve.wait_ge(s["d_y"], g + 1)
                group_residual(g, base + 2 * g, ch, s["d_x"])
                assert ch.n == PERD, ch.n


def _laid_out(a):
    def kmajor(w):
        return np.ascontiguousarray(w.reshape(KC, P, -1).transpose(1, 0, 2))

    def heads(w, n, k):
        wt = np.zeros((D, n, 32), w.dtype)
        wt[:, :, :k] = w.T.reshape(D, n, k)
        return kmajor(wt.reshape(D, n * 32))

    def strips(w):
        return np.ascontiguousarray(w.reshape(-1, P, D).transpose(1, 0, 2))

    quads = lambda w: w.reshape(D, 2, P, 4).transpose(0, 1, 3, 2).reshape(D, 1024)
    return {
        "x": a["L0_attn_x"].reshape(NB * T, D),
        "wq0": heads(a["L0_attn_Wq"], H0, HD0), "wk0": heads(a["L0_attn_Wk"], H0, HD0),
        "wv0": kmajor(a["L0_attn_Wv"].T), "wo0": kmajor(a["L0_attn_Wo"].T), "wr": kmajor(a["L0_ffn_Wr"].T),
        "te1": kmajor(a["L0_ffn_te_W1"].T), "te_b1": a["L0_ffn_te_b1"].reshape(P, 1),
        "te2": np.ascontiguousarray(a["L0_ffn_te_W2"].T), "te_b2": a["L0_ffn_te_b2"],
        "aff": np.ascontiguousarray(a["L0_ffn_affinity"].T), "rbias": a["L0_ffn_router_bias"],
        "wg": kmajor(a["L0_ffn_Wg"].transpose(1, 0, 2).reshape(D, E * FE)),
        "wu": kmajor(a["L0_ffn_Wu"].transpose(1, 0, 2).reshape(D, E * FE)),
        "wd": strips(a["L0_ffn_Wd"].reshape(E * FE, D)),
        "sg": kmajor(a["L0_ffn_Sg"].transpose(1, 0, 2).reshape(D, 512)),
        "su": kmajor(a["L0_ffn_Su"].transpose(1, 0, 2).reshape(D, 512)),
        "sd": strips(a["L0_ffn_Sd"].reshape(512, D)),
        "wq1": heads(a["L1_attn_Wq"], H1, QK1), "wk1": heads(a["L1_attn_Wk"], H1, QK1),
        "wv1": kmajor(a["L1_attn_Wv"].T), "wog1": kmajor(a["L1_attn_Wog"].T), "wo1": kmajor(a["L1_attn_Wout"].T),
        "wig": kmajor(a["L1_attn_Wig"].T), "wfg": kmajor(a["L1_attn_Wfg"].T),
        "big": a["L1_attn_big"].reshape(H1, 1), "bfg": a["L1_attn_bfg"].reshape(H1, 1),
        "gam": a["L1_attn_gamma"].reshape(D),
        "gate": kmajor(quads(a["L1_ffn_w_gate"])), "up": kmajor(quads(a["L1_ffn_w_up"])),
        "down": np.ascontiguousarray(a["L1_ffn_w_down"].reshape(2, P, 4, D).transpose(1, 0, 2, 3).reshape(P, NI, D)),
    }


def kernel(**inputs):
    import concourse.bacc as bacc
    from concourse.bass_utils import run_bass_kernel_spmd

    nc = bacc.Bacc("TRN2", target_bir_lowering=False, num_devices=1)
    arrays, io = {}, {}
    for name, v in _laid_out({k: np.asarray(v) for k, v in inputs.items()}).items():
        arrays[f"in_{name}"] = np.ascontiguousarray(v)
        io[name] = nc.dram_tensor(f"in_{name}", v.shape, mybir.dt.from_np(v.dtype), kind="ExternalInput").ap()
    out = nc.dram_tensor("out", (NB * T, D), F32, kind="ExternalOutput").ap()
    build(nc, io, out)
    r = run_bass_kernel_spmd(nc, [arrays], core_ids=[0])
    return r.results[0]["out"].reshape(NB, T, D)
```

```python
from contextlib import ExitStack

import numpy as np
import concourse.bass as bass
from concourse import mybir

ALU = mybir.AluOpType
ACT = mybir.ActivationFunctionType
AXX = mybir.AxisListType.X
F32 = mybir.dt.float32
F32R = mybir.dt.float32r
BF16 = mybir.dt.bfloat16
U32 = mybir.dt.uint32

P = 128
NB, T, D = 8, 256, 256
NT = NB * T // P
KC = D // P
NPASS = 2
NU = 2
NUNIT = NPASS * NU
H0, HD0 = 16, 16
H1, QK1, DV1 = 8, 16, 32
E, FE, TOPK, ND = 64, 64, 4, 4
NPAIR = E // 2
NSH = 4
NJ = NPAIR + NSH
RING = 4
BW = 2 * KC * P + D
NI = 8
STEPS = NUNIT * NI
CAP = 15.0
NEG = -3.0e38
LN_EPS, HEAD_EPS = 1e-5, 1e-6


class Chain:

    def __init__(self, eng, sem, base=0):
        self.eng, self.sem, self.base, self.n = eng, sem, base, 0

    def __call__(self, ins):
        self.n += 1
        ins.then_inc(self.sem, 1)
        self.eng.wait_ge(self.sem, self.base + self.n)


def build(nc, io, out):
    ctx = ExitStack()
    with ctx:
        def sb(name, shape, dt=F32):
            return ctx.enter_context(nc.sbuf_tensor(name, shape, dt))

        def sem(name):
            return ctx.enter_context(nc.semaphore(name))

        S = [ctx.enter_context(nc.psum_tensor(f"S{i}", [P, 512], F32)) for i in range(4)]
        T0 = ctx.enter_context(nc.psum_tensor("T0", [P, 512], F32))
        T1 = ctx.enter_context(nc.psum_tensor("T1", [P, 512], F32))
        Z = ctx.enter_context(nc.psum_tensor("Z", [P, 512], F32))
        O = ctx.enter_context(nc.psum_tensor("O", [P, 512], F32))
        TB = [T0, T1]

        x_sb = sb("x_sb", [P, NT, D])
        xr = sb("xr", [P, 2, KC, NB * T], F32R)
        ident = sb("ident", [P, P])
        identb = sb("identb", [P, P], BF16)
        mask_ts = sb("mask_ts", [P, P], BF16)
        mask_st = sb("mask_st", [P, P], BF16)
        sel1 = sb("sel1", [2 * 32, H1, P], F32R)
        gA = sb("gA", [2 * 32, T], F32R)
        eye1 = sb("eye1", [2 * 32, H1])
        iota = sb("iota", [P, E])
        mhalf = sb("mhalf", [P, 16])
        mv = sb("mv", [P, 2, 2])
        st = sb("st", [P, 2, 6])
        veps = sb("veps", [P, 2])
        rstd = sb("rstd", [P, 2])

        def views(name, nbytes):
            arena = sb(name, [P, nbytes // 4])
            at = [0]

            def view(shape, dt=F32):
                n = int(np.prod(shape[1:]))
                words = n if dt in (F32, U32) else (n + 1) // 2
                v = arena[0:shape[0], at[0]:at[0] + words]
                at[0] += words
                assert at[0] * 4 <= nbytes, (name, at[0] * 4)
                if dt != F32:
                    v = v.bitcast(dt)
                if len(shape) == 3:
                    v = v.rearrange("p (a b) -> p a b", b=shape[2])
                if len(shape) == 4:
                    v = v.rearrange("p (a b c) -> p a b c", b=shape[2], c=shape[3])
                return v

            def rewind():
                at[0] = 0
            return view, rewind

        view, rewind = views("attn_w", 24 * 1024)
        wq0 = view([P, KC, 512])
        wk0 = view([P, KC, 512])
        wv0 = view([P, KC, D])
        wo0 = view([P, KC, D])
        rows_sb = [w[:, k, :] for w in (wq0, wk0) for k in range(2)]
        wr = view([P, KC, E])
        wq1 = view([P, KC, 256])
        wk1 = view([P, KC, 256])
        wv1 = view([P, KC, D])
        wog1 = view([P, KC, D])
        wo1 = view([P, KC, D])
        gam = view([P, D])
        wgates = view([P, KC, 32 + H1])
        big = view([H1, 1])
        bfg = view([H1, 1])
        big15 = view([H1, 1])
        bfg15 = view([H1, 1])

        raw = sb("raw", [P, RING, BW])
        parts = sb("parts", [P, NI * 2 * BW + 4096], F32R)
        wpart = parts[:, 0:4 * BW].rearrange("p (a k w) -> p a k w", a=2, k=2)
        selE = parts[:, 4 * BW:4 * BW + E * FE].rearrange("p (e f) -> p e f", e=E)
        hp = parts[:, NI * 2 * BW:NI * 2 * BW + 2048].rearrange("p (m k t) -> p m k t", m=2, k=2)
        cpart = parts[:, NI * 2 * BW + 2048:]
        words = [0]

        def in_parts(n):
            words[0] += 2 * KC * n
            return parts[:, words[0] - 2 * KC * n:words[0]].rearrange("p (k c w) -> p k c w", k=2, c=KC)

        wq_p, wk_p, wv_p, wo_p, xn_p, z_p = (in_parts(n) for n in (512, 512, D, D, T, T))
        qk_at = parts[:, NI * 2 * BW - 4096:]
        q0, k0 = (qk_at[:, i * 2048:(i + 1) * 2048].rearrange("p (k g t) -> p k g t", k=2, g=4) for i in range(2))
        q1, k1 = (qk_at[:, 4096 + i * 1024:4096 + (i + 1) * 1024].rearrange("p (k g t) -> p k g t", k=2, g=2)
                  for i in range(2))
        lastw = parts[:, 0:NI * 2 * BW].rearrange("p (n k w) -> p n k w", n=NI, k=2)
        hsp = parts[:, NI * 2 * BW:].rearrange("p (k j t) -> p k j t", k=2, j=4)

        te1 = sb("te1", [P, KC, P])
        te_b1 = sb("te_b1", [P, 1])
        te2 = sb("te2", [P, ND])
        te_b2 = sb("te_b2", [NB, ND])
        aff = sb("aff", [ND, E])
        rbias = sb("rbias", [P, E])
        lg_all = sb("lg_all", [P, NT, E])
        xmT = sb("xmT", [P, KC, NB])

        view, rewind = views("work", 42 * 1024)
        xn = view([P, 2, D])
        xnT = view([P, KC, T])
        tmp = view([P, 2, D])
        vpad = view([P, 2, H0, 2 * HD0])
        prob = [view([P, 2, 384]) for _ in range(3)]
        probT = [view([P, 2, 384]) for _ in range(2)]
        negmax = view([P, 2, H0])
        rowsum = view([P, 2, H0])
        xn2 = view([P, 2, D])
        xn2T = view([P, KC, T])
        rewind()
        sgl = [view([P, 512]) for _ in range(2)]
        hf = [view([P, 512]) for _ in range(2)]
        tmp2 = view([P, 2, D])
        tdx = view([ND, NB, P])
        eye2 = view([P, E])
        lg = view([P, NT, E])
        rsel = view([P, NT, E])
        comb = view([P, NT, E])
        rmask = view([P, NT, E])
        top = view([P, NT, 8])
        topi = view([P, NT, 8], U32)
        topf = view([P, NT, 8])
        rmx = view([P, NT])
        rZ = view([P, NT])
        rS = view([P, NT])
        dom = view([P, NB, E])
        rewind()
        view([P, 5, 512])
        hb = view([P, 4, 512])
        ab = view([P, 4, 512])
        c1 = view([P, 1, 512], BF16)
        c2 = view([P, 2, 512], BF16)
        c3 = view([P, 3, 512], BF16)
        tallies = [view([P, 512], BF16) for _ in range(2)]
        rewind()
        view([P, 2, D])
        view([P, KC, T])
        view([P, 2, D])
        v1 = view([P, 2, H1, DV1 + 1])
        eo = view([P, 2, D])
        gi = view([H1, T])
        gf = view([H1, T])
        gls = view([H1, T])
        gF = view([H1, T])
        gm = view([H1, T])
        gAf = view([H1, T])
        gG = view([H1, T])
        ones1 = view([H1, T])
        gcol = view([P, 2, H1])
        em = view([P, 2, H1])
        dec = [view([P, 384]) for _ in range(2)]
        wt = [view([P, 384]) for _ in range(2)]
        den = view([P, 2, H1])
        hn = view([P, 2, D])
        hc = view([P, 2, D])
        sq = view([P, 2, D])
        hT = view([P, KC, T])
        mu = view([P, 16])
        hv = view([P, 16])
        xn4 = view([P, 2, D])

        h1T = sb("h1T", [P, NB])
        tl = sb("tl", [NB, ND])
        tm = sb("tm", [NB, 1])
        td = sb("td", [NB, ND])

        names = """x_in w_a w_te w_raw0 w_raw1 w_raw2 w_raw3 w_ffn w_c pool_c const_done vones
            ln_mv ln_rs
            a_xn a_xt a_xtc a_qk a_q a_k a_vps a_v a_sc a_mx a_exp a_pt a_ptc a_pv a_z a_zt a_ztc a_y
            a_wh a_wl a_xtl a_ztl a_norm a_yr a_xn2 a_x2t a_x2c a_xall a_xlo a_xm a_lg a_lgc
            t_h1 t_h1c t_lg t_sub t_exp t_td t_tT t_tx t_dom r_sub r_exp r_comb r_cT r_split sel_done
            f_g f_u f_sg f_cb f_h f_hh f_hl f_wh f_wl f_blk f_rows f_added
            c_xn c_xt c_xtc c_qk c_q c_k c_vog c_v c_eo c_gt c_tanh c_ef c_ls c_gates c_gT c_gcol c_em
            c_sd c_dec c_w c_pv c_hv c_hr c_ho c_hoT c_hoTc c_y c_xn4 c_x4t c_xhi c_xall c_ones
            d_g d_u d_sg d_h d_abs d_cmp d_hs d_hh d_hl d_dn d_x o_out
            turn_v turn_p turn_t ch0 chc0 cha chr chb chc chd chp chpa chpb chpc chpd""".split()
        s = {n: sem(n) for n in names}

        block = ctx.enter_context(nc.Block())

        def hold(eng, name):
            eng.sem_inc(s[name], 1)

        def halves(bank):
            return bank[:].rearrange("p (a b) -> p a b", b=T)

        def bc(ap, shape):
            return ap.to_broadcast(shape)

        @block.sync
        def _(sp):
            sp.dma_start(x_sb[:], io["x"].rearrange("(n p) d -> p n d", p=P)).then_inc(s["x_in"], 16)
            for dst, name in ((wq0, "wq0"), (wk0, "wk0"), (wv0, "wv0"), (wo0, "wo0"), (wr, "wr")):
                sp.dma_start(dst, io[name]).then_inc(s["w_a"], 16)
            for dst, name in ((te1[:], "te1"), (te_b1[:], "te_b1"), (te2[:], "te2"), (aff[:], "aff")):
                sp.dma_start(dst, io[name]).then_inc(s["w_te"], 16)
            sp.dma_start(te_b2[:], io["te_b2"].partition_broadcast(NB)).then_inc(s["w_te"], 16)
            sp.dma_start(rbias[:], io["rbias"].partition_broadcast(P)).then_inc(s["w_te"], 16)
            for dst, name in ((wq1, "wq1"), (wk1, "wk1"), (wv1, "wv1"), (wog1, "wog1"), (wo1, "wo1"),
                              (wgates, "wgates"), (big, "big"), (bfg, "bfg")):
                sp.dma_start(dst, io[name]).then_inc(s["w_c"], 16)
            sp.dma_start(gam, io["gam"].partition_broadcast(P)).then_inc(s["w_c"], 16)

            def blocks(source, n, load):
                for j in range(n):
                    if not (isinstance(load, int) and load + j < RING):
                        sp.wait_ge(s["f_wl"], load + j - RING + 1)
                    sp.dma_start(raw[:, j % RING, :], source[j]).then_inc(s[f"w_raw{j % RING}"], 16)

            blocks(io["moe"], NJ, 0)
            blocks(io["moe"], NJ, NJ)
            for half in range(2):
                sp.wait_ge(s["f_wl"], NPASS * NJ + half * RING)
                sp.dma_start(raw[:], io["ffn"][half * RING:(half + 1) * RING].rearrange("n p w -> p n w")
                             ).then_inc(s["w_ffn"], 16)
            for u in range(NUNIT):
                sp.wait_ge(s["d_x"], u + 1)
                sp.dma_start(out[u * 512:(u + 1) * 512, :].rearrange("(n p) d -> p n d", p=P),
                             x_sb[:, 4 * u:4 * u + 4, :]).then_inc(s["o_out"], 16)
            sp.wait_ge(s["o_out"], 16 * NUNIT)

        @block.gpsimd
        def _(pool):
            ch = Chain(pool, s["pool_c"])
            pool.memset(ident[:], 0.0)
            pool.memset(identb[:], 0.0)
            pool.memset(mask_ts[:], 0.0)
            pool.memset(mask_st[:], 0.0)
            pool.memset(eye1[:], 0.0)
            pool.memset(mhalf[:], -0.5)
            pool.memset(vpad, 0.0)
            ch(pool.iota(iota[:], [[1, E]], base=0, channel_multiplier=0, allow_small_or_imprecise_dtypes=True))
            for m in (ident, identb):
                pool.affine_select(out=m[:], in_=m[:], compare_op=ALU.not_equal, fill=1.0, base=0,
                                   pattern=[[-1, P]], channel_multiplier=1)
            pool.affine_select(out=mask_ts[:], in_=mask_ts[:], compare_op=ALU.is_ge, fill=NEG, base=0,
                               pattern=[[-1, P]], channel_multiplier=1)
            pool.affine_select(out=mask_st[:], in_=mask_st[:], compare_op=ALU.is_ge, fill=NEG, base=0,
                               pattern=[[1, P]], channel_multiplier=-1)
            ch(pool.affine_select(out=eye1[:], in_=eye1[:], compare_op=ALU.not_equal, fill=1.0, base=0,
                                  pattern=[[-1, H1]], channel_multiplier=1))
            pool.affine_select(out=eye1[:], in_=eye1[:], compare_op=ALU.not_equal, fill=1.0, base=-32,
                               pattern=[[-1, H1]], channel_multiplier=1).then_inc(s["const_done"], 1)

            def ln_event(event, cp):
                pool.wait_ge(s["ln_mv"], event + 1)
                hold(pool, "turn_p")
                cp(pool.tensor_scalar(veps[:], mv[:, :, 1], LN_EPS, None, ALU.add))
                pool.tensor_tensor(rstd[:], veps[:], mhalf[:, 0:2], ALU.pow).then_inc(s["ln_rs"], 1)

            with pool.Fori(0, 3 * NB) as e:
                ln_event(e, Chain(pool, s["chpa"], e))
            cs = Chain(pool, s["chp"])
            pool.wait_ge(s["a_lgc"], NB)
            cs(pool.memset(eye2, 0.0))
            cs(pool.affine_select(out=eye2, in_=eye2, compare_op=ALU.not_equal, fill=1.0,
                                  base=0, pattern=[[-1, E]], channel_multiplier=1))
            pool.affine_select(out=eye2, in_=eye2, compare_op=ALU.not_equal, fill=1.0,
                               base=-E, pattern=[[-1, E]], channel_multiplier=1).then_inc(s["sel_done"], 1)
            with pool.Fori(3 * NB, 3 * NB + 4 * (NPASS - 1)) as e:
                ln_event(e, Chain(pool, s["chpb"], e - 3 * NB))
            pool.wait_ge(s["f_hl"], NPASS * NU * NJ)
            pool.memset(v1, 1.0)
            pool.memset(ones1, 1.0).then_inc(s["c_ones"], 1)
            base = 3 * NB + NT // 2

            def head_event(b, cp):
                pool.wait_ge(s["c_hv"], b + 1)
                hold(pool, "turn_p")
                cp(pool.tensor_scalar(hv, hv, 1.0 / DV1, HEAD_EPS, ALU.mult, ALU.add))
                pool.tensor_tensor(hv, hv, mhalf[:], ALU.pow).then_inc(s["c_hr"], 1)

            cp = Chain(pool, s["chpc"])
            for k in range(6):
                ln_event(base - 4 + k, cp)
            head_event(0, cp)
            with pool.Fori(1, NB - 1) as b:
                cp = Chain(pool, s["chpc"], b * 4 + 3)
                for k in range(3):
                    ln_event(base + b * 3 - 1 + k, cp)
                head_event(b, cp)
            cp = Chain(pool, s["chpc"], 4 * NB - 1)
            for k in range(2):
                ln_event(base + 3 * NB - 4 + k, cp)
            head_event(NB - 1, cp)
            for k in range(2):
                ln_event(base + 3 * NB - 2 + k, cp)
            base += 3 * NB
            cp = Chain(pool, s["chpd"])
            for i in range(STEPS + 4):
                u, n = divmod(i, NI)
                if i >= 4:
                    k = i - 4
                    pool.wait_ge(s["d_hh"], k + 1)
                    pool.tensor_tensor(hsp[:, 1, k % 4, :], hb[:, k % 4, :], hsp[:, 0, k % 4, :],
                                       ALU.subtract).then_inc(s["d_hl"], 1)
                if i < STEPS and u and n in (5, 6):
                    ln_event(base + 2 * (u - 1) + n - 5, cp)
            for k in range(2):
                ln_event(base + 2 * (NUNIT - 1) + k, cp)

        @block.scalar
        def _(act):
            def input_copy(b):
                act.wait_ge(s["a_xt"], b + 1)
                act.activation(xn_p[:, 0], halves(O), ACT.Copy).then_inc(s["a_xtc"], 1)

            def query_copies(b, groups):
                for g in groups:
                    act.wait_ge(s["a_qk"], b * 4 + g + 1)
                    act.activation(q0[:, 0, g, :], S[g][:, 0:T], ACT.Copy, scale=0.25)
                    act.activation(k0[:, 0, g, :], S[g][:, T:2 * T], ACT.Copy).then_inc(s["a_q"], 1)

            def exponentials(b, u):
                act.wait_ge(s["a_mx"], b * 8 + u + 1)
                if u >= 3:
                    act.wait_ge(s["a_pt"], b * 8 + u - 2)
                for r in range(2):
                    h = 2 * u + r
                    bank = S[2 * (u % 2) + r]
                    act.activation(prob[u % 3][:, r, 0:128], bank[:, 0:128], ACT.Exp, bias=negmax[:, 0, h:h + 1],
                                   accum_out=rowsum[:, 0, h:h + 1])
                    last = act.activation(prob[u % 3][:, r, 128:384], bank[:, 128:384], ACT.Exp,
                                          bias=negmax[:, 1, h:h + 1], accum_out=rowsum[:, 1, h:h + 1])
                last.then_inc(s["a_exp"], 1)

            def next_input_copies(b):
                act.wait_ge(s["a_x2t"], b + 1)
                act.activation(xn2T, halves(O), ACT.Copy).then_inc(s["a_x2c"], 1)
                act.activation(xr[:, 0, :, bass.ds(b * T, T)], halves(O), ACT.Copy).then_inc(s["a_xall"], 1)

            def attention(b, first, last):
                for u in range(8):
                    exponentials(b, u)
                    if u == 4 and not first:
                        next_input_copies(b - 1)
                    if u == 6 and not last:
                        input_copy(b + 1)
                if not last:
                    query_copies(b + 1, range(4))
                act.wait_ge(s["a_pv"], b * 8 + 8)
                act.activation(z_p[:, 0], halves(Z), ACT.Copy).then_inc(s["a_ztc"], 1)

            act.wait_ge(s["w_a"], 80)
            for w, wp in ((wq0, wq_p), (wk0, wk_p), (wv0, wv_p), (wo0, wo_p)):
                act.activation(wp[:, 0], w, ACT.Copy).then_inc(s["a_wh"], 1)
            input_copy(0)
            query_copies(0, range(4))
            attention(0, True, False)
            with act.Fori(1, NB - 1) as b:
                attention(b, False, False)
            attention(NB - 1, False, True)
            next_input_copies(NB - 1)
            act.wait_ge(s["t_h1"], 1)
            act.wait_ge(s["w_te"], 96)
            act.activation(h1T[:], S[3][:, 0:NB], ACT.Gelu, bias=te_b1[:, 0:1], scale=1.0 / T).then_inc(s["t_h1c"], 1)
            def high_weights(load, j):
                act.wait_ge(s[f"w_raw{j % RING}"], 16 * ((load + j) // RING + 1))
                if load + j >= 2:
                    act.wait_ge(s["f_blk"], load + j - 1)
                act.activation(wpart[:, j % 2, 0, :], raw[:, j % RING, :], ACT.Copy).then_inc(s["f_wh"], 1)

            def experts(p):
                for n in range(NU * NJ):
                    j, m = n // NU, n % NU
                    act.wait_ge(s["f_g"], p * NU * NJ + n + 1)
                    if p * NU * NJ + n >= 2:
                        act.wait_ge(s["f_h"], p * NU * NJ + n - 1)
                    act.activation(sgl[m], S[m][:], ACT.Silu).then_inc(s["f_sg"], 1)
                    act.wait_ge(s["f_h"], p * NU * NJ + n + 1)
                    act.activation(hp[:, m, 0, :], hf[m], ACT.Copy).then_inc(s["f_hh"], 1)
                    if m == 0 and p * NJ + j + 1 < NPASS * NJ:
                        high_weights(0, p * NJ + j + 1)
                    if p == 0 and n == 3:
                        act.wait_ge(s["r_sub"], 1)
                        act.activation(comb, lg, ACT.Exp).then_inc(s["r_exp"], 1)

            high_weights(0, 0)
            act.wait_ge(s["t_sub"], 1)
            act.activation(td[:], tl[:], ACT.Exp).then_inc(s["t_exp"], 1)
            for p in range(NPASS):
                experts(p)
                act.wait_ge(s["f_blk"], (p + 1) * NJ)
                for k, bank in enumerate((T0, T1, Z, O)):
                    if p:
                        act.wait_ge(s["f_added"], (p - 1) * 4 + k + 1)
                    act.activation(rows_sb[k], bank[:], ACT.Copy).then_inc(s["f_rows"], 1)
            def input_copy1(b):
                act.wait_ge(s["c_xt"], b + 1)
                act.activation(xnT, halves(T0), ACT.Copy).then_inc(s["c_xtc"], 1)

            def gate_functions(b):
                act.wait_ge(s["c_gt"], b + 1)
                act.activation(gi, T1[0:H1, 0:T], ACT.Tanh, bias=big15, scale=1.0 / CAP)
                act.activation(gf, T1[32:32 + H1, 0:T], ACT.Tanh, bias=bfg15, scale=1.0 / CAP).then_inc(s["c_tanh"], 1)
                act.wait_ge(s["c_tanh"], b + 1)
                act.activation(gf, gf, ACT.Exp, scale=-CAP).then_inc(s["c_ef"], 1)
                act.wait_ge(s["c_ef"], b + 1)
                act.activation(gls, gf, ACT.Ln, bias=1.0).then_inc(s["c_ls"], 1)

            def query_copies1(b):
                for g in range(2):
                    act.wait_ge(s["c_qk"], b * 2 + g + 1)
                    act.activation(q1[:, 0, g, :], S[g][:, 0:T], ACT.Copy, scale=0.25)
                    act.activation(k1[:, 0, g, :], S[g][:, T:2 * T], ACT.Copy).then_inc(s["c_q"], 1)

            def output_gate(b):
                act.wait_ge(s["c_vog"], b + 1)
                act.activation(eo, halves(S[3]), ACT.Exp, scale=-1.0).then_inc(s["c_eo"], 1)
                act.wait_ge(s["c_gcol"], b + 1)
                act.activation(em, T1[:, 16:32].rearrange("p (a b) -> p a b", b=H1), ACT.Exp,
                               scale=-1.0).then_inc(s["c_em"], 1)

            def final_input_copy(b):
                act.wait_ge(s["c_x4t"], b + 1)
                act.activation(xr[:, 0, :, bass.ds(b * T, T)], halves(T0), ACT.Copy).then_inc(s["c_xhi"], 1)

            def last_high_weights(n):
                act.wait_ge(s["w_ffn"], 16 * (n // RING + 1))
                act.activation(lastw[:, n, 0, :], raw[:, n % RING, :], ACT.Copy).then_inc(s["f_wh"], 1)

            def mlstm(b, first, last):
                for h in range(H1):
                    if (first or last) and h % 2 == 0:
                        last_high_weights(h // 2 + (RING if last else 0))
                    act.wait_ge(s["c_sd"], b * H1 + h + 1)
                    if h >= 2:
                        act.wait_ge(s["c_w"], b * H1 + h - 1)
                    act.activation(dec[h % 2][:, 0:256], S[2 + h % 2][:, 0:256], ACT.Exp, bias=gcol[:, 0, h:h + 1])
                    act.activation(dec[h % 2][:, 256:384], S[2 + h % 2][:, 256:384], ACT.Exp,
                                   bias=gcol[:, 1, h:h + 1]).then_inc(s["c_dec"], 1)
                    if h == 4 and not first:
                        final_input_copy(b - 1)
                    if h == 6 and not last:
                        input_copy1(b + 1)
                if not last:
                    gate_functions(b + 1)
                    query_copies1(b + 1)
                act.wait_ge(s["c_hoT"], b + 1)
                act.activation(hT, halves(T0), ACT.Copy).then_inc(s["c_hoTc"], 1)
                if not last:
                    output_gate(b + 1)

            input_copy1(0)
            gate_functions(0)
            query_copies1(0)
            output_gate(0)
            mlstm(0, True, False)
            with act.Fori(1, NB - 1) as b:
                mlstm(b, False, False)
            mlstm(NB - 1, False, True)
            final_input_copy(NB - 1)
            def silu(i):
                act.wait_ge(s["d_g"], i + 1)
                if i >= 2:
                    act.wait_ge(s["d_h"], i - 1)
                act.activation(sgl[i % 2], S[i % 2][:], ACT.Silu).then_inc(s["d_sg"], 1)

            def magnitudes(i):
                act.wait_ge(s["d_h"], i + 1)
                if i % 4 == 0 and i:
                    act.wait_ge(s["d_cmp"], i // 4)
                act.activation(ab[:, i % 4, :], hb[:, i % 4, :], ACT.Abs).then_inc(s["d_abs"], 1)

            def high_hidden(i):
                act.wait_ge(s["d_hs"], i + 1)
                if i >= 4:
                    act.wait_ge(s["d_dn"], i - 3)
                act.activation(hsp[:, 0, i % 4, :], hb[:, i % 4, :], ACT.Copy).then_inc(s["d_hh"], 1)

            silu(0)
            for i in range(STEPS + 3):
                if i < STEPS:
                    magnitudes(i)
                if i >= 3 and i % 4 != 3:
                    high_hidden(i - 3)
                if i + 1 < STEPS:
                    silu(i + 1)
                if i >= 3 and i % 4 == 3:
                    high_hidden(i - 3)

        @block.tensor
        def _(pe):
            def transposes(src, bank):
                for t in range(2):
                    for c in range(KC):
                        last = pe.transpose(bank[:, c * T + t * P:c * T + (t + 1) * P], src[:, t, c * P:(c + 1) * P],
                                            ident[:])
                return last

            def project(dst, lhs, rhs, t):
                for c in range(KC):
                    last = pe.matmul(dst, lhs[:, c, t * P:(t + 1) * P], rhs[:, c, :], start=(c == 0), stop=(c == KC - 1))
                return last

            pe.wait_ge(s["const_done"], 1)
            pe.wait_ge(s["w_a"], 80)
            for n in ("a_xall", "c_xall"):
                pe.sem_inc(s[n], 1)
            def input_transposes(b):
                pe.wait_ge(s["a_xn"], b + 1)
                transposes(xn, O).then_inc(s["a_xt"], 1)

            def three(dst, a, b, start, stop):
                pe.matmul(dst, a(0), b(0), start=start, stop=False, skip_group_check=True)
                pe.matmul(dst, a(0), b(1), start=False, stop=False, skip_group_check=True)
                return pe.matmul(dst, a(1), b(0), start=False, stop=stop, skip_group_check=True)

            def project_parts(dst, lhs, rhs, t):
                for c in range(KC):
                    last = three(dst, lambda k: lhs[:, k, c, t * P:(t + 1) * P], lambda k: rhs[:, k, c, :],
                                 c == 0, c == KC - 1)
                return last

            def project_qk(b, g):
                if g == 0:
                    pe.wait_ge(s["a_xtl"], b + 1)
                for w, o in ((wq_p, 0), (wk_p, T)):
                    for c in range(KC):
                        last = three(S[g][:, o:o + T], lambda k: w[:, k, c, g * P:(g + 1) * P],
                                     lambda k: xn_p[:, k, c, :], c == 0, c == KC - 1)
                last.then_inc(s["a_qk"], 1)

            def project_v(b):
                for t in range(2):
                    last = project_parts(O[:, t * D:(t + 1) * D], xn_p, wv_p, t)
                last.then_inc(s["a_vps"], 1)

            def scores(b, u):
                if u >= 2:
                    pe.wait_ge(s["a_exp"], b * 8 + u - 1)
                for r in range(2):
                    h = 2 * u + r
                    g, p0 = h // 4, 32 * (h % 4)
                    bank = S[2 * (u % 2) + r]
                    q, k = q0[p0:p0 + HD0, :, g, :], k0[p0:p0 + HD0, :, g, :]
                    three(bank[:, 0:128], lambda i: q[:, i, 0:128], lambda i: k[:, i, 0:128], True, True)
                    pe.matmul(bank[:, 0:128], identb[:], mask_ts[:], start=False, stop=True, skip_group_check=True)
                    three(bank[:, 128:384], lambda i: q[:, i, 128:256], lambda i: k[:, i, :], True, True)
                    last = pe.matmul(bank[:, 256:384], identb[:], mask_ts[:], start=False, stop=True,
                                     skip_group_check=True)
                last.then_inc(s["a_sc"], 1)

            def prob_transposes(b, u, first):
                pe.wait_ge(s["a_norm"], b * 8 + u + 1)
                if u >= 1:
                    pe.wait_ge(s["a_ptc"], b * 8 + u)
                elif not first:
                    pe.wait_ge(s["a_yr"], b)
                for r in range(2):
                    for c in range(3):
                        last = pe.transpose(TB[r][:, c * P:(c + 1) * P], prob[u % 3][:, r, c * P:(c + 1) * P],
                                            ident[:])
                last.then_inc(s["a_pt"], 1)

            def values(b, u):
                pe.wait_ge(s["a_ptc"], b * 8 + u + 1)
                p0, o = 32 * (u % 4), (u // 4) * T
                for r in range(2):
                    h, pt = 2 * u + r, probT[u % 2][:, r, :]
                    pe.matmul(Z[p0:p0 + 32, o:o + T], vpad[:, 0, h, :], pt[:, 0:256], start=(r == 0), stop=True,
                              skip_group_check=True)
                    last = pe.matmul(Z[p0:p0 + 32, o + 128:o + T], vpad[:, 1, h, :], pt[:, 256:384], start=False,
                                     stop=True, skip_group_check=True)
                last.then_inc(s["a_pv"], 1)

            def next_input_transposes(b):
                pe.wait_ge(s["a_xn2"], b + 1)
                transposes(xn2, O).then_inc(s["a_x2t"], 1)

            def router_logits(b):
                pe.wait_ge(s["a_xall"], b + 2)
                for t in range(2):
                    last = project(O[:, t * E:(t + 1) * E], xn2T, wr, t)
                last.then_inc(s["a_lg"], 1)

            def attention(b, first, last):
                for u in range(11):
                    if u < 8:
                        if u < 2:
                            pe.wait_ge(s["a_k"], b * 4 + 2 * u + 2)
                        scores(b, u)
                    if u == 0:
                        pe.wait_ge(s["a_v"], b + 1)
                    if 2 <= u <= 9:
                        prob_transposes(b, u - 2, first)
                    if u == 4 and not first:
                        next_input_transposes(b - 1)
                    if u == 6 and not first:
                        router_logits(b - 1)
                    if u == 7 and not last:
                        if not first:
                            pe.wait_ge(s["a_lgc"], b)
                        input_transposes(b + 1)
                    if u >= 3:
                        values(b, u - 3)
                    if u == 8 and not last:
                        pe.wait_ge(s["a_exp"], b * 8 + 7)
                        project_qk(b + 1, 0)
                        project_qk(b + 1, 1)
                    if u == 9 and not last:
                        pe.wait_ge(s["a_exp"], b * 8 + 8)
                        project_qk(b + 1, 2)
                        project_qk(b + 1, 3)
                if not last:
                    project_v(b + 1)
                pe.wait_ge(s["a_ztl"], b + 1)
                for t in range(2):
                    last_mm = project_parts(T1[:, t * D:(t + 1) * D], z_p, wo_p, t)
                last_mm.then_inc(s["a_y"], 1)

            input_transposes(0)
            pe.wait_ge(s["a_wl"], 4)
            for g in range(4):
                project_qk(0, g)
            project_v(0)
            attention(0, True, False)
            with pe.Fori(1, NB - 1) as b:
                attention(b, False, False)
            attention(NB - 1, False, True)
            next_input_transposes(NB - 1)
            router_logits(NB - 1)

            pe.wait_ge(s["a_xm"], NB)
            pe.wait_ge(s["w_te"], 96)
            for c in range(KC):
                last = pe.matmul(S[3][:, 0:NB], te1[:, c, :], xmT[:, c, :], start=(c == 0), stop=(c == KC - 1))
            last.then_inc(s["t_h1"], 1)

            def task_domains():
                pe.wait_ge(s["t_h1c"], 1)
                pe.matmul(S[1][0:NB, 0:ND], h1T[:], te2[:], start=True, stop=True).then_inc(s["t_lg"], 1)
                pe.wait_ge(s["t_td"], 1)
                pe.transpose(S[1][0:ND, 0:NB], td[:], ident[0:NB, 0:NB]).then_inc(s["t_tT"], 1)
                pe.wait_ge(s["t_tx"], 1)
                for i in range(NB):
                    last = pe.matmul(S[3][:, i * E:(i + 1) * E], tdx[:, i, :], aff[:], start=True, stop=True)
                last.then_inc(s["t_dom"], 1)

            def combine_transposes():
                pe.wait_ge(s["r_comb"], 1)
                pe.wait_ge(s["f_sg"], NU * NSH)
                pe.wait_ge(s["f_h"], NU * NSH)
                for i in range(NT):
                    last = pe.transpose(S[i // 4][0:E, (i % 4) * P:(i % 4 + 1) * P], comb[:, i, :], ident[:])
                last.then_inc(s["r_cT"], 1)

            pe.wait_ge(s["a_xall"], NB + 1)
            pe.wait_ge(s["a_xlo"], NB)
            ROWS = (T0, T1, Z, O)

            def gate_up(bank, which, w, tok):
                for c in range(KC):
                    o = (which * KC + c) * P
                    last = three(bank[:], lambda k: w[:, k, o:o + P], lambda k: xr[:, k, c, tok],
                                 c == 0, c == KC - 1)
                return last

            def rows_down(m, h, w, first, final):
                for t in range(4):
                    bank, o = ROWS[2 * m + t // 2], (t % 2) * D
                    last = three(bank[:, o:o + D], lambda k: h(k)[:, t * P:(t + 1) * P], w,
                                 first and t % 2 == 0, final)
                return last

            for p in range(NPASS):
                def unit(n):
                    j, m = n // NU, n % NU
                    i = p * NU * NJ + n
                    if m == 0:
                        pe.wait_ge(s["f_wh"], p * NJ + j + 1)
                        pe.wait_ge(s["f_wl"], p * NJ + j + 1)
                    if i >= 2:
                        pe.wait_ge(s["f_sg"], i - 1)
                    tok = slice(p * 1024 + m * 512, p * 1024 + (m + 1) * 512)
                    if i == NU * NSH:
                        pe.wait_ge(s["r_split"], 1)
                    gate_up(S[m], 0, wpart[:, j % 2], tok).then_inc(s["f_g"], 1)
                    if i:
                        pe.wait_ge(s["f_h"], i)
                    if j >= NSH:
                        e = 2 * (j - NSH)
                        pe.matmul(S[3][:], selE[:, e:e + 2, :].rearrange("p e f -> p (e f)"), cpart[:, tok],
                                  start=True, stop=True).then_inc(s["f_cb"], 1)
                    gate_up(S[2], 1, wpart[:, j % 2], tok).then_inc(s["f_u"], 1)

                def down_unit(n):
                    j, m = n // NU, n % NU
                    pe.wait_ge(s["f_hl"], p * NU * NJ + n + 1)
                    if p and j == 0:
                        pe.wait_ge(s["f_rows"], (p - 1) * 4 + 2 * m + 2)
                    last = rows_down(m, lambda k: hp[:, m, k, :], lambda k: wpart[:, j % 2, k, 2 * KC * P:BW],
                                     j == 0, j == NJ - 1)
                    if m == NU - 1:
                        last.then_inc(s["f_blk"], 1)

                for n in range(NU * NJ):
                    if p == 0 and n == NU * NSH:
                        combine_transposes()
                        down_unit(n - 1)
                        unit(n)
                        continue
                    unit(n)
                    if p == 0 and n == 0:
                        task_domains()
                    if n:
                        down_unit(n - 1)
                down_unit(NU * NJ - 1)

            pe.wait_ge(s["w_c"], 144)
            pe.wait_ge(s["f_rows"], 4 * NPASS)
            def input_transposes1(b):
                pe.wait_ge(s["c_xn"], b + 1)
                transposes(xn, T0).then_inc(s["c_xt"], 1)

            def gates(b):
                pe.wait_ge(s["c_xtc"], b + 1)
                for c in range(KC):
                    last = pe.matmul(T1[0:32 + H1, 0:T], wgates[:, c, :], xnT[:, c, :], start=(c == 0),
                                     stop=(c == KC - 1))
                last.then_inc(s["c_gt"], 1)

            def projections(b):
                for g in range(2):
                    for w, o in ((wq1, 0), (wk1, T)):
                        for c in range(KC):
                            last = pe.matmul(S[g][:, o:o + T], w[:, c, g * P:(g + 1) * P], xnT[:, c, :],
                                             start=(c == 0), stop=(c == KC - 1))
                    last.then_inc(s["c_qk"], 1)
                for t in range(2):
                    project(S[2][:, t * D:(t + 1) * D], xnT, wv1, t)
                    last = project(S[3][:, t * D:(t + 1) * D], xnT, wog1, t)
                last.then_inc(s["c_vog"], 1)

            def gate_columns(b):
                pe.wait_ge(s["c_gates"], b + 1)
                hold(pe, "turn_t")
                for i, src in enumerate((gG, gm)):
                    for t in range(2):
                        o = (2 * i + t) * H1
                        last = pe.transpose(T1[:, o:o + H1], src[:, t * P:(t + 1) * P], ident[0:H1, 0:H1])
                last.then_inc(s["c_gT"], 1)

            def scores1(b, h):
                if h >= 2:
                    pe.wait_ge(s["c_w"], b * H1 + h - 1)
                g, p0 = h // 4, 32 * (h % 4)
                q, k = q1[p0:p0 + QK1, :, g, :], k1[p0:p0 + QK1, :, g, :]
                sc, dc = S[h % 2], S[2 + h % 2]
                three(sc[:, 0:256], lambda i: k[:, i, 0:128], lambda i: q[:, i, :], True, True)
                three(sc[:, 256:384], lambda i: k[:, i, 128:256], lambda i: q[:, i, 128:256], True, True)
                for o, t0 in ((0, 0), (256, 128)):
                    pe.matmul(dc[:, o:o + 256 - t0], sel1[:, h, :], gA[:, t0:256], start=True, stop=True)
                    last = pe.matmul(dc[:, o:o + 128], identb[:], mask_st[:], start=False, stop=True,
                                     skip_group_check=True)
                last.then_inc(s["c_sd"], 1)

            def values1(b, h):
                pe.wait_ge(s["c_w"], b * H1 + h + 1)
                o = h * (DV1 + 1)
                w = wt[h % 2]
                pe.matmul(Z[:, o:o + 33], w[:, 0:128], v1[:, 0, h, :], start=True, stop=True)
                pe.matmul(O[:, o:o + 33], w[:, 128:256], v1[:, 0, h, :], start=True, stop=False)
                return pe.matmul(O[:, o:o + 33], w[:, 256:384], v1[:, 1, h, :], start=False, stop=True)

            def final_input_transposes(b):
                pe.wait_ge(s["c_xn4"], b + 1)
                transposes(xn4, T0).then_inc(s["c_x4t"], 1)

            def hidden(i):
                u, n = divmod(i, NI)
                if i >= 2:
                    pe.wait_ge(s["d_sg"], i - 1)
                tok = slice(u * 512, (u + 1) * 512)
                gate_up(S[i % 2], 0, lastw[:, n], tok).then_inc(s["d_g"], 1)
                if i >= 2:
                    pe.wait_ge(s["d_h"], i - 1)
                gate_up(S[2 + i % 2], 1, lastw[:, n], tok).then_inc(s["d_u"], 1)

            def mlstm(b, first, last):
                pe.wait_ge(s["c_q"], b * 2 + 2)
                pe.wait_ge(s["c_k"], b * 2 + 2)
                pe.wait_ge(s["c_v"], b + 1)
                pe.wait_ge(s["c_em"], b + 1)
                for h in range(H1 + 1):
                    if h < H1:
                        scores1(b, h)
                    if h == 4 and not first:
                        final_input_transposes(b - 1)
                    if h == 6 and not last:
                        if not first:
                            pe.wait_ge(s["c_xall"], b + 1)
                        input_transposes1(b + 1)
                    if h == 8 and not last:
                        gates(b + 1)
                    if h:
                        last_mm = values1(b, h - 1)
                last_mm.then_inc(s["c_pv"], 1)
                if not last:
                    projections(b + 1)
                    gate_columns(b + 1)
                else:
                    pe.wait_ge(s["f_wl"], NPASS * NJ + NI)
                    pe.wait_ge(s["c_xall"], 3)
                    hidden(0)
                    hidden(1)
                pe.wait_ge(s["c_ho"], b + 1)
                transposes(hn, T0).then_inc(s["c_hoT"], 1)
                pe.wait_ge(s["c_hoTc"], b + 1)
                for t in range(2):
                    last_mm = project(T0[:, t * D:(t + 1) * D], hT, wo1, t)
                last_mm.then_inc(s["c_y"], 1)

            input_transposes1(0)
            gates(0)
            projections(0)
            gate_columns(0)
            mlstm(0, True, False)
            with pe.Fori(1, NB - 1) as b:
                mlstm(b, False, False)
            mlstm(NB - 1, False, True)
            final_input_transposes(NB - 1)

            pe.wait_ge(s["c_xall"], NB + 1)

            def down2(i):
                u, n = divmod(i, NI)
                pe.wait_ge(s["d_hl"], i + 1)
                if n == 0 and u >= 2:
                    pe.wait_ge(s["d_x"], u - 1)
                rows_down(u % 2, lambda k: hsp[:, k, n % 4, :], lambda k: lastw[:, n, k, 2 * KC * P:BW],
                          n == 0, n == NI - 1).then_inc(s["d_dn"], 1)

            for i in range(STEPS + 5):
                if 2 <= i < STEPS:
                    hidden(i)
                if i >= 5:
                    down2(i - 5)

        @block.vector
        def _(dve):
            def ln_stats(srcs, event, ch):
                ln_moments(srcs, ch)
                dve.wait_ge(s["ln_rs"], event + 1)

            def ln_moments(srcs, ch):
                hold(dve, "turn_v")
                for t, src in enumerate(srcs):
                    last = dve.bn_stats(st[:, t, :], src)
                ch(last)
                hold(dve, "turn_v")
                for t in range(2):
                    last = dve.bn_aggr(mv[:, t, :], st[:, t, :])
                last.then_inc(s["ln_mv"], 1)

            def ln_apply(dsts, srcs):
                for t, (dst, src) in enumerate(zip(dsts, srcs)):
                    last = dve.tensor_scalar(dst, src, mv[:, t, 0:1], rstd[:, t:t + 1], ALU.subtract, ALU.mult)
                return last

            def tile(i):
                return x_sb[:, bass.ds(i, 1), :].squeeze(1)

            dve.wait_ge(s["x_in"], 16)
            def input_stats(b, ch):
                ln_moments([tile(2 * b + t) for t in range(2)], ch)

            def input_norm(b):
                dve.wait_ge(s["ln_rs"], event(b) + 1)
                ln_apply([xn[:, t, :] for t in range(2)], [tile(2 * b + t) for t in range(2)]).then_inc(s["a_xn"], 1)

            def input_low(b):
                dve.wait_ge(s["a_xtc"], b + 1)
                dve.tensor_tensor(xn_p[:, 1], halves(O), xn_p[:, 0], ALU.subtract).then_inc(s["a_xtl"], 1)

            def output_low(b):
                dve.wait_ge(s["a_ztc"], b + 1)
                dve.tensor_tensor(z_p[:, 1], halves(Z), z_p[:, 0], ALU.subtract).then_inc(s["a_ztl"], 1)

            def key_copies(b):
                for g in range(4):
                    dve.wait_ge(s["a_q"], b * 4 + g + 1)
                    dve.scalar_tensor_tensor(q0[:, 1, g, :], S[g][:, 0:T], 0.25, q0[:, 0, g, :], ALU.mult, ALU.subtract)
                    dve.tensor_tensor(k0[:, 1, g, :], S[g][:, T:2 * T], k0[:, 0, g, :], ALU.subtract).then_inc(s["a_k"], 1)

            def value_copy(b):
                dve.wait_ge(s["a_vps"], b + 1)
                for r in range(2):
                    last = dve.tensor_copy(
                        vpad[:, :, r::2, r * HD0:(r + 1) * HD0].rearrange("p t h e -> p (t h) e"),
                        O[:].rearrange("p (t h r e) -> p (t h) r e", t=2, r=2, e=HD0)[:, :, r, :])
                last.then_inc(s["a_v"], 1)

            def maxima(b, u):
                dve.wait_ge(s["a_sc"], b * 8 + u + 1)
                for r in range(2):
                    h = 2 * u + r
                    bank = S[2 * (u % 2) + r]
                    dve.tensor_reduce(negmax[:, 0, h:h + 1], bank[:, 0:128], AXX, ALU.max, negate=True)
                    last = dve.tensor_reduce(negmax[:, 1, h:h + 1], bank[:, 128:384], AXX, ALU.max, negate=True)
                last.then_inc(s["a_mx"], 1)

            def normalise(b, u, ch):
                dve.wait_ge(s["a_exp"], b * 8 + u + 1)
                sums = rowsum[:, :, 2 * u:2 * u + 2]
                ch(dve.reciprocal(sums, sums))
                for r in range(2):
                    h, pr = 2 * u + r, prob[u % 3][:, r, :]
                    dve.tensor_scalar(pr[:, 0:128], pr[:, 0:128], rowsum[:, 0, h:h + 1], None, ALU.mult)
                    last = dve.tensor_scalar(pr[:, 128:384], pr[:, 128:384], rowsum[:, 1, h:h + 1], None, ALU.mult)
                last.then_inc(s["a_norm"], 1)

            def copies(b, u):
                dve.wait_ge(s["a_pt"], b * 8 + u + 1)
                for r in range(2):
                    last = dve.tensor_copy(probT[u % 2][:, r, :], TB[r][:, 0:384])
                last.then_inc(s["a_ptc"], 1)

            def output_stats(b, ch):
                dve.wait_ge(s["a_y"], b + 1)
                ln_moments([T1[:, t * D:(t + 1) * D] for t in range(2)], ch)

            def output_norm(b, ch):
                dve.wait_ge(s["ln_rs"], post_event(b) + 1)
                ch(ln_apply([tmp[:, t, :] for t in range(2)], [T1[:, t * D:(t + 1) * D] for t in range(2)]))
                dve.sem_inc(s["a_yr"], 1)

            def residual(b, ch):
                both = x_sb[:, bass.ds(2 * b, 2), :]
                ch(dve.tensor_tensor(both, both, tmp, ALU.add))
                ln_moments([tile(2 * b + t) for t in range(2)], ch)

            def next_input_norm(b):
                dve.wait_ge(s["ln_rs"], post_event(b) + 2)
                ln_apply([xn2[:, t, :] for t in range(2)], [tile(2 * b + t) for t in range(2)]).then_inc(s["a_xn2"], 1)

            def next_input_low(b):
                dve.wait_ge(s["a_x2c"], b + 1)
                dve.tensor_reduce(xmT[:, :, bass.ds(b, 1)], xn2T, AXX, ALU.add).then_inc(s["a_xm"], 1)
                dve.wait_ge(s["a_xall"], b + 2)
                dve.tensor_tensor(xr[:, 1, :, bass.ds(b * T, T)], xn2T, xr[:, 0, :, bass.ds(b * T, T)],
                                  ALU.subtract).then_inc(s["a_xlo"], 1)

            def router_copy(b):
                dve.wait_ge(s["a_lg"], b + 1)
                dve.tensor_copy(lg_all[:, bass.ds(2 * b, 2), :],
                                O[:, 0:2 * E].rearrange("p (t e) -> p t e", e=E)).then_inc(s["a_lgc"], 1)

            def event(b):
                return b if isinstance(b, int) and b == 0 else 3 * b - 2

            def post_event(b):
                return 3 * b + (1 if isinstance(b, int) and b == NB - 1 else 2)

            def attention(b, first, last):
                ch = Chain(dve, s["cha"], A_LINKS(b))
                for u in range(11):
                    if u == 0 and not first:
                        output_stats(b - 1, ch)
                    if u == 7 and not first:
                        router_copy(b - 1)
                    if u < 8:
                        maxima(b, u)
                    if u == 1 and not first:
                        output_norm(b - 1, ch)
                    if 1 <= u <= 8:
                        normalise(b, u - 1, ch)
                    if u == 2 and not first:
                        residual(b - 1, ch)
                    if u == 3 and not first:
                        next_input_norm(b - 1)
                    if u == 5 and not last:
                        input_stats(b + 1, ch)
                    if u == 6 and not last:
                        input_norm(b + 1)
                    if u == 6 and not first:
                        next_input_low(b - 1)
                    if 2 <= u <= 9:
                        copies(b, u - 2)
                    if u == 7 and not last:
                        input_low(b + 1)
                if not last:
                    key_copies(b + 1)
                    value_copy(b + 1)
                output_low(b)
                return ch.n

            ch = Chain(dve, s["ch0"])
            input_stats(0, ch)
            input_norm(0)
            dve.wait_ge(s["w_a"], 80)
            for i, (w, wp) in enumerate(((wq0, wq_p), (wk0, wk_p), (wv0, wv_p), (wo0, wo_p))):
                dve.wait_ge(s["a_wh"], i + 1)
                dve.tensor_tensor(wp[:, 1], w, wp[:, 0], ALU.subtract).then_inc(s["a_wl"], 1)
            input_low(0)
            key_copies(0)
            dve.wait_ge(s["const_done"], 1)
            value_copy(0)
            def A_LINKS(b):
                return 0 if isinstance(b, int) and b == 0 else 9 + (b - 1) * 13
            assert attention(0, True, False) == 9
            with dve.Fori(1, NB - 1) as b:
                assert attention(b, False, False) == 13
            n = attention(NB - 1, False, True)
            ch = Chain(dve, s["cha"], A_LINKS(NB - 1) + n)
            output_stats(NB - 1, ch)
            output_norm(NB - 1, ch)
            residual(NB - 1, ch)
            next_input_norm(NB - 1)
            next_input_low(NB - 1)
            router_copy(NB - 1)

            chr_ = Chain(dve, s["chr"])

            def task_softmax():
                dve.wait_ge(s["w_te"], 96)
                dve.wait_ge(s["t_lg"], 1)
                chr_(dve.tensor_tensor(tl[:], S[1][0:NB, 0:ND], te_b2[:], ALU.add))
                chr_(dve.tensor_reduce(tm[:], tl[:], AXX, ALU.max, negate=True))
                dve.tensor_scalar(tl[:], tl[:], tm[:, 0:1], None, ALU.add).then_inc(s["t_sub"], 1)
                dve.wait_ge(s["t_exp"], 1)
                chr_(dve.tensor_reduce(tm[:], td[:], AXX, ALU.add))
                chr_(dve.reciprocal(tm[:], tm[:]))
                dve.tensor_scalar(td[:], td[:], tm[:, 0:1], None, ALU.mult).then_inc(s["t_td"], 1)
                dve.wait_ge(s["t_tT"], 1)
                dve.tensor_copy(tdx, bc(S[1][0:ND, 0:NB].unsqueeze(2), [ND, NB, P])).then_inc(s["t_tx"], 1)

            def logits():
                dve.wait_ge(s["t_dom"], 1)
                chr_(dve.tensor_scalar(dom.rearrange("p b e -> p (b e)"), S[3][:], 0.5, None, ALU.mult))
                chr_(dve.tensor_tensor(lg.rearrange("p (b t) e -> p b t e", t=2),
                                       lg_all[:].rearrange("p (b t) e -> p b t e", t=2),
                                       bc(dom.unsqueeze(2), [P, NB, 2, E]), ALU.add))
                dve.tensor_tensor(rsel, lg, bc(rbias[:].unsqueeze(1), [P, NT, E]), ALU.add)
                chr_(dve.tensor_reduce(rmx, lg, AXX, ALU.max))

            def best_experts():
                for i in range(NT):
                    last = dve.max(top[:, i, :], rsel[:, i, :])
                chr_(last)
                for i in range(NT):
                    last = dve.max_index(topi[:, i, :], top[:, i, :], rsel[:, i, :])
                chr_(last)
                chr_(dve.tensor_copy(topf, topi))
                dve.tensor_tensor(lg, lg, bc(rmx.unsqueeze(2), [P, NT, E]), ALU.subtract).then_inc(s["r_sub"], 1)

            def mark_experts(ks):
                iob = bc(iota[:].unsqueeze(1), [P, NT, E])
                for k in ks:
                    dst = rmask if k == 0 else rsel
                    chr_(dve.tensor_tensor(dst, iob, bc(topf[:, :, k:k + 1], [P, NT, E]), ALU.is_equal))
                    if k:
                        chr_(dve.tensor_tensor(rmask, rmask, rsel, ALU.add))

            def combine_sums():
                dve.wait_ge(s["r_exp"], 1)
                chr_(dve.tensor_reduce(rZ, comb, AXX, ALU.add))
                chr_(dve.tensor_tensor(comb, comb, rmask, ALU.mult))
                chr_(dve.tensor_reduce(rS, comb, AXX, ALU.add))

            def combine_weights():
                chr_(dve.scalar_tensor_tensor(rS, rZ, 1e-8, rS, ALU.mult, ALU.add))
                chr_(dve.reciprocal(rS, rS))
                dve.tensor_tensor(comb, comb, bc(rS.unsqueeze(2), [P, NT, E]), ALU.mult).then_inc(s["r_comb"], 1)
                dve.wait_ge(s["sel_done"], 1)
                dve.tensor_copy(selE, bc(eye2.unsqueeze(2), [P, E, FE]))

            def combine_parts():
                dve.wait_ge(s["r_cT"], 1)
                for i in range(4):
                    cols = slice(i * 512, (i + 1) * 512)
                    chr_(dve.tensor_copy(cpart[0:E, cols], S[i][0:E, :]))
                    last = dve.tensor_tensor(cpart[E:P, cols], S[i][0:E, :], cpart[0:E, cols], ALU.subtract)
                last.then_inc(s["r_split"], 1)

            def router_step(n):
                if n == 0:
                    logits()
                if n == 1:
                    best_experts()
                if n == 2:
                    mark_experts((0, 1))
                if n == 3:
                    mark_experts((2, 3))
                if n == 4:
                    combine_sums()
                if n == 5:
                    combine_weights()
                if n == NU * NSH - 1:
                    combine_parts()

            def rows_stats(p, k, ch):
                dve.wait_ge(s["f_rows"], 4 * p + k + 1)
                ln_moments([rows_sb[k][:, t * D:(t + 1) * D] for t in range(2)], ch)

            def rows_add(p, k, event, scratch, ch):
                dve.wait_ge(s["ln_rs"], event + 1)
                ch(ln_apply([scratch[:, t, :] for t in range(2)], [rows_sb[k][:, t * D:(t + 1) * D] for t in range(2)]))
                rows = x_sb[:, 8 * p + 2 * k:8 * p + 2 * k + 2, :]
                ch(dve.tensor_tensor(rows, rows, scratch, ALU.add))
                dve.sem_inc(s["f_added"], 1)

            def low_weights(load, j):
                dve.wait_ge(s["f_wh"], load + j + 1)
                dve.tensor_tensor(wpart[:, j % 2, 1, :], raw[:, j % RING, :], wpart[:, j % 2, 0, :],
                                  ALU.subtract).then_inc(s["f_wl"], 1)

            ch = Chain(dve, s["chb"])
            low_weights(0, 0)
            task_softmax()
            for p in range(NPASS):
                for n in range(NU * NJ):
                    j, m = n // NU, n % NU
                    i = p * NU * NJ + n
                    dve.wait_ge(s["f_sg"], i + 1)
                    if j >= NSH:
                        dve.wait_ge(s["f_cb"], p * NU * NPAIR + n - NU * NSH + 1)
                        ch(dve.tensor_tensor(sgl[m], sgl[m], S[3][:], ALU.mult))
                    dve.wait_ge(s["f_u"], i + 1)
                    dve.tensor_tensor(hf[m], sgl[m], S[2][:], ALU.mult).then_inc(s["f_h"], 1)
                    dve.wait_ge(s["f_hh"], i + 1)
                    dve.tensor_tensor(hp[:, m, 1, :], hf[m], hp[:, m, 0, :], ALU.subtract).then_inc(s["f_hl"], 1)
                    if m == 0 and p * NJ + j + 1 < NPASS * NJ:
                        low_weights(0, p * NJ + j + 1)
                    if p == 0 and n < NU * NSH:
                        router_step(n)
                    if p and 4 <= n <= 7:
                        rows_add(p - 1, n - 4, 3 * NB + 4 * (p - 1) + n - 4, tmp2, ch)
                    if p and 3 <= n <= 6:
                        rows_stats(p - 1, n - 3, ch)

            ch = Chain(dve, s["chc0"])
            dve.wait_ge(s["w_c"], 144)
            dve.wait_ge(s["c_ones"], 1)
            dve.tensor_scalar(big15, big, 1.0 / CAP, None, ALU.mult)
            dve.tensor_scalar(bfg15, bfg, 1.0 / CAP, None, ALU.mult)
            dve.tensor_copy(sel1[:], bc(eye1[:].unsqueeze(2), [2 * 32, H1, P]))
            ch(dve.tensor_copy(gA[:], bc(ident[0:64, 127:128], [2 * 32, T])))
            base = 3 * NB + NT // 2

            def input_stats1(b, ch):
                ln_moments([tile(2 * b + t) for t in range(2)], ch)

            def input_norm1(b):
                dve.wait_ge(s["ln_rs"], base + (event(b) if not isinstance(b, int) or b else -4) + 1)
                ln_apply([xn[:, t, :] for t in range(2)], [tile(2 * b + t) for t in range(2)]).then_inc(s["c_xn"], 1)

            def scans(b, ch):
                dve.wait_ge(s["c_ls"], b + 1)
                dve.tensor_scalar(gi, gi, CAP, None, ALU.mult)
                ch(dve.tensor_scalar(gls, gls, -1.0, None, ALU.mult))
                dve.tensor_tensor_scan(gF, ones1, gls, 0.0, ALU.mult, ALU.add)
                ch(dve.tensor_tensor_scan(gm, gls, gi, 0.0, ALU.add, ALU.max))

            def gate_rows(b, ch):
                ch(dve.tensor_tensor(gAf, gF, gm, ALU.subtract))
                ch(dve.tensor_copy(gA[0:H1, :], gAf))
                dve.tensor_tensor(gA[32:32 + H1, :], gAf, gA[0:H1, :], ALU.subtract)
                dve.tensor_tensor(gG, gi, gF, ALU.subtract).then_inc(s["c_gates"], 1)

            def gate_columns(b):
                dve.wait_ge(s["c_gT"], b + 1)
                dve.tensor_copy(gcol, T1[:, 0:16].rearrange("p (a b) -> p a b", b=H1)).then_inc(s["c_gcol"], 1)

            def key_value_copies(b):
                for g in range(2):
                    dve.wait_ge(s["c_q"], b * 2 + g + 1)
                    dve.scalar_tensor_tensor(q1[:, 1, g, :], S[g][:, 0:T], 0.25, q1[:, 0, g, :], ALU.mult, ALU.subtract)
                    dve.tensor_tensor(k1[:, 1, g, :], S[g][:, T:2 * T], k1[:, 0, g, :], ALU.subtract).then_inc(s["c_k"], 1)
                dve.wait_ge(s["c_vog"], b + 1)
                dve.tensor_copy(v1[:, :, :, 0:DV1].rearrange("p t h e -> p (t h) e"),
                                S[2][:].rearrange("p (h e) -> p h e", e=DV1)).then_inc(s["c_v"], 1)

            def output_gate(b, t, ch):
                if t == 0:
                    dve.wait_ge(s["c_eo"], b + 1)
                    ch(dve.tensor_scalar(eo, eo, 1.0, None, ALU.add))
                ch(dve.reciprocal(eo[:, t, :], eo[:, t, :]))
                if t:
                    ch(dve.tensor_tensor(eo, eo, bc(gam.unsqueeze(1), [P, 2, D]), ALU.mult))

            def output_stats1(b, ch):
                dve.wait_ge(s["c_y"], b + 1)
                ln_moments([T0[:, t * D:(t + 1) * D] for t in range(2)], ch)

            def output_norm1(b, ch):
                dve.wait_ge(s["ln_rs"], base + post_event(b) + 1)
                ch(ln_apply([tmp[:, t, :] for t in range(2)], [T0[:, t * D:(t + 1) * D] for t in range(2)]))

            def residual1(b, ch):
                res = x_sb[:, bass.ds(2 * b, 2), :]
                ch(dve.tensor_tensor(res, res, tmp, ALU.add))
                ln_moments([tile(2 * b + t) for t in range(2)], ch)

            def final_input_norm(b):
                dve.wait_ge(s["ln_rs"], base + post_event(b) + 2)
                ln_apply([xn4[:, t, :] for t in range(2)], [tile(2 * b + t) for t in range(2)]).then_inc(s["c_xn4"], 1)

            def final_input_low(b):
                dve.wait_ge(s["c_xhi"], b + 1)
                dve.tensor_tensor(xr[:, 1, :, bass.ds(b * T, T)], halves(T0), xr[:, 0, :, bass.ds(b * T, T)],
                                  ALU.subtract).then_inc(s["c_xall"], 1)

            def weights1(b, h):
                dve.wait_ge(s["c_dec"], b * H1 + h + 1)
                dve.tensor_tensor(wt[h % 2], dec[h % 2], S[h % 2][:, 0:384], ALU.mult).then_inc(s["c_w"], 1)

            def last_low_weights(n):
                dve.wait_ge(s["f_wh"], NPASS * NJ + n + 1)
                dve.tensor_tensor(lastw[:, n, 1, :], raw[:, n % RING, :], lastw[:, n, 0, :],
                                  ALU.subtract).then_inc(s["f_wl"], 1)

            def mlstm(b, ch, first, last):
                for h in range(H1):
                    if h == 0 and not first:
                        output_stats1(b - 1, ch)
                    weights1(b, h)
                    if (first or last) and h % 2 == 1:
                        last_low_weights(h // 2 + (RING if last else 0))
                    if first and 1 <= h <= 4:
                        rows_add(NPASS - 1, h - 1, base - 3 + h - 1, tmp, ch)
                    if first and h <= 3:
                        rows_stats(NPASS - 1, h, ch)
                    if h == 1 and not first:
                        output_norm1(b - 1, ch)
                    if h == 2 and not first:
                        residual1(b - 1, ch)
                    if h == 3 and not first:
                        final_input_norm(b - 1)
                    if h in (6, 7):
                        output_gate(b, h - 6, ch)
                    if h == 4 and not last:
                        input_stats1(b + 1, ch)
                    if h == 5 and not last:
                        input_norm1(b + 1)
                    if h == 5 and not first:
                        final_input_low(b - 1)
                dve.wait_ge(s["c_pv"], b + 1)
                both = [bank[:, 0:H1 * (DV1 + 1)].rearrange("p (h e) -> p h e", e=DV1 + 1) for bank in (Z, O)]
                for t in range(2):
                    last_op = dve.tensor_copy(den[:, t, :], both[t][:, :, DV1])
                ch(last_op)
                ch(dve.scalar_tensor_tensor(den, den, -1.0, den, ALU.mult, ALU.max))
                ch(dve.tensor_tensor(den, den, em, ALU.max))
                ch(dve.tensor_scalar(den, den, HEAD_EPS, None, ALU.add))
                ch(dve.reciprocal(den, den))
                hn4 = hn.rearrange("p t (h e) -> p t h e", e=DV1)
                for t in range(2):
                    last_op = dve.tensor_tensor(hn4[:, t], both[t][:, :, 0:DV1],
                                                bc(den[:, t, :].unsqueeze(2), [P, H1, DV1]), ALU.mult)
                ch(last_op)
                hnf = hn.rearrange("p t (h e) -> p (t h) e", e=DV1)
                hcf = hc.rearrange("p t (h e) -> p (t h) e", e=DV1)
                sqf = sq.rearrange("p t (h e) -> p (t h) e", e=DV1)
                ch(dve.tensor_reduce(mu, hnf, AXX, ALU.add))
                ch(dve.tensor_scalar(mu, mu, 1.0 / DV1, None, ALU.mult))
                ch(dve.tensor_tensor(hcf, hnf, bc(mu.unsqueeze(2), [P, 16, DV1]), ALU.subtract))
                ch(dve.tensor_tensor(sq, hc, hc, ALU.mult))
                dve.tensor_reduce(hv, sqf, AXX, ALU.add).then_inc(s["c_hv"], 1)
                ch(dve.tensor_tensor(hc, hc, eo, ALU.mult))
                if not last:
                    scans(b + 1, ch)
                    gate_rows(b + 1, ch)
                dve.wait_ge(s["c_hr"], b + 1)
                dve.tensor_tensor(hnf, hcf, bc(hv.unsqueeze(2), [P, 16, DV1]), ALU.mult).then_inc(s["c_ho"], 1)
                if not last:
                    gate_columns(b + 1)
                    key_value_copies(b + 1)

            FIRST1, PER1 = 32, 24
            ch = Chain(dve, s["chc"])
            input_stats1(0, ch)
            input_norm1(0)
            scans(0, ch)
            gate_rows(0, ch)
            gate_columns(0)
            key_value_copies(0)
            head = ch.n
            mlstm(0, ch, True, False)
            assert ch.n == head + FIRST1, ch.n
            with dve.Fori(1, NB - 1) as b:
                ch = Chain(dve, s["chc"], head + FIRST1 + (b - 1) * PER1)
                mlstm(b, ch, False, False)
                assert ch.n == PER1, ch.n
            ch = Chain(dve, s["chc"], head + FIRST1 + (NB - 2) * PER1)
            mlstm(NB - 1, ch, False, True)
            output_stats1(NB - 1, ch)
            output_norm1(NB - 1, ch)
            residual1(NB - 1, ch)
            final_input_norm(NB - 1)
            final_input_low(NB - 1)

            base += 3 * NB
            ch = Chain(dve, s["chd"])

            def product(i):
                dve.wait_ge(s["d_sg"], i + 1)
                dve.wait_ge(s["d_u"], i + 1)
                if i >= 4:
                    dve.wait_ge(s["d_hl"], i - 3)
                dve.tensor_tensor(hb[:, i % 4, :], sgl[i % 2], S[2 + i % 2][:], ALU.mult).then_inc(s["d_h"], 1)

            def compare(dst, j, i):
                dve.wait_ge(s["d_abs"], i - i % 4 + j + 1)
                return dve.tensor_tensor(dst, ab[:, 0:j, :], bc(ab[:, j:j + 1, :], [P, j, 512]), ALU.is_ge)

            c01, c02, c12, c03, c13, c23 = c1[:, 0], c2[:, 0], c2[:, 1], c3[:, 0], c3[:, 1], c3[:, 2]
            rules = (((c01, c02, ALU.add), (c03, ALU.add), ALU.is_ge, 2.0),
                     ((c12, c13, ALU.add), (c01, ALU.subtract), ALU.is_ge, 1.0),
                     ((c23, c02, ALU.subtract), (c12, ALU.subtract), ALU.is_ge, 0.0),
                     ((c03, c13, ALU.add), (c23, ALU.add), ALU.is_le, 1.0))

            def sparsify(i):
                (a, b_, op), (c, op2), keep, least = rules[i % 4]
                tally = tallies[i % 2]
                if i >= 2:
                    dve.wait_ge(s["d_hs"], i - 1)
                ch(dve.tensor_tensor(tally, a, b_, op))
                ch(dve.tensor_tensor(tally, tally, c, op2))
                dve.scalar_tensor_tensor(hb[:, i % 4, :], tally, least, hb[:, i % 4, :],
                                         keep, ALU.mult).then_inc(s["d_hs"], 1)

            ROWS = (T0, T1, Z, O)

            def unit_stats(u, k):
                if k == 0:
                    dve.wait_ge(s["d_dn"], NI * (u + 1))
                bank = ROWS[2 * (u % 2) + k]
                ln_moments([bank[:, t * D:(t + 1) * D] for t in range(2)], ch)

            def unit_residual(u, k):
                bank, rows = ROWS[2 * (u % 2) + k], x_sb[:, 4 * u + 2 * k:4 * u + 2 * k + 2, :]
                dve.wait_ge(s["ln_rs"], base + 2 * u + k + 1)
                ch(ln_apply([tmp2[:, t, :] for t in range(2)], [bank[:, t * D:(t + 1) * D] for t in range(2)]))
                ch(dve.tensor_tensor(rows, rows, tmp2, ALU.add))
                if k:
                    dve.sem_inc(s["d_x"], 1)

            for i in range(STEPS + 3):
                u, n = divmod(i, NI)
                j = i % 4
                if i >= 4 and j < 3:
                    sparsify(i - 3)
                if i < STEPS:
                    if j == 2:
                        ch(compare(c1, 1, i))
                    if j == 3:
                        compare(c2, 2, i)
                    product(i)
                    if j == 3:
                        last = compare(c3, 3, i)
                        last.then_inc(s["d_cmp"], 1)
                        dve.wait_ge(s["d_cmp"], i // 4 + 1)
                        sparsify(i - 3)
                if i < STEPS and u:
                    if n == 5:
                        unit_stats(u - 1, 0)
                    if n == 6:
                        unit_residual(u - 1, 0)
                        unit_stats(u - 1, 1)
                if u > 1 and n == 0:
                    unit_residual(u - 2, 1)
            unit_stats(NUNIT - 1, 0)
            unit_residual(NUNIT - 1, 0)
            unit_stats(NUNIT - 1, 1)
            unit_residual(NUNIT - 1, 1)


def _laid_out(a):
    def kmajor(w):
        return np.ascontiguousarray(w.reshape(KC, P, -1).transpose(1, 0, 2))

    def heads(w, n, k):
        wt = np.zeros((D, n, 32), w.dtype)
        wt[:, :, :k] = w.T.reshape(D, n, k)
        return kmajor(wt.reshape(D, n * 32))

    def blocks(g, u, d):
        n = g.shape[1] // P
        gu = [w.reshape(KC, P, n, P).transpose(2, 1, 0, 3).reshape(n, P, KC * P) for w in (g, u)]
        return np.concatenate(gu + [d.reshape(n, P, D)], axis=2)

    quads = lambda w: w.reshape(D, 2, P, 4).transpose(0, 1, 3, 2).reshape(D, 1024)
    return {
        "x": a["L0_attn_x"].reshape(NB * T, D),
        "wq0": heads(a["L0_attn_Wq"], H0, HD0), "wk0": heads(a["L0_attn_Wk"], H0, HD0),
        "wv0": kmajor(a["L0_attn_Wv"].T), "wo0": kmajor(a["L0_attn_Wo"].T), "wr": kmajor(a["L0_ffn_Wr"].T),
        "te1": kmajor(a["L0_ffn_te_W1"].T), "te_b1": a["L0_ffn_te_b1"].reshape(P, 1),
        "te2": np.ascontiguousarray(a["L0_ffn_te_W2"].T), "te_b2": a["L0_ffn_te_b2"],
        "aff": np.ascontiguousarray(a["L0_ffn_affinity"].T), "rbias": a["L0_ffn_router_bias"],
        "moe": np.concatenate([
            blocks(a["L0_ffn_Sg"].transpose(1, 0, 2).reshape(D, 512), a["L0_ffn_Su"].transpose(1, 0, 2).reshape(D, 512),
                   a["L0_ffn_Sd"].reshape(512, D)),
            blocks(a["L0_ffn_Wg"].transpose(1, 0, 2).reshape(D, E * FE), a["L0_ffn_Wu"].transpose(1, 0, 2).reshape(D, E * FE),
                   a["L0_ffn_Wd"].reshape(E * FE, D))]),
        "wq1": heads(a["L1_attn_Wq"], H1, QK1), "wk1": heads(a["L1_attn_Wk"], H1, QK1),
        "wv1": kmajor(a["L1_attn_Wv"].T), "wog1": kmajor(a["L1_attn_Wog"].T), "wo1": kmajor(a["L1_attn_Wout"].T),
        "wgates": kmajor(np.concatenate([a["L1_attn_Wig"].T, np.zeros((D, 32 - H1), a["L1_attn_Wig"].dtype),
                                          a["L1_attn_Wfg"].T], axis=1)),
        "big": a["L1_attn_big"].reshape(H1, 1), "bfg": a["L1_attn_bfg"].reshape(H1, 1),
        "gam": a["L1_attn_gamma"].reshape(D),
        "ffn": blocks(quads(a["L1_ffn_w_gate"]), quads(a["L1_ffn_w_up"]),
                      a["L1_ffn_w_down"].reshape(2, P, 4, D).transpose(0, 2, 1, 3).reshape(NI * P, D)),
    }


def kernel(**inputs):
    import concourse.bacc as bacc
    from concourse.bass_utils import run_bass_kernel_spmd

    nc = bacc.Bacc("TRN2", target_bir_lowering=False, num_devices=1)
    arrays, io = {}, {}
    for name, v in _laid_out({k: np.asarray(v) for k, v in inputs.items()}).items():
        arrays[f"in_{name}"] = np.ascontiguousarray(v)
        io[name] = nc.dram_tensor(f"in_{name}", v.shape, mybir.dt.from_np(v.dtype), kind="ExternalInput").ap()
    out = nc.dram_tensor("out", (NB * T, D), F32, kind="ExternalOutput").ap()
    build(nc, io, out)
    r = run_bass_kernel_spmd(nc, [arrays], core_ids=[0])
    return r.results[0]["out"].reshape(NB, T, D)
```
